# Optimizing a Trainium2 kernel written in Bass

```python
import numpy as np
import jax
import jax.numpy as jnp

def _softmax(x, axis=-1):
    return jax.nn.softmax(x, axis=axis)

def _gelu(x):
    return jax.nn.gelu(x, approximate=True)

def _silu(x):
    return jax.nn.silu(x)

def _sigmoid(x):
    return jax.nn.sigmoid(x)

def _layernorm(x, axis=-1, eps=1e-05):
    m = jnp.mean(x, axis=axis, keepdims=True)
    v = jnp.var(x, axis=axis, keepdims=True)
    return (x - m) / jnp.sqrt(v + eps)

def _scatter_add(tgt, idx, src, axis=0):
    return tgt.at[idx].add(src)

def _segment_sum(src, seg, n):
    return jax.ops.segment_sum(src, seg, n)
kernel_name = 'mk_decoder_postln_d2_seqx_r4_d4b7d4'

def setup_inputs(seed: int=0):
    np.random.seed(seed)
    _w = jnp.asarray

    def _rec_inputs():
        import jax
        import jax.numpy as jnp
        _rk = jax.random.key(seed)
        x = -0.0003929 + 0.9999 * jax.random.normal(jax.random.fold_in(_rk, 1), (2, 1024, 256), jnp.float32)
        _lenS = 1024 - jax.random.randint(jax.random.fold_in(_rk, 7), (2,), 0, max(1, 1024 // 4) + 1, jnp.int32)
        _lenS2 = 154 - jax.random.randint(jax.random.fold_in(_rk, 8), (2,), 0, max(1, 154 // 4) + 1, jnp.int32)
        _ctx_1024P = jax.random.normal(jax.random.fold_in(_rk, 11), (2, 16, 256), jnp.float32)
        _ctx_1024c = jax.random.dirichlet(jax.random.fold_in(_rk, 511), 0.3 * jnp.ones((16,), jnp.float32), (2, 154))
        _ctx_1024t = jnp.einsum('bsk,bkd->bsd', _ctx_1024c, _ctx_1024P)
        _ctx_1024t = _ctx_1024t * jax.lax.rsqrt(jnp.mean(jnp.square(_ctx_1024t)) + 1e-12) * 0.953939
        ctx_1024 = 2.81802e-05 + 1.00001 * (_ctx_1024t + 0.3 * jax.random.normal(jax.random.fold_in(_rk, 611), (2, 154, 256), jnp.float32))
        return (x, ctx_1024)
    x, ctx_1024 = _rec_inputs()

    def _L0_attn_setup():
        import jax, jax.numpy as jnp
        import numpy as np
        H = 16
        SEG = 512
        DIL = 8
        BLOCK_M = 64
        key = jax.random.key(seed)
        k1, k2, k3 = jax.random.split(key, 3)
        B, M, D = (2, 2048, 256)
        x = jax.random.normal(k1, (B, M, D), dtype=jnp.float32)
        Wqkv = jax.random.normal(k2, (3 * D, D), dtype=jnp.float32) * 0.02
        Wout = jax.random.normal(k3, (D, D), dtype=jnp.float32) * 0.02
        return {'x': x, 'Wqkv': Wqkv, 'Wout': Wout}
    _L0_attn_all = _L0_attn_setup()
    _L0_attn_in = {k: v for k, v in _L0_attn_all.items() if k in ('Wqkv', 'Wout')}
    del _L0_attn_all

    def _L0_xattn_setup():
        import jax, jax.numpy as jnp
        import numpy as np
        B, LQ, LS, H = (4, 1024, 1024, 256)
        key = jax.random.key(seed)
        k1, k2 = jax.random.split(key)
        query_input = jax.random.normal(k1, (B, LQ, H), dtype=jnp.float32)
        source_input = jax.random.normal(k2, (B, LS, H), dtype=jnp.float32)
        return {'query_input': query_input, 'source_input': source_input}
    _L0_xattn_all = _L0_xattn_setup()
    _L0_xattn_in = {k: v for k, v in _L0_xattn_all.items() if k in ()}
    del _L0_xattn_all

    def _L0_ffn_setup():
        import jax, jax.numpy as jnp
        import numpy as np
        DIM = 256

        def _reference_tuple_inner(x, W_r, W_k, W_v, mu_r, mu_k):
            B, T, C = x.shape
            x_prev = jnp.concatenate([jnp.zeros((B, 1, C), x.dtype), x[:, :-1, :]], axis=1)
            xr = mu_r * x + (1.0 - mu_r) * x_prev
            xk = mu_k * x + (1.0 - mu_k) * x_prev
            r = jax.nn.sigmoid(jnp.einsum('btc,dc->btd', xr, W_r))
            k = jnp.einsum('btc,dc->btd', xk, W_k)
            k_act = jnp.square(jax.nn.relu(k))
            out = r * jnp.einsum('btc,dc->btd', k_act, W_v)
            new_state = x[:, -1, :]
            return (out, new_state)
        key = jax.random.key(seed)
        ks = jax.random.split(key, 6)
        B, T, C = (8, 512, DIM)
        x = jax.random.normal(ks[0], (B, T, C), dtype=jnp.float32)
        s = 1.0 / np.sqrt(C)
        W_r = jax.random.uniform(ks[1], (C, C), jnp.float32, -s, s)
        W_k = jax.random.uniform(ks[2], (C, C), jnp.float32, -s, s)
        W_v = jax.random.uniform(ks[3], (C, C), jnp.float32, -s, s)
        mu_r = jax.random.uniform(ks[4], (C,), jnp.float32)
        mu_k = jax.random.uniform(ks[5], (C,), jnp.float32)
        return {'x': x, 'W_r': W_r, 'W_k': W_k, 'W_v': W_v, 'mu_r': mu_r, 'mu_k': mu_k}
    _L0_ffn_all = _L0_ffn_setup()
    _L0_ffn_in = {k: v for k, v in _L0_ffn_all.items() if k in ('W_r', 'W_k', 'W_v', 'mu_r', 'mu_k')}
    del _L0_ffn_all

    def _L1_attn_setup():
        import jax, jax.numpy as jnp
        import numpy as np
        SHIFTS = (-32, -16, -4, -1, 1, 4, 16, 32)
        LN_EPS = 1e-05
        key = jax.random.key(seed)
        k_x, k_g, k_v, k_gm, k_bt = jax.random.split(key, 5)
        B, L, D = (4, 1024, 256)
        n = len(SHIFTS) + 1
        scale = 1.0 / np.sqrt(D)
        x = jax.random.normal(k_x, (B, L, D), dtype=jnp.float32)
        gate_W = jax.random.normal(k_g, (n * D, D), dtype=jnp.float32) * scale
        value_W = jax.random.normal(k_v, (D, D), dtype=jnp.float32) * scale
        gamma = jnp.ones((D,), dtype=jnp.float32)
        beta = jnp.zeros((D,), dtype=jnp.float32)
        return {'x': x, 'gate_W': gate_W, 'value_W': value_W, 'gamma': gamma, 'beta': beta}
    _L1_attn_all = _L1_attn_setup()
    _L1_attn_in = {k: v for k, v in _L1_attn_all.items() if k in ('gate_W', 'value_W', 'gamma', 'beta')}
    del _L1_attn_all

    def _L1_xattn_setup():
        import jax, jax.numpy as jnp
        import numpy as np
        from jax import lax
        BIG = jnp.float32(1e+30)

        def _pairwise_euclidean(a, b):
            aa = jnp.sum(a * a, axis=-1)[:, None]
            bb = jnp.sum(b * b, axis=-1)[None, :]
            ab = a @ b.T
            return jnp.sqrt(jnp.maximum(aa + bb - 2.0 * ab, 0.0))

        def _dtw_cost(D):
            row0 = jnp.cumsum(D[0])

            def row_step(prev_row, d_row):
                first = d_row[0] + prev_row[0]

                def col_step(left, inp):
                    d_ij, up, diag = inp
                    r = d_ij + jnp.minimum(jnp.minimum(up, left), diag)
                    return (r, r)
                _, rest = lax.scan(col_step, first, (d_row[1:], prev_row[1:], prev_row[:-1]))
                row = jnp.concatenate([first[None], rest])
                return (row, row)
            _, rows = lax.scan(row_step, row0, D[1:])
            return jnp.concatenate([row0[None], rows], axis=0)

        def _backtrack(R, T1, T2):
            L = T1 + T2 - 1

            def step(carry, _):
                i, j, done = carry
                valid = jnp.logical_not(done)
                cd = jnp.where((i > 0) & (j > 0), R[jnp.maximum(i - 1, 0), jnp.maximum(j - 1, 0)], BIG)
                cu = jnp.where(i > 0, R[jnp.maximum(i - 1, 0), j], BIG)
                cl = jnp.where(j > 0, R[i, jnp.maximum(j - 1, 0)], BIG)
                choice = jnp.argmin(jnp.stack([cd, cu, cl]))
                ni = jnp.where(choice <= 1, i - 1, i)
                nj = jnp.where((choice == 0) | (choice == 2), j - 1, j)
                at_origin = (i == 0) & (j == 0)
                ni = jnp.where(at_origin, 0, ni)
                nj = jnp.where(at_origin, 0, nj)
                return ((ni, nj, done | at_origin), (i, j, valid))
            init = (jnp.int32(T1 - 1), jnp.int32(T2 - 1), jnp.bool_(False))
            _, (i_idx, j_idx, valid) = lax.scan(step, init, None, length=L)
            return (i_idx, j_idx, valid)

        def _align_one(small, large):
            T_small, d = small.shape
            T_large = large.shape[0]
            D = _pairwise_euclidean(small, large)
            R = _dtw_cost(D)
            i_idx, j_idx, valid = _backtrack(R, T_small, T_large)
            contrib = small[i_idx] * valid[:, None].astype(small.dtype)
            expanded = jnp.zeros((T_large, d), dtype=small.dtype).at[j_idx].add(contrib)
            return expanded
        key = jax.random.key(seed)
        k1, k2 = jax.random.split(key)
        teacher = jax.random.normal(k1, (16, 100, 256), dtype=jnp.float32)
        student = jax.random.normal(k2, (16, 150, 256), dtype=jnp.float32)
        return {'teacher_features': teacher, 'student_features': student}
    _L1_xattn_all = _L1_xattn_setup()
    _L1_xattn_in = {k: v for k, v in _L1_xattn_all.items() if k in ()}
    del _L1_xattn_all

    def _L1_ffn_setup():
        import jax, jax.numpy as jnp
        import numpy as np

        def gelu(x):
            return jax.nn.gelu(x, approximate=False)
        key = jax.random.key(seed)
        ks = jax.random.split(key, 6)
        B, S, d_model = (4, 512, 256)
        n_input, n_process, n_output, d_pv = (2048, 1024, 2048, 128)
        s = 0.02
        return {'x': jax.random.normal(ks[0], (B, S, d_model), jnp.float32), 'input_patterns': jax.random.normal(ks[1], (n_input, d_model), jnp.float32) * s, 'process_input_weights': jax.random.normal(ks[2], (n_process, n_input), jnp.float32) * s, 'process_values': jax.random.normal(ks[3], (n_process, d_pv), jnp.float32) * s, 'output_input_weights': jax.random.normal(ks[4], (n_output, d_pv), jnp.float32) * s, 'output_patterns': jax.random.normal(ks[5], (n_output, d_model), jnp.float32) * s}
    _L1_ffn_all = _L1_ffn_setup()
    _L1_ffn_in = {k: v for k, v in _L1_ffn_all.items() if k in ('input_patterns', 'process_input_weights', 'process_values', 'output_input_weights', 'output_patterns')}
    del _L1_ffn_all
    return {'x': x, 'ctx_1024': ctx_1024, 'L0_attn_Wqkv': _L0_attn_in['Wqkv'], 'L0_attn_Wout': _L0_attn_in['Wout'], 'L0_ffn_W_r': _L0_ffn_in['W_r'], 'L0_ffn_W_k': _L0_ffn_in['W_k'], 'L0_ffn_W_v': _L0_ffn_in['W_v'], 'L0_ffn_mu_r': _L0_ffn_in['mu_r'], 'L0_ffn_mu_k': _L0_ffn_in['mu_k'], 'L1_attn_gate_W': _L1_attn_in['gate_W'], 'L1_attn_value_W': _L1_attn_in['value_W'], 'L1_attn_gamma': _L1_attn_in['gamma'], 'L1_attn_beta': _L1_attn_in['beta'], 'L1_ffn_input_patterns': _L1_ffn_in['input_patterns'], 'L1_ffn_process_input_weights': _L1_ffn_in['process_input_weights'], 'L1_ffn_process_values': _L1_ffn_in['process_values'], 'L1_ffn_output_input_weights': _L1_ffn_in['output_input_weights'], 'L1_ffn_output_patterns': _L1_ffn_in['output_patterns']}

def reference(x, ctx_1024, L0_attn_Wqkv, L0_attn_Wout, L0_ffn_W_r, L0_ffn_W_k, L0_ffn_W_v, L0_ffn_mu_r, L0_ffn_mu_k, L1_attn_gate_W, L1_attn_value_W, L1_attn_gamma, L1_attn_beta, L1_ffn_input_patterns, L1_ffn_process_input_weights, L1_ffn_process_values, L1_ffn_output_input_weights, L1_ffn_output_patterns):
    import jax
    import jax.numpy as jnp

    def _L0_attn_ref(x, Wqkv, Wout):
        import jax, jax.numpy as jnp
        import numpy as np
        H = 16
        SEG = 512
        DIL = 8
        BLOCK_M = 64
        B, M, D = x.shape
        hd = D // H
        scale = hd ** (-0.5)
        S = M // SEG
        Kn = SEG // DIL
        nb = SEG // BLOCK_M
        qkv = jnp.einsum('bmd,ed->bme', x, Wqkv).reshape(B, M, 3, H, hd)
        qkv = jnp.transpose(qkv, (2, 0, 3, 1, 4))
        q, k, v = (qkv[0] * scale, qkv[1], qkv[2])
        q4 = q.reshape(B, H, S, SEG, hd)
        k4 = k.reshape(B, H, S, SEG, hd)[:, :, :, ::DIL]
        v4 = v.reshape(B, H, S, SEG, hd)[:, :, :, ::DIL]
        scores = jnp.einsum('bhspd,bhskd->bhspk', q4, k4)
        scores = scores.reshape(B, H, S, nb, BLOCK_M, Kn)
        c = jnp.max(scores, axis=4, keepdims=True)
        w = jnp.exp(scores - c)
        den = jnp.sum(w, axis=-1) + 1e-10
        num = jnp.einsum('bhsnmk,bhskd->bhsnmd', w, v4)
        out = num / den[..., None]
        out = out.reshape(B, H, M, hd)
        out = jnp.transpose(out, (0, 2, 1, 3)).reshape(B, M, D)
        return jnp.einsum('bmd,ed->bme', out, Wout)

    def _L0_xattn_ref(query_input, source_input):
        import jax, jax.numpy as jnp
        import numpy as np
        B, LQ, LS, H = (4, 1024, 1024, 256)
        dk = jnp.asarray(query_input.shape[-1], dtype=query_input.dtype)
        logits = jnp.einsum('bqh,bsh->bqs', query_input, source_input) / jnp.sqrt(dk)
        weights = jax.nn.softmax(logits, axis=-1)
        return jnp.einsum('bqs,bsh->bqh', weights, source_input)

    def _L0_ffn_ref(x, W_r, W_k, W_v, mu_r, mu_k):
        import jax, jax.numpy as jnp
        import numpy as np
        DIM = 256

        def _reference_tuple_inner(x, W_r, W_k, W_v, mu_r, mu_k):
            B, T, C = x.shape
            x_prev = jnp.concatenate([jnp.zeros((B, 1, C), x.dtype), x[:, :-1, :]], axis=1)
            xr = mu_r * x + (1.0 - mu_r) * x_prev
            xk = mu_k * x + (1.0 - mu_k) * x_prev
            r = jax.nn.sigmoid(jnp.einsum('btc,dc->btd', xr, W_r))
            k = jnp.einsum('btc,dc->btd', xk, W_k)
            k_act = jnp.square(jax.nn.relu(k))
            out = r * jnp.einsum('btc,dc->btd', k_act, W_v)
            new_state = x[:, -1, :]
            return (out, new_state)
        return _reference_tuple_inner(x, W_r, W_k, W_v, mu_r, mu_k)[0]

    def _L1_attn_ref(x, gate_W, value_W, gamma, beta):
        import jax, jax.numpy as jnp
        import numpy as np
        SHIFTS = (-32, -16, -4, -1, 1, 4, 16, 32)
        LN_EPS = 1e-05
        B, L, D = x.shape
        n = len(SHIFTS) + 1
        v = jnp.einsum('bld,ed->ble', x, value_W)
        stacked = jnp.stack([v] + [jnp.roll(v, -s, axis=1) for s in SHIFTS], axis=2)
        gates = jax.nn.sigmoid(jnp.einsum('bld,ed->ble', x, gate_W))
        gates = gates.reshape(B, L, n, D)
        out = jnp.sum(stacked * gates, axis=2)
        mu = jnp.mean(out, axis=-1, keepdims=True)
        var = jnp.mean(jnp.square(out - mu), axis=-1, keepdims=True)
        return (out - mu) * jax.lax.rsqrt(var + LN_EPS) * gamma + beta

    def _L1_xattn_ref(teacher_features, student_features):
        import jax, jax.numpy as jnp
        import numpy as np
        from jax import lax
        BIG = jnp.float32(1e+30)

        def _pairwise_euclidean(a, b):
            aa = jnp.sum(a * a, axis=-1)[:, None]
            bb = jnp.sum(b * b, axis=-1)[None, :]
            ab = a @ b.T
            return jnp.sqrt(jnp.maximum(aa + bb - 2.0 * ab, 0.0))

        def _dtw_cost(D):
            row0 = jnp.cumsum(D[0])

            def row_step(prev_row, d_row):
                first = d_row[0] + prev_row[0]

                def col_step(left, inp):
                    d_ij, up, diag = inp
                    r = d_ij + jnp.minimum(jnp.minimum(up, left), diag)
                    return (r, r)
                _, rest = lax.scan(col_step, first, (d_row[1:], prev_row[1:], prev_row[:-1]))
                row = jnp.concatenate([first[None], rest])
                return (row, row)
            _, rows = lax.scan(row_step, row0, D[1:])
            return jnp.concatenate([row0[None], rows], axis=0)

        def _backtrack(R, T1, T2):
            L = T1 + T2 - 1

            def step(carry, _):
                i, j, done = carry
                valid = jnp.logical_not(done)
                cd = jnp.where((i > 0) & (j > 0), R[jnp.maximum(i - 1, 0), jnp.maximum(j - 1, 0)], BIG)
                cu = jnp.where(i > 0, R[jnp.maximum(i - 1, 0), j], BIG)
                cl = jnp.where(j > 0, R[i, jnp.maximum(j - 1, 0)], BIG)
                choice = jnp.argmin(jnp.stack([cd, cu, cl]))
                ni = jnp.where(choice <= 1, i - 1, i)
                nj = jnp.where((choice == 0) | (choice == 2), j - 1, j)
                at_origin = (i == 0) & (j == 0)
                ni = jnp.where(at_origin, 0, ni)
                nj = jnp.where(at_origin, 0, nj)
                return ((ni, nj, done | at_origin), (i, j, valid))
            init = (jnp.int32(T1 - 1), jnp.int32(T2 - 1), jnp.bool_(False))
            _, (i_idx, j_idx, valid) = lax.scan(step, init, None, length=L)
            return (i_idx, j_idx, valid)

        def _align_one(small, large):
            T_small, d = small.shape
            T_large = large.shape[0]
            D = _pairwise_euclidean(small, large)
            R = _dtw_cost(D)
            i_idx, j_idx, valid = _backtrack(R, T_small, T_large)
            contrib = small[i_idx] * valid[:, None].astype(small.dtype)
            expanded = jnp.zeros((T_large, d), dtype=small.dtype).at[j_idx].add(contrib)
            return expanded
        return jax.vmap(_align_one)(teacher_features, student_features)

    def _L1_ffn_ref(x, input_patterns, process_input_weights, process_values, output_input_weights, output_patterns):
        import jax, jax.numpy as jnp
        import numpy as np

        def gelu(x):
            return jax.nn.gelu(x, approximate=False)
        B, S, d_model = x.shape
        n_input = input_patterns.shape[0]
        n_process = process_input_weights.shape[0]
        n_output = output_input_weights.shape[0]
        k_input = max(n_input // 8, 64)
        k_process = max(n_process // 8, 32)
        k_output = max(n_output // 8, 64)
        input_acts = gelu(jnp.einsum('bsd,nd->bsn', x, input_patterns))
        input_acts_seq = input_acts.mean(axis=1)
        top_input_acts, top_input_idx = jax.lax.top_k(input_acts_seq, k_input)
        brow = jnp.arange(B)[:, None]
        input_repr = jnp.zeros((B, n_input), x.dtype).at[brow, top_input_idx].set(top_input_acts)
        process_acts = gelu(jnp.einsum('bn,pn->bp', input_repr, process_input_weights))
        top_process_acts, top_process_idx = jax.lax.top_k(process_acts, k_process)
        selected_process_values = process_values[top_process_idx]
        process_weights = jax.nn.softmax(top_process_acts, axis=-1)
        aggregated_value = jnp.einsum('bk,bkd->bd', process_weights, selected_process_values)
        output_acts_seq = gelu(jnp.einsum('bd,od->bo', aggregated_value, output_input_weights))
        top_output_acts, top_output_idx = jax.lax.top_k(output_acts_seq, k_output)
        selected_output_patterns = output_patterns[top_output_idx]
        out_per_seq = jnp.einsum('bk,bkm->bm', top_output_acts, selected_output_patterns)
        output = jnp.broadcast_to(out_per_seq[:, None, :], (B, S, d_model))
        return output
    x = _layernorm(x + _L0_attn_ref(x, L0_attn_Wqkv, L0_attn_Wout), axis=-1)
    x = _layernorm(x + _L0_xattn_ref(x, ctx_1024), axis=-1)
    x = _layernorm(x + _L0_ffn_ref(x, L0_ffn_W_r, L0_ffn_W_k, L0_ffn_W_v, L0_ffn_mu_r, L0_ffn_mu_k), axis=-1)
    x = _layernorm(x + _L1_attn_ref(x, L1_attn_gate_W, L1_attn_value_W, L1_attn_gamma, L1_attn_beta), axis=-1)
    x = _layernorm(x + _L1_xattn_ref(ctx_1024, x), axis=-1)
    x = _layernorm(x + _L1_ffn_ref(x, L1_ffn_input_patterns, L1_ffn_process_input_weights, L1_ffn_process_values, L1_ffn_output_input_weights, L1_ffn_output_patterns), axis=-1)
    return x

_drawn_inputs = setup_inputs


def setup_inputs(seed=0):
    import zlib

    import numpy as np

    out = dict(_drawn_inputs(seed))
    spreads = {'L1_attn_gamma': (1.0, 0.2), 'L1_attn_beta': (0.0, 0.1)}
    factors = {'L0_attn_Wqkv': 4.274,
     'L0_ffn_mu_r': 8.0,
     'L1_ffn_input_patterns': 8.0,
     'L1_ffn_process_input_weights': 8.0,
     'L1_ffn_process_values': 8.0,
     'L1_ffn_output_input_weights': 8.0,
     'L1_ffn_output_patterns': 8.0}
    for name, (base, spread) in spreads.items():
        noise = np.random.default_rng([zlib.crc32(name.encode()), seed]).standard_normal(out[name].shape)
        drawn = base * np.exp(spread * noise) if base else spread * noise
        out[name] = jnp.asarray(drawn.astype(out[name].dtype))
    for name, factor in factors.items():
        out[name] = (out[name] * factor).astype(out[name].dtype)
    return out
```

```python
from contextlib import ExitStack

import concourse.bass as bass
from concourse import mybir

F32 = mybir.dt.float32
I32 = mybir.dt.int32
ALU = mybir.AluOpType
ACT = mybir.ActivationFunctionType
AX = mybir.AxisListType

P = 128
SHIFTS = (0, -32, -16, -4, -1, 1, 4, 16, 32)
HALO = 32
BIG = 1e30
EPS = 1e-5


def decoder(nc, x, ctx_in, w_qkv, w_out, w_r, w_k, w_v, mu_r, mu_k, gate_w, value_w, gamma, beta,
            in_pat, proc_w, proc_v, out_w, out_pat, out, wave_d, wave_r):
    B, L, D = x.shape
    TOK = B * L
    NT = TOK // P
    NG = 4
    G = TOK // NG
    TB = L // P
    S = ctx_in.shape[1]
    SB_ = S - P
    HEADS, HD, SEG, DIL, BLK = 16, 16, 512, 8, 64
    KEYS = SEG // DIL
    NPAIR = HEADS // 2
    NSH = len(SHIFTS)
    W = 64
    C = L // W
    SKEW = 2
    T = S + SKEW * (C - 1)
    NIN, NPROC, NOUT, DPV = in_pat.shape[0], proc_w.shape[0], out_w.shape[0], proc_v.shape[1]
    KIN, KPROC, KOUT = max(NIN // 8, 64), max(NPROC // 8, 32), max(NOUT // 8, 64)

    with ExitStack() as top:
        block_stack = ExitStack()

        def sb(stack, name, shape, dt=F32):
            return stack.enter_context(nc.sbuf_tensor(name, shape, dt))

        def sem(name):
            return top.enter_context(nc.semaphore(name))

        X = sb(top, "X", [P, NT, D])
        XT = [sb(top, f"XT{i}", [P, 2, TOK]) for i in range(2)]
        ident = sb(top, "ident", [P, P])
        ones = sb(top, "ones", [P, P])
        nhalf = sb(top, "nhalf", [P, 4])
        bigt = sb(top, "bigt", [P, C * B * T * W // P // 8])
        res = sb(top, "res", [P, 2, 4, D])
        stat = sb(top, "stat", [P, 4, 6])
        mv = sb(top, "mv", [P, NT, 2])
        ve = sb(top, "ve", [P, NT])
        rstd = sb(top, "rstd", [P, NT])
        ctxA = [sb(top, f"ctxA{b}", [P, D]) for b in range(B)]
        ctxB = [sb(top, f"ctxB{b}", [P, D]) for b in range(B)]
        ctxBB = sb(top, "ctxBB", [P, D])
        ctxT = [sb(top, f"ctxT{b}", [P, 2, S]) for b in range(B)]

        a_mem = ExitStack()
        rawq = sb(a_mem, "rawq", [P, 6, D])
        raws = sb(a_mem, "raws", [P, 10, D])
        rawg = sb(a_mem, "rawg", [P, 2 * NSH, D])
        wqkvT = sb(a_mem, "wqkvT", [P, 2, 3 * D])
        wsT = sb(a_mem, "wsT", [P, 5, 2, D])
        gateT = sb(a_mem, "gateT", [P, 2, NSH * D])
        mus = sb(a_mem, "mus", [P, 2, 2])
        omm = sb(a_mem, "omm", [P, 2, 2])
        gam = sb(a_mem, "gam", [P, D])
        bet = sb(a_mem, "bet", [P, D])
        at_mem = ExitStack()
        qT = sb(at_mem, "qT", [P, 2, TOK])
        kbd = sb(at_mem, "kbd", [P, 2, NG, 2, KEYS])
        vbd = sb(at_mem, "vbd", [P, NG, NPAIR, 2, HD])
        halves = sb(at_mem, "halves", [P, 2, HD])
        pidx = sb(at_mem, "pidx", [P, 1], I32)
        pbit = sb(at_mem, "pbit", [P, 1], I32)
        parm = sb(at_mem, "parm", [P, 2])
        cmax = sb(at_mem, "cmax", [P, 32, SEG // BLK])
        Sm = sb(at_mem, "Sm", [P, 4, SEG])
        Wx = sb(at_mem, "Wx", [P, 8, SEG])
        den = sb(at_mem, "den", [P, SEG])
        rden = sb(at_mem, "rden", [P, SEG])
        oT = sb(at_mem, "oT", [P, 2, TOK])
        at_mem.close()
        ff_mem = ExitStack()
        Et = sb(ff_mem, "Et", [P, 4, S])
        WT2 = sb(ff_mem, "WT2", [P, 4, 2, P])
        mx = sb(ff_mem, "mx", [P, NT])
        nmx = sb(ff_mem, "nmx", [P, NT])
        ssum = sb(ff_mem, "ssum", [P, NT])
        rsum = sb(ff_mem, "rsum", [P, NT])
        mixT = sb(ff_mem, "mixT", [P, 2, TOK])
        mtmp = sb(ff_mem, "mtmp", [P, 2, L])
        rgate = sb(ff_mem, "rgate", [P, NT, D])
        krel = sb(ff_mem, "krel", [P, 2, G])
        ff_mem.close()
        mix_mem = ExitStack()
        VW = L + 2 * HALO
        Vh = sb(mix_mem, "Vh", [P, 2, B, VW])
        gs = sb(mix_mem, "gs", [P, 4, G])
        pr = sb(mix_mem, "pr", [P, 4, G])
        acc = sb(mix_mem, "acc", [P, 2, 2, G])
        y2 = sb(mix_mem, "y2", [P, 4, D])
        mix_mem.close()
        a_mem.close()

        b_mem = ExitStack()
        aa = sb(b_mem, "aa", [P, 3])
        adump = sb(b_mem, "adump", [P, D])
        Rc = sb(b_mem, "Rc", [P, 3, L + 1])
        Rp = sb(b_mem, "Rp", [P, 3, L + 1])
        iota2 = sb(b_mem, "iota2", [P, L])
        iotaf = sb(b_mem, "iotaf", [1, 2 * L])
        Zi = sb(b_mem, "Zi", [P, 3, L], I32)
        zrow = sb(b_mem, "zrow", [1, B, S + 1])
        zcol = sb(b_mem, "zcol", [P, 4, 2])
        w_mem = ExitStack()
        ctx2 = [sb(w_mem, f"ctx2{b}", [P, 2, S]) for b in range(B)]
        Drow = sb(w_mem, "Drow", [P, 3, L])
        Dw = sb(w_mem, "Dw", [64, T, W])
        RING = 64
        Rw = sb(w_mem, "Rw", [64, RING, W + 1])
        Mw = sb(w_mem, "Mw", [64, 2, W])
        w_mem.close()
        p_mem = ExitStack()
        tmpa = sb(p_mem, "tmpa", [P, L])
        tmpb = sb(p_mem, "tmpb", [P, L])
        Zf = sb(p_mem, "Zf", [P, L])
        Pm = sb(p_mem, "Pm", [P, 4, L])
        p_mem.close()
        b_mem.close()
        c_mem = ExitStack()
        ipraw = sb(c_mem, "ipraw", [P, NIN // P, D])
        ipT = sb(c_mem, "ipT", [P, 2, NIN])
        owraw = sb(c_mem, "owraw", [P, NOUT // P, DPV])
        owT = sb(c_mem, "owT", [P, NOUT])
        pv = sb(c_mem, "pv", [P, NPROC // P, DPV])
        op = sb(c_mem, "op", [P, NOUT // P, D])
        acts = sb(c_mem, "acts", [P, B, 16])
        lt = sb(c_mem, "lt", [P, P])
        gt = sb(c_mem, "gt", [P, P])
        row = sb(c_mem, "row", [P, NIN])
        dg = sb(c_mem, "dg", [P, 2, 4, P])
        ddump = sb(c_mem, "ddump", [P, 2, 2, P])
        mact = sb(c_mem, "mact", [P, 16])
        wt = sb(c_mem, "wt", [P, 8])
        cdump = sb(c_mem, "cdump", [P, 2, NIN])
        cnt = sb(c_mem, "cnt", [P, 4, 16])
        rank = sb(c_mem, "rank", [P, 2, 16])
        msk = sb(c_mem, "msk", [P, 16])
        kept = sb(c_mem, "kept", [P, 16])
        pwt = sb(c_mem, "pwt", [P, 3, NIN])
        pacc = sb(c_mem, "pacc", [P, 8])
        pact = sb(c_mem, "pact", [P, 16])
        pex = sb(c_mem, "pex", [P, 8])
        sc = sb(c_mem, "sc", [P, 8])
        agg = sb(c_mem, "agg", [P, 1])
        oact = sb(c_mem, "oact", [P, 16])
        c_mem.close()

        PS = top.enter_context(nc.psum_tensor("PS", [P, 8, 512], F32))
        TP = [PS[:, i, :] for i in range(2)]
        M = [PS[:, 2 + i, :] for i in range(6)]

        ld_wq, ld_ws, ld_wg, ld_ctx, ld_vec = (sem(n) for n in ("ld_wq", "ld_ws", "ld_wg", "ld_ctx", "ld_vec"))
        ld_x = [sem(f"ld_x{g}") for g in range(NG)]
        consts = sem("consts")
        tp_done, tp_out = sem("tp_done"), sem("tp_out")
        dv = sem("dv")
        q_mm, q_sb, k_mm, k_sb, v_mm, v_sb = (sem(n) for n in ("q_mm", "q_sb", "k_mm", "k_sb", "v_mm", "v_sb"))
        s_mm, s_sub, w_exp, nd_mm, o_sb = (sem(n) for n in ("s_mm", "s_sub", "w_exp", "nd_mm", "o_sb"))
        par_ok = sem("par_ok")
        NL = range(1, 7)
        pm = [None] + [sem(f"pm{n}") for n in NL]
        rs = [None] + [sem(f"rs{n}") for n in NL]
        vr = [None] + [sem(f"vr{n}") for n in NL]
        sd = [None] + [sem(f"sd{n}") for n in NL]
        xo = [None] + [sem(f"xo{n}") for n in NL]
        iv, isd = sem("iv"), sem("isd")
        l_mm, l_mx, l_exp = sem("l_mm"), sem("l_mx"), sem("l_exp")
        mix_sb, r_mm, r_sb, kk_mm, kk_rel, kk_sb = (sem(n) for n in ("mix_sb", "r_mm", "r_sb", "kk_mm", "kk_rel", "kk_sb"))
        vv_mm, vv_sb, halo, g_mm, g_sig, g_mul, acc_sb, at_mm, at_rd = (
            sem(n) for n in ("vv_mm", "vv_sb", "halo", "g_mm", "g_sig", "g_mul", "acc_sb", "at_mm", "at_rd"))
        wt_half, k_free, c_zero, big_ok = sem("wt_half"), sem("k_free"), sem("c_zero"), sem("big_ok")
        a_ok, sq_sb, c2_sb, d_mm, d_max, d_rt, dw_fill, big_st, dw_st, dw_ld = (
            sem(n) for n in ("a_ok", "sq_sb", "c2_sb", "d_mm", "d_max", "d_rt", "dw_fill", "big_st", "dw_st", "dw_ld"))
        w_init, w_min, w_row, w_edge = (sem(n) for n in ("w_init", "w_min", "w_row", "w_edge"))
        rw_st = [sem(f"rw_st{i}") for i in range(-(-T // 16))]
        rrA_ld, rrB_ld, pad_ok, z_ok, io_f, z_mm, p_ok = (
            sem(n) for n in ("rrA_ld", "rrB_ld", "pad_ok", "z_ok", "io_f", "z_mm", "p_ok"))
        chased = [sem(f"chased{b}") for b in range(B)]
        ld_ip, ld_ow, ld_pv, ld_op = sem("ld_ip"), sem("ld_ow"), sem("ld_pv"), sem("ld_op")
        ld_pw = [sem(f"ld_pw{i}") for i in range(3)]
        pw_used = sem("pw_used")
        a_mm, a_gelu, dg_ok, bc_mm, bc_out, p_pre, p_act, c_ok = (
            sem(n) for n in ("a_mm", "a_gelu", "dg_ok", "bc_mm", "bc_out", "p_pre", "p_act", "c_ok"))
        e_arg, e_ok, wt_ok, tot_mm, agg_ok, oa_mm, oa_act, ko_ok, f_mm = (
            sem(n) for n in ("e_arg", "e_ok", "wt_ok", "tot_mm", "agg_ok", "oa_mm", "oa_act", "ko_ok", "f_mm"))
        out_st = sem("out_st")

        TP_WQ, TP_X0, TP_CTX, TP_WS, TP_WG = 0, 6, 22, 26, 36
        TP_X1 = TP_WG + 2 * NSH
        TP_E = TP_X1 + NT
        TP_X2 = TP_E + NT
        TP_X3 = TP_X2 + NT
        TP_X4 = TP_X3 + NT
        TP_IP = TP_X4 + NT
        TP_OW = TP_IP + NIN // P
        TP_X5 = TP_OW + NOUT // P // 2

        SIDE = [range(0, 4), range(4, 9), range(9, 14), range(14, 19), range(19, 24), range(24, 28), range(28, 32), range(0)]
        NP_ = NPROC // P
        STEP = 16
        STORES = {}
        for t0 in range(0, T, STEP):
            n = min(T, t0 + STEP) - t0
            STORES[t0] = 2 * B if (t0 + 1) % RING + n > RING else B

        def stored(eng, t):
            eng.wait_ge(rw_st[t // STEP], 16 * STORES[t // STEP * STEP])

        block = block_stack.enter_context(nc.Block())

        def rows(w):
            return w.rearrange("(r p) c -> p r c", p=P)

        @block.sync
        def _(sp):
            xt = x.rearrange("b l d -> (b l) d").rearrange("(t p) d -> p t d", p=P)
            ot = out.rearrange("b l d -> (b l) d").rearrange("(t p) d -> p t d", p=P)
            sp.dma_start(rawq[:, :, :], rows(w_qkv)).then_inc(ld_wq, 16)
            for g in range(NG):
                sp.dma_start(X[:, 4 * g:4 * g + 4, :], xt[:, 4 * g:4 * g + 4, :]).then_inc(ld_x[g], 16)
            sp.wait_ge(c_zero, 1)
            for b in range(B):
                sp.dma_start(ctxA[b][:, :], ctx_in[b, 0:P, :]).then_inc(ld_ctx, 16)
                sp.dma_start(ctxB[b][0:SB_, :], ctx_in[b, P:S, :]).then_inc(ld_ctx, 16)
                sp.dma_start(ctxBB[32 * b:32 * b + SB_, :], ctx_in[b, P:S, :]).then_inc(ld_ctx, 16)
            for n, w in enumerate((w_out, w_r, w_k, w_v, value_w)):
                sp.dma_start(raws[:, 2 * n:2 * n + 2, :], rows(w)).then_inc(ld_ws, 16)
            sp.dma_start(rawg[:, :, :], rows(gate_w)).then_inc(ld_wg, 16)
            with nc.allow_non_contiguous_dma(reason="two vectors of 256 values onto partitions"):
                for n, v in enumerate((mu_r, mu_k)):
                    sp.dma_start(mus[:, :, n:n + 1], v.rearrange("(k p) -> p k", p=P).unsqueeze(2)).then_inc(ld_vec, 16)
            for t_, v in ((gam, gamma), (bet, beta)):
                sp.dma_start(t_[:, :], bass.AP(tensor=v.tensor, offset=v.offset, ap=[[0, P], [1, D]])).then_inc(ld_vec, 16)
            sp.wait_ge(big_ok, 1)
            per = C * B * T * W // P
            sp.dma_start(bass.AP(tensor=wave_d.tensor, offset=wave_d.offset, ap=[[per, P], [per // 8, 8], [1, per // 8]]),
                         bass.AP(tensor=bigt[:, :].tensor, offset=bigt[:, :].offset, ap=[bigt[:, :].ap[0], [0, 8], [1, per // 8]])).then_inc(big_st, 16)

            def skewed(dram, b, i0, n):
                return bass.AP(tensor=dram.tensor, offset=dram.offset + b * C * T * W + i0 * W,
                               ap=[[W, n], [(T + SKEW) * W, C], [1, W]])

            def chunks(ap):
                return ap.rearrange("p (c w) -> p c w", w=W)

            sp.wait_ge(big_st, 16)
            for b in range(B):
                sp.wait_ge(d_rt, 4 * b + 3)
                sp.dma_start(skewed(wave_d, b, 0, P), chunks(Drow[:, b, :])).then_inc(dw_st, 16)
                sp.wait_ge(d_rt, 4 * b + 4)
                sp.dma_start(skewed(wave_d, b, P, SB_), chunks(Drow[32 * b:32 * b + SB_, 2, :])).then_inc(dw_st, 16)
            sp.wait_ge(dw_st, 64)
            sp.wait_ge(dw_fill, 1)
            for b in range(B):
                sp.dma_start(Dw[32 * b + 1:32 * b + 1 + C, :, :].rearrange("p t w -> p (t w)"),
                             wave_d[b * C:(b + 1) * C].rearrange("p t w -> p (t w)")).then_inc(dw_ld, 16)
            tA = P + SKEW * (C - 1)
            for t0 in list(range(0, T, STEP)):
                t1 = min(T, t0 + STEP)
                sp.wait_ge(w_row, t1)
                for b in range(B):
                    s0 = (t0 + 1) % RING
                    n0 = min(t1 - t0, RING - s0)
                    sp.dma_start(wave_r[b * C:(b + 1) * C, t0:t0 + n0, :],
                                 Rw[32 * b + 1:32 * b + 1 + C, s0:s0 + n0, 1:W + 1]).then_inc(rw_st[t0 // STEP], 16)
                    if n0 < t1 - t0:
                        sp.dma_start(wave_r[b * C:(b + 1) * C, t0 + n0:t1, :],
                                     Rw[32 * b + 1:32 * b + 1 + C, 0:t1 - t0 - n0, 1:W + 1]).then_inc(rw_st[t0 // STEP], 16)
                if t0 < tA <= t1:
                    for s0 in range(0, t1, STEP):
                        sp.wait_ge(rw_st[s0 // STEP], 16 * STORES[s0])
                    sp.wait_ge(pad_ok, 6)
                    for b in range(B):
                        sp.dma_start(chunks(Rc[:, b, 1:L + 1]), skewed(wave_r, b, 0, P)).then_inc(rrA_ld, 16)
                        sp.dma_start(chunks(Rp[1:P, b, 1:L + 1]), skewed(wave_r, b, 0, P - 1)).then_inc(rrA_ld, 16)
            for s0 in range(0, T, STEP):
                sp.wait_ge(rw_st[s0 // STEP], 16 * STORES[s0])
            for b in range(B):
                q0 = 32 * b
                sp.dma_start(chunks(Rc[q0:q0 + SB_, 2, 1:L + 1]), skewed(wave_r, b, P, SB_)).then_inc(rrB_ld, 16)
                sp.dma_start(chunks(Rp[q0:q0 + SB_, 2, 1:L + 1]), skewed(wave_r, b, P - 1, SB_)).then_inc(rrB_ld, 16)
            sp.wait_ge(pm[5], NT)
            sp.dma_start(ipraw[:, :, :], rows(in_pat)).then_inc(ld_ip, 16)
            sp.dma_start(owraw[:, :, :], rows(out_w)).then_inc(ld_ow, 16)
            sp.dma_start(pv[:, :, :], rows(proc_v)).then_inc(ld_pv, 16)
            sp.dma_start(op[:, :, :], rows(out_pat)).then_inc(ld_op, 16)
            for n in range(B * NP_):
                if n >= 3:
                    sp.wait_ge(pw_used, n - 2)
                sp.dma_start(pwt[:, n % 3, :], rows(proc_w)[:, n % NP_, :]).then_inc(ld_pw[n % 3], 16)
            for g in range(NG):
                sp.wait_ge(xo[6], 4 * g + 4)
                sp.dma_start(ot[:, 4 * g:4 * g + 4, :], X[:, 4 * g:4 * g + 4, :]).then_inc(out_st, 16)
            sp.wait_ge(out_st, 16 * NG)

        def walk_back(eng, copy, b):
            at = L - 1
            for i in range(S - 1, -1, -1):
                if i == S - 1:
                    eng.wait_ge(z_ok, 1)
                if i == P - 1:
                    eng.wait_ge(z_ok, 2 + b)
                q = i if i < P else 32 * b + i - P
                z = eng.value_load(Zi[q:q + 1, b if i < P else 2, bass.ds(at, 1)], min_val=0, max_val=2 * (L - 1))
                copy(zrow[:, b, i:i + 1], iotaf[:, bass.ds(z, 1)]).then_inc(chased[b], 1)
                at = z // 2

        @block.gpsimd
        def _(pool):
            nc.gpsimd.memset(ctxBB[:, :], 0.0).then_inc(c_zero, 1)
            nc.gpsimd.memset(ident[:, :], 0.0).then_inc(consts, 1)
            nc.gpsimd.memset(ones[:, :], 1.0).then_inc(consts, 1)
            nc.gpsimd.memset(nhalf[:, :], -0.5).then_inc(consts, 1)
            nc.gpsimd.iota(pidx[:, :], pattern=[[0, 1]], base=0, channel_multiplier=1).then_inc(consts, 1)
            nc.gpsimd.memset(vbd[:, :, :, :, :], 0.0).then_inc(consts, 1)
            nc.gpsimd.memset(halves[:, :, :], 0.0).then_inc(consts, 1)
            pool.wait_ge(consts, 6)
            nc.gpsimd.affine_select(out=ident[:, :], in_=ident[:, :], compare_op=ALU.not_equal, fill=1.0, base=0,
                                    pattern=[[-1, P]], channel_multiplier=1).then_inc(consts, 1)
            for h in range(2):
                pool.wait_ge(consts, 7 + h)
                nc.gpsimd.memset(halves[64 * h:64 * h + 64, h, :], 1.0).then_inc(consts, 1)
            pool.wait_ge(consts, 9)
            nc.gpsimd.memset(bigt[:, :], BIG).then_inc(big_ok, 1)

            def inv_std(seen, made, g):
                pool.wait_ge(seen, g + 1)
                nc.gpsimd.tensor_tensor(rstd[:, 4 * g:4 * g + 4], ve[:, 4 * g:4 * g + 4], nhalf[:, :], ALU.pow).then_inc(made, 1)

            for n in (1, 2, 3):
                for g in range(NG):
                    inv_std(vr[n], sd[n], g)
            for g in range(NG):
                inv_std(iv, isd, g)
                inv_std(vr[4], sd[4], g)
            pool.wait_ge(xo[4], NT)
            nc.gpsimd.memset(Dw[:, :, :], BIG).then_inc(dw_fill, 1)
            nc.gpsimd.memset(Rc[:, :, 0:1], BIG).then_inc(pad_ok, 1)
            nc.gpsimd.memset(Rp[:, :, 0:1], BIG).then_inc(pad_ok, 1)
            nc.gpsimd.memset(Rp[0:1, 0, 1:L + 1], BIG).then_inc(pad_ok, 1)
            nc.gpsimd.memset(Rp[0:1, 1, 1:L + 1], BIG).then_inc(pad_ok, 1)
            nc.gpsimd.memset(Rc[:, 2, 1:L + 1], BIG).then_inc(pad_ok, 1)
            nc.gpsimd.memset(Rp[:, 2, 1:L + 1], BIG).then_inc(pad_ok, 1)
            nc.gpsimd.memset(zcol[:, :, :], BIG).then_inc(pad_ok, 1)
            nc.gpsimd.iota(Zi[:, 2, :], pattern=[[2, L]], base=0, channel_multiplier=0).then_inc(io_f, 1)
            nc.gpsimd.iota(Zi[0:1, 0:2, :], pattern=[[1, 2 * L]], base=0, channel_multiplier=0).then_inc(io_f, 1)
            nc.gpsimd.memset(zrow[:, :, S:S + 1], float(2 * (L - 1))).then_inc(io_f, 1)
            pool.wait_ge(io_f, 3)
            nc.gpsimd.tensor_copy(iota2[:, :], Zi[:, 2, :]).then_inc(io_f, 1)
            nc.gpsimd.tensor_copy(iotaf[:, :], Zi[0:1, 0:2, :].rearrange("p a b -> p (a b)")).then_inc(io_f, 1)
            pool.wait_ge(io_f, 5)
            walk_back(pool, nc.gpsimd.tensor_copy, 1)
            for g in range(NG):
                inv_std(vr[5], sd[5], g)
            pool.wait_ge(pm[5], NT)
            nc.gpsimd.memset(lt[:, :], 1.0).then_inc(c_ok, 1)
            nc.gpsimd.memset(gt[:, :], 1.0).then_inc(c_ok, 1)
            pool.wait_ge(c_ok, 2)
            nc.gpsimd.affine_select(out=lt[:, :], in_=lt[:, :], compare_op=ALU.is_gt, fill=0.0, base=0,
                                    pattern=[[-1, P]], channel_multiplier=1).then_inc(c_ok, 1)
            nc.gpsimd.affine_select(out=gt[:, :], in_=gt[:, :], compare_op=ALU.is_gt, fill=0.0, base=0,
                                    pattern=[[1, P]], channel_multiplier=-1).then_inc(c_ok, 1)
            for g in range(NG):
                inv_std(vr[6], sd[6], g)

        @block.scalar
        def _(act):
            def pair(i):
                return TP[i % 2][:, 0:2 * P].rearrange("p (k c) -> p k c", k=2)

            def tp_copy(i, dst, n=P):
                act.wait_ge(tp_done, i + 1)
                nc.scalar.copy(dst, pair(i)[:, :, 0:n]).then_inc(tp_out, 1)

            def x_copy(first, buf, t):
                tp_copy(first + t, XT[buf][:, :, P * t:P * t + P])

            for r in range(6):
                tp_copy(TP_WQ + r, wqkvT[:, :, P * r:P * r + P])
            for t in range(NT):
                x_copy(TP_X0, 0, t)
            for u in range(32):
                act.wait_ge(s_sub, u + 1)
                if u >= 8:
                    act.wait_ge(nd_mm, u // 4 - 1)
                nc.scalar.activation(Wx[:, u % 8, :], Sm[:, u % 4, :], ACT.Exp, scale=float(HD) ** -0.5).then_inc(w_exp, 1)
                if u % 4 == 3:
                    for n in SIDE[u // 4]:
                        if n < 4:
                            tp_copy(TP_CTX + n, ctxT[n // 2][:, :, 0:P] if n % 2 == 0 else ctxT[n // 2][:, :, P:S], P if n % 2 == 0 else SB_)
                        elif n < 14:
                            tp_copy(TP_CTX + n, wsT[:, (n - 4) // 2, :, P * (n % 2):P * (n % 2) + P])
                        else:
                            tp_copy(TP_CTX + n, gateT[:, :, P * (n - 14):P * (n - 14) + P])
            for t in range(NT):
                x_copy(TP_X1, 1, t)
            for t in range(NT + 2):
                if t < NT:
                    act.wait_ge(l_mx, t + 1)
                    if t >= 4:
                        act.wait_ge(tp_done, TP_E + t - 3)
                    nc.scalar.activation(Et[:, t % 4, :], M[4 + t % 2][:, 0:S], ACT.Exp, scale=float(D) ** -0.5,
                                         bias=nmx[:, t:t + 1], accum_out=ssum[:, t:t + 1]).then_inc(l_exp, 1)
                if t >= 2:
                    s = t - 2
                    act.wait_ge(tp_done, TP_E + s + 1)
                    if s >= 4:
                        act.wait_ge(pm[2], s - 3)
                    src = pair(TP_E + s)
                    nc.scalar.copy(WT2[:, s % 4, 0, :], src[:, 0, :]).then_inc(wt_half, 1)
                    nc.scalar.copy(WT2[0:SB_, s % 4, 1, :], src[0:SB_, 1, :]).then_inc(tp_out, 1)
            for t in range(NT):
                x_copy(TP_X2, 0, t)
            for t in range(NT):
                act.wait_ge(r_mm, t + 1)
                nc.scalar.activation(rgate[:, t, :], M[t % 2][:, 0:D], ACT.Sigmoid).then_inc(r_sb, 1)
            for u in range(8):
                act.wait_ge(kk_mm, u + 1)
                if u >= 2:
                    act.wait_ge(kk_sb, u - 1)
                nc.scalar.activation(krel[:, u % 2, :], M[2 + u % 2], ACT.Relu).then_inc(kk_rel, 1)
            for t in range(NT):
                x_copy(TP_X3, 1, t)
            for u in range(8):
                c, g = u // NG, u % NG
                act.wait_ge(vv_mm, u + 1)
                c0 = HALO + (g % 2) * G
                nc.scalar.copy(Vh[:, c, g // 2, c0:c0 + G], M[u % 2]).then_inc(vv_sb, 1)
            for u in range(NG * 2 * NSH):
                act.wait_ge(g_mm, u + 1)
                if u >= 4:
                    act.wait_ge(g_mul, u - 3)
                nc.scalar.activation(gs[:, u % 4, :], M[u % 4], ACT.Sigmoid).then_inc(g_sig, 1)
            for t in range(NT):
                x_copy(TP_X4, 0, t)
                if t % 4 == 3:
                    g = t // 4
                    act.wait_ge(tp_out, TP_X4 + t + 1)
                    for k in range(2):
                        nc.scalar.activation(XT[1][:, k, G * g:G * g + G], XT[0][:, k, G * g:G * g + G], ACT.Square).then_inc(sq_sb, 1)
            for u in range(2 * NG):
                g, r = u // 2, u % 2
                b, h = g // 2, g % 2
                act.wait_ge(d_max, u + 1)
                q0, n = (0, P) if r == 0 else (32 * b, SB_)
                dst = Drow[q0:q0 + n, b if r == 0 else 2, G * h:G * h + G]
                nc.scalar.activation(dst, dst, ACT.Sqrt).then_inc(d_rt, 1)
            act.wait_ge(io_f, 5)
            walk_back(act, nc.scalar.copy, 0)
            for r in range(NIN // P):
                tp_copy(TP_IP + r, ipT[:, :, P * r:P * r + P])
            for r in range(NOUT // P // 2):
                tp_copy(TP_OW + r, owT[:, 2 * P * r:2 * P * r + 2 * P].rearrange("p (k c) -> p k c", k=2))
            for t in range(NT):
                x_copy(TP_X5, 1, t)
            for u in range(B * 16):
                act.wait_ge(a_mm, u + 1)
                both = PS[:, 2 + 2 * (u % 2):4 + 2 * (u % 2), :]
                nc.scalar.activation(both, both, ACT.Gelu,
                                     accum_out=acts[:, u // 16, u % 16:u % 16 + 1]).then_inc(a_gelu, 1)

            def spread_copy(base, n):
                for i in range(n):
                    act.wait_ge(bc_mm, base + i + 1)
                    nc.scalar.copy(row[:, 512 * i:512 * i + 512], M[(base + i) % 2]).then_inc(bc_out, 1)

            for b in range(B):
                o = 14 * b
                act.wait_ge(k_free, 4 * b) if b else None
                spread_copy(o, 4)
                act.wait_ge(k_free, 4 * b + 1)
                spread_copy(o + 4, 4)
                act.wait_ge(p_pre, b + 1)
                nc.scalar.activation(pact[:, 0:NP_], pacc[:, :], ACT.Gelu).then_inc(p_act, 1)
                act.wait_ge(k_free, 4 * b + 2)
                spread_copy(o + 8, 2)
                act.wait_ge(e_arg, b + 1)
                nc.scalar.activation(pex[:, :], pact[:, 0:NP_], ACT.Exp, bias=sc[:, 1:2]).then_inc(e_ok, 1)
                act.wait_ge(oa_mm, b + 1)
                nc.scalar.activation(oact[:, :], M[2][:, 0:16], ACT.Gelu).then_inc(oa_act, 1)
                act.wait_ge(k_free, 4 * b + 3)
                spread_copy(o + 10, 4)

        @block.tensor
        def _(pe):
            def turn(i, lo, hi, n=P):
                if i >= 2:
                    pe.wait_ge(tp_out, i - 1)
                nc.tensor.transpose(TP[i % 2][0:lo.shape[1], 0:n], lo, ident[0:n, 0:n])
                nc.tensor.transpose(TP[i % 2][0:hi.shape[1], P:P + n], hi, ident[0:n, 0:n]).then_inc(tp_done, 1)

            def turn_tile(i, src, n=P):
                turn(i, src[:, 0:P], src[:, P:2 * P], n)

            def accumulate(dst, parts, sem_=None):
                for i, (a, b_) in enumerate(parts):
                    last = nc.tensor.matmul(dst, a, b_, start=i == 0, stop=i == len(parts) - 1)
                if sem_ is not None:
                    last.then_inc(sem_, 1)

            def side_jobs(q):
                for n in SIDE[q]:
                    i = TP_CTX + n
                    if n < 4:
                        pe.wait_ge(ld_ctx, 96)
                        if n % 2 == 0:
                            turn_tile(i, ctxA[n // 2][:, :])
                        else:
                            turn_tile(i, ctxB[n // 2][0:SB_, :], SB_)
                    elif n < 14:
                        pe.wait_ge(ld_ws, 80)
                        turn_tile(i, raws[:, n - 4, :])
                    else:
                        pe.wait_ge(ld_wg, 16)
                        turn_tile(i, rawg[:, n - 14, :])

            pe.wait_ge(consts, 9)
            pe.wait_ge(ld_wq, 16)
            for r in range(6):
                turn_tile(TP_WQ + r, rawq[:, r, :])
            for t in range(NT):
                if t % 4 == 0:
                    pe.wait_ge(ld_x[t // 4], 16)
                turn_tile(TP_X0 + t, X[:, t, :])
            pe.wait_ge(tp_out, TP_X0 + NT)
            for m in range(2):
                accumulate(M[2][:, 256 * m:256 * m + 256],
                           [(wqkvT[:, k, D + P * m:D + P * m + P], XT[0][:, k, ::DIL]) for k in range(2)], k_mm)
            for g in range(NG):
                keys = [XT[0][:, k, SEG * g:SEG * g + SEG:DIL] for k in range(2)]
                for h in range(2):
                    accumulate(M[3 + g // 2][64 * h:64 * h + 64, 256 * (g % 2):256 * (g % 2) + 256],
                               [(keys[k], wqkvT[:, k, 2 * D:3 * D]) for k in range(2)], v_mm if h else None)
            for u in range(8):
                g, m = u // 2, u % 2
                if u >= 2:
                    pe.wait_ge(q_sb, u - 1)
                accumulate(M[u % 2], [(wqkvT[:, k, P * m:P * m + P], XT[0][:, k, G * g:G * g + G]) for k in range(2)], q_mm)
            pe.wait_ge(q_sb, 8)
            pe.wait_ge(k_sb, 4)
            pe.wait_ge(v_sb, 8)
            for q in range(9):
                if q < 8:
                    g, m = q // 2, q % 2
                    for j in range(4):
                        if q >= 1:
                            pe.wait_ge(s_sub, 4 * (q - 1) + j + 1)
                        r = slice(32 * j, 32 * j + 32)
                        nc.tensor.matmul(M[j], kbd[r, m, g, :, :].rearrange("p h k -> p (h k)"),
                                         qT[r, m, G * g:G * g + G], start=True, stop=True).then_inc(s_mm, 1)
                if q >= 1:
                    g, m = (q - 1) // 2, (q - 1) % 2
                    if q >= 2:
                        pe.wait_ge(o_sb, q - 1)
                    for j in range(4):
                        u = 4 * (q - 1) + j
                        pe.wait_ge(w_exp, u + 1)
                        r = slice(32 * j, 32 * j + 32)
                        nc.tensor.matmul(M[4][r, :], vbd[:, g, 4 * m + j, :, :].rearrange("p h d -> p (h d)"),
                                         Wx[:, u % 8, :], start=True, stop=True)
                        last = nc.tensor.matmul(M[5][r, :], halves[:, :, :].rearrange("p h d -> p (h d)"),
                                                Wx[:, u % 8, :], start=True, stop=True)
                    last.then_inc(nd_mm, 1)
                    side_jobs(q - 1)
            for t in range(NT):
                pe.wait_ge(o_sb, 2 * (t // 4) + 2)
                pe.wait_ge(s_sub, 32)
                if t >= 4:
                    pe.wait_ge(rs[1], t - 3)
                accumulate(M[t % 4][:, 0:D], [(oT[:, k, P * t:P * t + P], wsT[:, 0, k, :]) for k in range(2)], pm[1])

            def turn_x(first, n):
                for t in range(NT):
                    pe.wait_ge(xo[n], t + 1)
                    turn_tile(first + t, X[:, t, :])

            turn_x(TP_X1, 1)
            for t in range(NT + 3):
                if t < NT:
                    pe.wait_ge(tp_out, TP_X1 + t + 1)
                    if t >= 2:
                        pe.wait_ge(l_exp, t - 1)
                    accumulate(M[4 + t % 2][:, 0:S], [(XT[1][:, k, P * t:P * t + P], ctxT[t // TB][:, k, :]) for k in range(2)], l_mm)
                if 1 <= t <= NT:
                    s = t - 1
                    i = TP_E + s
                    pe.wait_ge(l_exp, s + 1)
                    pe.wait_ge(tp_out, i - 1)
                    nc.tensor.transpose(TP[i % 2][:, 0:P], Et[:, s % 4, 0:P], ident[:, :])
                    nc.tensor.transpose(TP[i % 2][0:SB_, P:2 * P], Et[:, s % 4, P:S], ident[:, :]).then_inc(tp_done, 1)
                if t >= 3:
                    s = t - 3
                    pe.wait_ge(tp_out, TP_E + s + 1)
                    pe.wait_ge(wt_half, s + 1)
                    if s >= 4:
                        pe.wait_ge(rs[2], s - 3)
                    accumulate(M[s % 4][:, 0:D], [(WT2[:, s % 4, 0, :], ctxA[s // TB][:, :]),
                                                  (WT2[0:SB_, s % 4, 1, :], ctxB[s // TB][0:SB_, :])], pm[2])
            turn_x(TP_X2, 2)
            pe.wait_ge(mix_sb, 2)
            for t in range(NT):
                if t % TB == 0:
                    pe.wait_ge(mix_sb, 2 * (t // TB) + 2)
                pe.wait_ge(rs[2], NT)
                if t >= 2:
                    pe.wait_ge(r_sb, t - 1)
                accumulate(M[t % 2][:, 0:D], [(mixT[:, k, P * t:P * t + P], wsT[:, 1, k, :]) for k in range(2)], r_mm)
            for u in range(8):
                g, m = u // 2, u % 2
                pe.wait_ge(mix_sb, 4 + 2 * (g // 2) + 2)
                if u >= 2:
                    pe.wait_ge(kk_rel, u - 1)
                accumulate(M[2 + u % 2], [(wsT[:, 2, k, P * m:P * m + P], XT[0][:, k, G * g:G * g + G]) for k in range(2)], kk_mm)
            pe.wait_ge(r_sb, NT)
            for t in range(NT):
                pe.wait_ge(kk_sb, 8)
                if t >= 4:
                    pe.wait_ge(rs[3], t - 3)
                accumulate(M[t % 4][:, 0:D], [(XT[1][:, k, P * t:P * t + P], wsT[:, 3, k, :]) for k in range(2)], pm[3])
            turn_x(TP_X3, 3)
            pe.wait_ge(tp_out, TP_X3 + NT)
            pe.wait_ge(rs[3], NT)
            for u in range(8):
                c, g = u // NG, u % NG
                if u >= 2:
                    pe.wait_ge(vv_sb, u - 1)
                accumulate(M[u % 2], [(wsT[:, 4, k, P * c:P * c + P], XT[1][:, k, G * g:G * g + G]) for k in range(2)], vv_mm)
            pe.wait_ge(vv_sb, 8)

            def turn_mixed(g):
                pe.wait_ge(acc_sb, 2 * g + 2)
                pe.wait_ge(at_rd, 4 * g) if g else None
                for j in range(4):
                    for c in range(2):
                        c0 = 256 * (j % 2) + P * c
                        last = nc.tensor.transpose(M[4 + j // 2][:, c0:c0 + P], acc[:, g % 2, c, P * j:P * j + P], ident[:, :])
                    last.then_inc(at_mm, 1)

            for g in range(NG):
                for c in range(2):
                    for n in range(NSH):
                        u = (2 * g + c) * NSH + n
                        if u >= 4:
                            pe.wait_ge(g_sig, u - 3)
                        e0 = D * n + P * c
                        accumulate(M[u % 4], [(gateT[:, k, e0:e0 + P], XT[1][:, k, G * g:G * g + G]) for k in range(2)], g_mm)
                    if c == 0 and g >= 1:
                        turn_mixed(g - 1)
            turn_mixed(NG - 1)
            turn_x(TP_X4, 4)
            pe.wait_ge(c2_sb, 2)
            pe.wait_ge(tp_out, TP_X4 + NT)
            for u in range(2 * NG):
                g, r = u // 2, u % 2
                b = g // 2
                pe.wait_ge(sq_sb, 2 * g + 2)
                if u >= 4:
                    pe.wait_ge(d_max, u - 3)
                q0, n = (0, P) if r == 0 else (32 * b, SB_)
                cols = slice(0, P) if r == 0 else slice(P, S)
                accumulate(M[u % 4][q0:q0 + n, :],
                           [(ctx2[b][:, k, cols], XT[0][:, k, G * g:G * g + G]) for k in range(2)]
                           + [(ones[:, 0:n], XT[1][:, k, G * g:G * g + G]) for k in range(2)], d_mm)
            for b in range(B):
                pe.wait_ge(chased[b], S)
                pe.wait_ge(io_f, 3)
                for n, (i0, cnt_) in enumerate(((0, P), (P, SB_))):
                    q0 = 0 if n == 0 else 32 * b
                    for e in range(2):
                        last = nc.tensor.matmul(M[b][q0:q0 + cnt_, 2 * n + e:2 * n + e + 1], zrow[:, b, i0 + e:i0 + e + cnt_],
                                                ones[0:1, 0:1], start=True, stop=True)
                last.then_inc(z_mm, 1)
            for t in range(NT):
                b, c0 = t // TB, P * (t % TB)
                pe.wait_ge(p_ok, 2 * b + 2)
                if t >= 4:
                    pe.wait_ge(rs[5], t - 3)
                else:
                    pe.wait_ge(p_ok, 4)
                accumulate(M[t % 4][:, 0:D], [(Pm[:, b, c0:c0 + P], ctxA[b][:, :]), (Pm[:, 2 + b, c0:c0 + P], ctxBB[:, :])], pm[5])
            pe.wait_ge(ld_ip, 16)
            for r in range(NIN // P):
                turn_tile(TP_IP + r, ipraw[:, r, :])
            pe.wait_ge(ld_ow, 16)
            for r in range(NOUT // P // 2):
                turn(TP_OW + r, owraw[:, 2 * r, :], owraw[:, 2 * r + 1, :])
            turn_x(TP_X5, 5)
            pe.wait_ge(tp_out, TP_X5 + NT)
            for u in range(B * 16):
                b, q = u // 16, u % 16
                if u >= 2:
                    pe.wait_ge(a_gelu, u - 1)
                for h in range(2):
                    accumulate(M[2 * (u % 2) + h], [(ipT[:, k, P * q:P * q + P], XT[1][:, k, L * b + G * h:L * b + G * h + G]) for k in range(2)],
                               a_mm if h else None)
            pe.wait_ge(a_gelu, B * 16)

            def spread(base, n):
                for i in range(n):
                    pe.wait_ge(dg_ok, 4 * (base + i + 1))
                    if base + i >= 2:
                        pe.wait_ge(bc_out, base + i - 1)
                    for j in range(4):
                        last = nc.tensor.matmul(M[(base + i) % 2][:, P * j:P * j + P], ones[:, :], dg[:, (base + i) % 2, j, :], start=True, stop=True)
                    last.then_inc(bc_mm, 1)

            pe.wait_ge(ld_pv, 16)
            pe.wait_ge(ld_op, 16)
            for b in range(B):
                o = 14 * b
                spread(o, 4)
                spread(o + 4, 4)
                spread(o + 8, 2)
                pe.wait_ge(wt_ok, b + 1)
                nc.tensor.matmul(M[3][:, 0:NP_], ones[:, :], wt[:, :], start=True, stop=True)
                for r in range(NP_):
                    last = nc.tensor.matmul(M[4][:, 0:1], pv[:, r, :], wt[:, r:r + 1], start=r == 0, stop=r == NP_ - 1)
                last.then_inc(tot_mm, 1)
                pe.wait_ge(agg_ok, b + 1)
                for q in range(16):
                    last = nc.tensor.matmul(M[2][:, q:q + 1], owT[:, P * q:P * q + P], agg[:, :], start=True, stop=True)
                last.then_inc(oa_mm, 1)
                spread(o + 10, 4)
                pe.wait_ge(ko_ok, b + 1)
                for q in range(16):
                    a = kept[:, q:q + 1]
                    last = nc.tensor.matmul(M[5][:, 256 * b:256 * b + 256], bass.AP(tensor=a.tensor, offset=a.offset, ap=[a.ap[0], [0, P]]),
                                            op[:, q, :], start=q == 0, stop=q == 15)
                last.then_inc(f_mm, 1)

        @block.vector
        def _(dve):
            steps = [0]

            def tick(ins):
                ins.then_inc(dv, 1)
                steps[0] += 1

            def settle(but=0):
                dve.wait_ge(dv, steps[0] - but)

            V = nc.vector

            def moments(src, seen, g):
                for j in range(4):
                    tick(V.bn_stats(stat[:, j, :], src(j)))
                settle()
                for j in range(4):
                    tick(V.bn_aggr(mv[:, 4 * g + j, :], stat[:, j, :]))
                settle()
                V.tensor_scalar(ve[:, 4 * g:4 * g + 4], mv[:, 4 * g:4 * g + 4, 1], EPS, None, ALU.add).then_inc(seen, 1)

            def norm(n, g, summed):
                if g >= 2:
                    dve.wait_ge(xo[n], 4 * g - 4)
                elif g == 0 and n >= 2:
                    dve.wait_ge(xo[n - 1], NT)
                for j in range(4):
                    summed(4 * g + j, res[:, g % 2, j, :]).then_inc(rs[n], 1)
                dve.wait_ge(rs[n], 4 * g + 4)
                moments(lambda j: res[:, g % 2, j, :], vr[n], g)

            def apply(n, g):
                dve.wait_ge(sd[n], g + 1)
                for j in range(4):
                    t = 4 * g + j
                    V.tensor_scalar(X[:, t, :], res[:, g % 2, j, :], mv[:, t, 0:1], rstd[:, t:t + 1],
                                    ALU.subtract, ALU.mult).then_inc(xo[n], 1)

            def plus_x(n):
                def summed(t, dst):
                    dve.wait_ge(pm[n], t + 1)
                    return V.tensor_tensor(dst, M[t % 4][:, 0:D], X[:, t, :], ALU.add)
                return summed

            dve.wait_ge(consts, 9)
            tick(V.tensor_scalar(pbit[:, :], pidx[:, :], 4, 1, ALU.logical_shift_right, ALU.bitwise_and))
            settle()
            tick(V.tensor_copy(parm[:, 1:2], pbit[:, :]))
            settle()
            tick(V.tensor_scalar(parm[:, 0:1], parm[:, 1:2], -1.0, 1.0, ALU.mult, ALU.add))
            settle()
            for m in range(2):
                dve.wait_ge(k_mm, 2)
                src = M[2][:, 256 * m:256 * m + 256].rearrange("p (g k) -> p g k", g=NG)
                for h in range(2):
                    V.tensor_scalar(kbd[:, m, :, h, :], src, parm[:, h:h + 1], None, ALU.mult).then_inc(k_sb, 1)
            for g in range(NG):
                dve.wait_ge(v_mm, 2 * (g // 2) + 2)
                src = M[3 + g // 2][:, 256 * (g % 2):256 * (g % 2) + 256].rearrange("p (a h d) -> p a h d", a=NPAIR, h=2)
                for h in range(2):
                    V.tensor_copy(vbd[64 * h:64 * h + 64, g, :, h, :], src[64 * h:64 * h + 64, :, h, :]).then_inc(v_sb, 1)
            for u in range(8):
                dve.wait_ge(q_mm, u + 1)
                V.tensor_copy(qT[:, u % 2, G * (u // 2):G * (u // 2) + G], M[u % 2]).then_inc(q_sb, 1)
            for q in range(9):
                if q < 8:
                    for j in range(4):
                        u = 4 * q + j
                        dve.wait_ge(s_mm, u + 1)
                        tick(V.tensor_reduce(cmax[:, u, :], M[j].rearrange("p (n b) -> p n b", b=BLK), AX.X, ALU.max))
                    settle()
                    for j in range(4):
                        u = 4 * q + j
                        if u >= 4:
                            dve.wait_ge(w_exp, u - 3)
                        cm = cmax[:, u, :]
                        V.tensor_tensor(Sm[:, j, :].rearrange("p (n b) -> p n b", b=BLK), M[j].rearrange("p (n b) -> p n b", b=BLK),
                                        bass.AP(tensor=cm.tensor, offset=cm.offset, ap=[cm.ap[0], cm.ap[1], [0, BLK]]),
                                        ALU.subtract).then_inc(s_sub, 1)
                if q >= 1:
                    g, m = (q - 1) // 2, (q - 1) % 2
                    dve.wait_ge(nd_mm, q)
                    tick(V.tensor_scalar(den[:, :], M[5], 1e-10, None, ALU.add))
                    settle()
                    tick(V.reciprocal(rden[:, :], den[:, :]))
                    settle()
                    V.tensor_tensor(oT[:, m, G * g:G * g + G], M[4], rden[:, :], ALU.mult).then_inc(o_sb, 1)
            for g in range(NG):
                norm(1, g, plus_x(1))
                if g:
                    apply(1, g - 1)
            apply(1, NG - 1)
            for t in range(NT):
                dve.wait_ge(l_mm, t + 1)
                tick(V.tensor_reduce(mx[:, t:t + 1], M[4 + t % 2][:, 0:S], AX.X, ALU.max))
                settle()
                V.tensor_scalar(nmx[:, t:t + 1], mx[:, t:t + 1], -float(D) ** -0.5, None, ALU.mult).then_inc(l_mx, 1)
                if t % 4 == 3 and t >= 7:
                    g = t // 4 - 1

                    def summed(s, dst):
                        dve.wait_ge(pm[2], s + 1)
                        tick(V.reciprocal(rsum[:, s:s + 1], ssum[:, s:s + 1]))
                        settle()
                        return V.scalar_tensor_tensor(out=dst, in0=M[s % 4][:, 0:D], scalar=rsum[:, s:s + 1], in1=X[:, s, :], op0=ALU.mult, op1=ALU.add)
                    norm(2, g, summed)
                    if g:
                        apply(2, g - 1)
            norm(2, NG - 1, summed)
            apply(2, NG - 2)
            apply(2, NG - 1)
            dve.wait_ge(ld_vec, 64)
            tick(V.tensor_scalar(omm[:, :, :], mus[:, :, :], -1.0, 1.0, ALU.mult, ALU.add))
            settle()
            tick(V.memset(mtmp[:, :, 0:1], 0.0))
            for n in range(2):
                for b in range(B):
                    dve.wait_ge(tp_out, TP_X2 + TB * b + TB)
                    c0 = L * b
                    if n or b:
                        dve.wait_ge(mix_sb, 4 * n + 2 * b)
                    for k in range(2):
                        tick(V.tensor_scalar(mtmp[:, k, 1:L], XT[0][:, k, c0:c0 + L - 1], omm[:, k, n:n + 1], None, ALU.mult))
                    settle()
                    for k in range(2):
                        dst = (mixT if n == 0 else XT[0])[:, k, c0:c0 + L]
                        V.scalar_tensor_tensor(out=dst, in0=XT[0][:, k, c0:c0 + L], scalar=mus[:, k, n:n + 1], in1=mtmp[:, k, :],
                                               op0=ALU.mult, op1=ALU.add).then_inc(mix_sb, 1)
            for u in range(8):
                g, m = u // 2, u % 2
                dve.wait_ge(kk_rel, u + 1)
                V.tensor_tensor(XT[1][:, m, G * g:G * g + G], krel[:, u % 2, :], krel[:, u % 2, :], ALU.mult).then_inc(kk_sb, 1)

            def gated(t, dst):
                dve.wait_ge(pm[3], t + 1)
                tick(V.tensor_tensor(dst, M[t % 4][:, 0:D], rgate[:, t, :], ALU.mult))
                settle()
                return V.tensor_tensor(dst, dst, X[:, t, :], ALU.add)
            dve.wait_ge(r_sb, NT)
            for g in range(NG):
                norm(3, g, gated)
                if g:
                    apply(3, g - 1)
            apply(3, NG - 1)
            for c in range(2):
                for b in range(B):
                    dve.wait_ge(vv_sb, NG * c + 2 * b + 2)
                    V.tensor_copy(Vh[:, c, b, 0:HALO], Vh[:, c, b, L:L + HALO]).then_inc(halo, 1)
                    V.tensor_copy(Vh[:, c, b, HALO + L:], Vh[:, c, b, HALO:2 * HALO]).then_inc(halo, 1)
            dve.wait_ge(halo, 8)

            def mixed_norm(g):
                dve.wait_ge(at_mm, 4 * g + 4)

                def at(j):
                    return M[4 + j // 2][:, 256 * (j % 2):256 * (j % 2) + 256]
                moments(at, iv, g)
                dve.wait_ge(isd, g + 1)
                for j in range(4):
                    t = 4 * g + j
                    V.tensor_scalar(y2[:, j, :], at(j), mv[:, t, 0:1], rstd[:, t:t + 1], ALU.subtract, ALU.mult).then_inc(at_rd, 1)
                dve.wait_ge(at_rd, 4 * g + 4)
                for j in range(4):
                    tick(V.tensor_tensor(y2[:, j, :], y2[:, j, :], gam[:, :], ALU.mult))
                settle()
                for j in range(4):
                    tick(V.tensor_tensor(y2[:, j, :], y2[:, j, :], bet[:, :], ALU.add))
                settle()
                norm(4, g, lambda t, dst: V.tensor_tensor(dst, y2[:, t % 4, :], X[:, t, :], ALU.add))
                apply(4, g)

            pend = None
            for g in range(NG):
                b, h = g // 2, g % 2
                for c in range(2):
                    for n in range(NSH):
                        u = (2 * g + c) * NSH + n
                        dve.wait_ge(g_sig, u + 1)
                        v0 = HALO + SHIFTS[n] + G * h
                        dst = acc[:, g % 2, c, :] if n == 0 else pr[:, u % 4, :]
                        V.tensor_tensor(dst, gs[:, u % 4, :], Vh[:, c, b, v0:v0 + G], ALU.mult).then_inc(g_mul, 1)
                        if n >= 2:
                            dve.wait_ge(g_mul, u)
                            settle()
                            tick(V.tensor_tensor(acc[:, g % 2, c, :], acc[:, g % 2, c, :], pr[:, (u - 1) % 4, :], ALU.add))
                    dve.wait_ge(g_mul, u + 1)
                    settle()
                    V.tensor_tensor(acc[:, g % 2, c, :], acc[:, g % 2, c, :], pr[:, u % 4, :], ALU.add).then_inc(acc_sb, 1)
                    if c == 0 and g >= 1:
                        mixed_norm(g - 1)
            mixed_norm(NG - 1)
            for b in range(B):
                tick(V.tensor_scalar(ctx2[b][:, :, :], ctxT[b][:, :, :], -2.0, None, ALU.mult))
                settle()
            for b in range(B):
                tick(V.scalar_tensor_tensor(out=adump[:, :], in0=ctxA[b][:, :], scalar=1.0, in1=ctxA[b][:, :], op0=ALU.mult, op1=ALU.mult,
                                            accum_out=aa[:, b:b + 1]))
                settle()
            tick(V.scalar_tensor_tensor(out=adump[:, :], in0=ctxBB[:, :], scalar=1.0, in1=ctxBB[:, :], op0=ALU.mult, op1=ALU.mult,
                                        accum_out=aa[:, 2:3]))
            settle()
            V.memset(Mw[:, :, :], 0.0).then_inc(c2_sb, 2)
            for u in range(2 * NG):
                g, r = u // 2, u % 2
                b, h = g // 2, g % 2
                q0, n = (0, P) if r == 0 else (32 * b, SB_)
                k = b if r == 0 else 2
                dve.wait_ge(d_mm, u + 1)
                V.tensor_scalar(Drow[q0:q0 + n, k, G * h:G * h + G], M[u % 4][q0:q0 + n, :], aa[q0:q0 + n, k:k + 1], 0.0,
                                ALU.add, ALU.max).then_inc(d_max, 1)
            V.memset(Rw[:, 0:3, :], BIG).then_inc(w_init, 1)
            dve.wait_ge(w_init, 1)
            dve.wait_ge(dw_ld, 32)
            lanes = [0] + list(range(31))
            for t in range(T):
                cur, prev, nxt2 = (t + 1) % RING, t % RING, (t + 3) % RING
                if t >= 1:
                    dve.wait_ge(w_row, t)
                V.tensor_tensor(Mw[:, t % 2, :], Rw[:, prev, 0:W], Rw[:, prev, 1:W + 1], ALU.min).then_inc(w_min, 1)
                if t >= 1:
                    if t + 1 >= RING:
                        stored(dve, t + 1 - RING)
                    V.stream_shuffle(Rw[:, (t + 2) % RING, 0:1], Rw[:, prev, W:W + 1], lanes).then_inc(w_edge, 1)
                dve.wait_ge(w_min, t + 1)
                if t >= 2:
                    dve.wait_ge(w_edge, t - 1)
                if t >= RING:
                    stored(dve, t - RING)
                V.tensor_tensor_scan(Rw[:, cur, 1:W + 1], Mw[:, t % 2, :], Dw[:, t, :], Rw[:, cur, 0:1] if t else 0.0,
                                     ALU.min, ALU.add).then_inc(w_row, 1)
            dve.wait_ge(pad_ok, 7)
            dve.wait_ge(io_f, 5)
            dve.wait_ge(w_row, T)
            for n, k in enumerate((2, 0, 1)):
                dve.wait_ge(*((rrB_ld, 64) if k == 2 else (rrA_ld, 64)))
                tick(V.tensor_tensor(tmpa[:, :], Rp[:, k, 0:L], Rp[:, k, 1:L + 1], ALU.min))
                tick(V.tensor_tensor(tmpb[:, :], Rp[:, k, 0:L], Rp[:, k, 1:L + 1], ALU.is_le))
                settle()
                tick(V.tensor_tensor(tmpa[:, :], Rc[:, k, 0:L], tmpa[:, :], ALU.is_ge))
                tick(V.tensor_tensor(tmpb[:, :], iota2[:, :], tmpb[:, :], ALU.subtract))
                settle()
                tick(V.tensor_tensor(tmpa[:, :], tmpa[:, :], tmpb[:, :], ALU.mult))
                settle()
                if n:
                    dve.wait_ge(z_ok, n)
                tick(V.tensor_tensor_scan(Zf[:, :], tmpa[:, :], tmpa[:, :], 0.0, ALU.max, ALU.max))
                settle()
                V.tensor_copy(Zi[:, k, :], Zf[:, :]).then_inc(z_ok, 1)
            for b in range(B):
                dve.wait_ge(z_mm, b + 1)
                tick(V.tensor_copy(zcol[:, b, :], M[b][:, 0:2]))
                tick(V.tensor_copy(zcol[32 * b:32 * b + SB_, 2 + b, :], M[b][32 * b:32 * b + SB_, 2:4]))
                settle()
                for k in (b, 2 + b):
                    if b or k > 1:
                        dve.wait_ge(p_ok, 2 * b + (1 if k > 1 else 0))
                    tick(V.tensor_scalar(tmpa[:, :], iota2[:, :], zcol[:, k, 0:1], None, ALU.is_ge))
                    settle()
                    V.scalar_tensor_tensor(out=Pm[:, k, :], in0=iota2[:, :], scalar=zcol[:, k, 1:2], in1=tmpa[:, :],
                                           op0=ALU.is_le, op1=ALU.mult).then_inc(p_ok, 1)
            for g in range(NG):
                norm(5, g, plus_x(5))
                if g:
                    apply(5, g - 1)
            apply(5, NG - 1)
            dve.wait_ge(c_ok, 4)
            dve.wait_ge(a_gelu, B * 16)

            def spread_diag(base, vals, n):
                for i in range(n):
                    if base + i >= 2:
                        dve.wait_ge(bc_mm, base + i - 1)
                    for j in range(4):
                        V.tensor_scalar(dg[:, (base + i) % 2, j, :], ident[:, :], vals[:, 4 * i + j:4 * i + j + 1], None, ALU.mult).then_inc(dg_ok, 1)

            def choose(vals, Q, K, base):
                spread_diag(base, vals, Q // 4)
                tick(V.memset(cnt[:, :, :], 0.0))
                settle()
                dve.wait_ge(bc_out, base + Q // 4)
                for q in range(Q):
                    v, c0, c1 = vals[:, q:q + 1], P * q, P * q + P
                    settle(4 if q else 0)
                    if q:
                        tick(V.tensor_scalar(cdump[:, q % 2, 0:c0], row[:, 0:c0], v, 0.0, ALU.is_ge, ALU.add, accum_out=cnt[:, 0, q:q + 1]))
                    if q < Q - 1:
                        tick(V.tensor_scalar(cdump[:, q % 2, c1:P * Q], row[:, c1:P * Q], v, 0.0, ALU.is_gt, ALU.add, accum_out=cnt[:, 1, q:q + 1]))
                    tick(V.scalar_tensor_tensor(out=ddump[:, q % 2, 0, :], in0=row[:, c0:c1], scalar=v, in1=lt[:, :], op0=ALU.is_ge, op1=ALU.mult, accum_out=cnt[:, 2, q:q + 1]))
                    tick(V.scalar_tensor_tensor(out=ddump[:, q % 2, 1, :], in0=row[:, c0:c1], scalar=v, in1=gt[:, :], op0=ALU.is_gt, op1=ALU.mult, accum_out=cnt[:, 3, q:q + 1]))
                settle()
                tick(V.tensor_tensor(rank[:, 0, 0:Q], cnt[:, 0, 0:Q], cnt[:, 1, 0:Q], ALU.add))
                tick(V.tensor_tensor(rank[:, 1, 0:Q], cnt[:, 2, 0:Q], cnt[:, 3, 0:Q], ALU.add))
                settle()
                tick(V.tensor_tensor(rank[:, 0, 0:Q], rank[:, 0, 0:Q], rank[:, 1, 0:Q], ALU.add))
                settle()
                tick(V.tensor_scalar(msk[:, 0:Q], rank[:, 0, 0:Q], float(K), None, ALU.is_lt))
                settle()

            for b in range(B):
                o = 14 * b
                tick(V.tensor_scalar(mact[:, :], acts[:, b, :], 1.0 / L, None, ALU.mult))
                settle()
                choose(mact, 16, KIN, o)
                tick(V.tensor_tensor(kept[:, :], mact[:, :], msk[:, :], ALU.mult))
                settle()
                V.memset(sc[:, 7:8], 0.0).then_inc(k_free, 1)
                spread_diag(o + 4, kept, 4)
                dve.wait_ge(bc_out, o + 8)
                for r in range(NP_):
                    n = NP_ * b + r
                    dve.wait_ge(ld_pw[n % 3], 16 * (n // 3 + 1))
                    if n >= 2:
                        dve.wait_ge(pw_used, n - 1)
                    V.scalar_tensor_tensor(out=cdump[:, r % 2, :], in0=pwt[:, n % 3, :], scalar=1.0, in1=row[:, :], op0=ALU.mult, op1=ALU.mult,
                                           accum_out=pacc[:, r:r + 1]).then_inc(pw_used, 1)
                dve.wait_ge(pw_used, NP_ * (b + 1))
                V.memset(sc[:, 7:8], 0.0).then_inc(p_pre, 1)
                V.memset(sc[:, 6:7], 0.0).then_inc(k_free, 1)
                dve.wait_ge(p_act, b + 1)
                choose(pact, NP_, KPROC, o + 8)
                tick(V.tensor_reduce(sc[:, 0:1], row[:, 0:NPROC], AX.X, ALU.max))
                settle()
                V.tensor_scalar(sc[:, 1:2], sc[:, 0:1], -1.0, None, ALU.mult).then_inc(e_arg, 1)
                dve.wait_ge(e_ok, b + 1)
                V.tensor_tensor(wt[:, :], pex[:, :], msk[:, 0:NP_], ALU.mult).then_inc(wt_ok, 1)
                dve.wait_ge(tot_mm, b + 1)
                tick(V.tensor_reduce(sc[:, 2:3], M[3][:, 0:NP_], AX.X, ALU.add))
                settle()
                tick(V.reciprocal(sc[:, 3:4], sc[:, 2:3]))
                settle()
                V.tensor_scalar(agg[:, :], M[4][:, 0:1], sc[:, 3:4], None, ALU.mult).then_inc(agg_ok, 1)
                V.memset(sc[:, 5:6], 0.0).then_inc(k_free, 1)
                dve.wait_ge(oa_act, b + 1)
                choose(oact, 16, KOUT, o + 10)
                V.tensor_tensor(kept[:, :], oact[:, :], msk[:, :], ALU.mult).then_inc(ko_ok, 1)
                V.memset(sc[:, 4:5], 0.0).then_inc(k_free, 1)
                dve.wait_ge(f_mm, b + 1)

                def patterned(t, dst):
                    return V.tensor_tensor(dst, M[5][:, 256 * b:256 * b + 256], X[:, t, :], ALU.add)
                for g in (2 * b, 2 * b + 1):
                    norm(6, g, patterned)
                    apply(6, g)

        block_stack.close()


_INS = ["x", "ctx_1024", "L0_attn_Wqkv", "L0_attn_Wout", "L0_ffn_W_r", "L0_ffn_W_k", "L0_ffn_W_v", "L0_ffn_mu_r",
        "L0_ffn_mu_k", "L1_attn_gate_W", "L1_attn_value_W", "L1_attn_gamma", "L1_attn_beta", "L1_ffn_input_patterns",
        "L1_ffn_process_input_weights", "L1_ffn_process_values", "L1_ffn_output_input_weights", "L1_ffn_output_patterns"]


def build(nc, arrays_of):
    args = [nc.dram_tensor(f"in_{n}", a.shape, F32, kind="ExternalInput").ap() for n, a in arrays_of.items()]
    out = nc.dram_tensor("out_0", arrays_of["x"].shape, F32, kind="ExternalOutput").ap()
    T = arrays_of["ctx_1024"].shape[1] + 2 * (arrays_of["x"].shape[1] // 64 - 1)
    C = arrays_of["x"].shape[1] // 64
    wave = [nc.dram_tensor(n, (2 * C, T, 64), F32, kind="Internal").ap() for n in ("wave_d", "wave_r")]
    decoder(nc, *args, out, *wave)


def kernel(**inputs):
    import numpy as np
    from concourse import bacc
    from concourse.bass_utils import run_bass_kernel_spmd

    nc = bacc.Bacc("TRN2", target_bir_lowering=False, num_devices=1)
    arrays = {n: np.ascontiguousarray(inputs[n]) for n in _INS}
    build(nc, arrays)
    r = run_bass_kernel_spmd(nc, [{f"in_{n}": a for n, a in arrays.items()}], core_ids=[0])
    return r.results[0]["out_0"]
```

```python
from contextlib import ExitStack

import concourse.bass as bass
from concourse import mybir

F32 = mybir.dt.float32
I32 = mybir.dt.int32
BF16 = mybir.dt.bfloat16
ALU = mybir.AluOpType
ACT = mybir.ActivationFunctionType
AX = mybir.AxisListType

P = 128
SHIFTS = (0, -32, -16, -4, -1, 1, 4, 16, 32)
HALO = 32
BIG = 1e30
EPS = 1e-5


def decoder(nc, x, ctx_in, w_qkv, w_out, w_r, w_k, w_v, mu_r, mu_k, gate_w, value_w, gamma, beta,
            in_pat, proc_w, proc_v, out_w, out_pat, out, wave_d, wave_r):
    B, L, D = x.shape
    TOK = B * L
    NT = TOK // P
    NG = 4
    G = TOK // NG
    TB = L // P
    S = ctx_in.shape[1]
    SB_ = S - P
    HEADS, HD, SEG, DIL, BLK = 16, 16, 512, 8, 64
    KEYS = SEG // DIL
    NPAIR = HEADS // 2
    NSH = len(SHIFTS)
    W = 64
    C = L // W
    SKEW = 2
    T = S + SKEW * (C - 1)
    NIN, NPROC, NOUT, DPV = in_pat.shape[0], proc_w.shape[0], out_w.shape[0], proc_v.shape[1]
    KIN, KPROC, KOUT = max(NIN // 8, 64), max(NPROC // 8, 32), max(NOUT // 8, 64)

    with ExitStack() as top:
        block_stack = ExitStack()

        def sb(stack, name, shape, dt=F32):
            return stack.enter_context(nc.sbuf_tensor(name, shape, dt))

        def sem(name):
            return top.enter_context(nc.semaphore(name))

        X = sb(top, "X", [P, NT, D])
        XT = [sb(top, f"XT{i}", [P, 2, TOK]) for i in range(2)]
        ident = sb(top, "ident", [P, P])
        ones = sb(top, "ones", [P, P])
        nhalf = sb(top, "nhalf", [P, 4])
        bigt = sb(top, "bigt", [P, C * B * T * W // P // 8])
        res = sb(top, "res", [P, 2, 4, D])
        stat = sb(top, "stat", [P, 4, 6])
        mv = sb(top, "mv", [P, NT, 2])
        ve = sb(top, "ve", [P, NT])
        rstd = sb(top, "rstd", [P, NT])
        ctxA = [sb(top, f"ctxA{b}", [P, D]) for b in range(B)]
        ctxB = [sb(top, f"ctxB{b}", [P, D]) for b in range(B)]
        ctxBB = sb(top, "ctxBB", [P, D])
        ctxT = [sb(top, f"ctxT{b}", [P, 2, S]) for b in range(B)]

        a_mem = ExitStack()
        rawq = sb(a_mem, "rawq", [P, 6, D])
        raws = sb(a_mem, "raws", [P, 10, D])
        rawg = sb(a_mem, "rawg", [P, 2 * NSH, D])
        wqkvT = sb(a_mem, "wqkvT", [P, 2, 3 * D])
        wsT = sb(a_mem, "wsT", [P, 5, 2, D])
        gateT = sb(a_mem, "gateT", [P, 2, NSH * D])
        mus = sb(a_mem, "mus", [P, 2, 2])
        omm = sb(a_mem, "omm", [P, 2, 2])
        gam = sb(a_mem, "gam", [P, D])
        bet = sb(a_mem, "bet", [P, D])
        at_mem = ExitStack()
        qT = sb(at_mem, "qT", [P, 2, TOK])
        kbd = sb(at_mem, "kbd", [P, 2, NG, 2, KEYS])
        vbd = sb(at_mem, "vbd", [P, NG, NPAIR, 2, HD])
        halves = sb(at_mem, "halves", [P, 2, HD])
        pidx = sb(at_mem, "pidx", [P, 1], I32)
        pbit = sb(at_mem, "pbit", [P, 1], I32)
        parm = sb(at_mem, "parm", [P, 2])
        cmax = sb(at_mem, "cmax", [P, 32, SEG // BLK])
        Sm = sb(at_mem, "Sm", [P, 4, SEG])
        Wx = sb(at_mem, "Wx", [P, 8, SEG])
        den = sb(at_mem, "den", [P, SEG])
        rden = sb(at_mem, "rden", [P, SEG])
        oT = sb(at_mem, "oT", [P, 2, TOK])
        at_mem.close()
        ff_mem = ExitStack()
        Et = sb(ff_mem, "Et", [P, 4, S])
        WT2 = sb(ff_mem, "WT2", [P, 4, 2, P])
        mx = sb(ff_mem, "mx", [P, NT])
        nmx = sb(ff_mem, "nmx", [P, NT])
        ssum = sb(ff_mem, "ssum", [P, NT])
        rsum = sb(ff_mem, "rsum", [P, NT])
        mixT = sb(ff_mem, "mixT", [P, 2, TOK])
        mtmp = sb(ff_mem, "mtmp", [P, 2, L])
        rgate = sb(ff_mem, "rgate", [P, NT, D])
        krel = sb(ff_mem, "krel", [P, 2, G])
        ff_mem.close()
        mix_mem = ExitStack()
        VW = L + 2 * HALO
        Vh = sb(mix_mem, "Vh", [P, 2, B, VW])
        gs = sb(mix_mem, "gs", [P, 4, G])
        pr = sb(mix_mem, "pr", [P, 4, G])
        acc = sb(mix_mem, "acc", [P, 2, 2, G])
        y2 = sb(mix_mem, "y2", [P, 4, D])
        mix_mem.close()
        a_mem.close()

        b_mem = ExitStack()
        aa = sb(b_mem, "aa", [P, 3])
        adump = sb(b_mem, "adump", [P, D])
        Rc = sb(b_mem, "Rc", [P, 3, L + 1])
        Rp = sb(b_mem, "Rp", [P, 3, L + 1])
        iota2 = sb(b_mem, "iota2", [P, L])
        iotaf = sb(b_mem, "iotaf", [1, 2 * L])
        Zi = sb(b_mem, "Zi", [P, 3, L], I32)
        zrow = sb(b_mem, "zrow", [1, B, S + 1])
        zcol = sb(b_mem, "zcol", [P, 4, 2])
        w_mem = ExitStack()
        ctx2 = [sb(w_mem, f"ctx2{b}", [P, 2, S]) for b in range(B)]
        Drow = sb(w_mem, "Drow", [P, 3, L])
        Dw = sb(w_mem, "Dw", [64, T, W])
        RING = 64
        Rw = sb(w_mem, "Rw", [64, RING, W + 1])
        Mw = sb(w_mem, "Mw", [64, 2, W])
        w_mem.close()
        p_mem = ExitStack()
        tmpa = sb(p_mem, "tmpa", [P, L])
        tmpb = sb(p_mem, "tmpb", [P, L])
        Zf = sb(p_mem, "Zf", [P, L])
        Pm = sb(p_mem, "Pm", [P, 4, L])
        owT = sb(p_mem, "owT", [P, NOUT])
        pv = sb(p_mem, "pv", [P, NPROC // P, DPV])
        op = sb(p_mem, "op", [P, NOUT // P, D])
        pwt = sb(p_mem, "pwt", [P, 3, NIN])
        p_mem.close()
        b_mem.close()
        ipraw = XT[1][:, :, :].rearrange("p k t -> p (k t)").rearrange("p (r c) -> p r c", c=D)
        ipT = XT[0]
        owraw = res[:, :, :, :].rearrange("p a j c -> p (a j c)").rearrange("p (r c) -> p r c", c=DPV)
        c_mem = ExitStack()
        acts = sb(c_mem, "acts", [P, B, 16, 2])
        mact = sb(c_mem, "mact", [P, B, 16])
        before = sb(c_mem, "before", [P, P])
        after = sb(c_mem, "after", [P, P])
        ones_h = sb(c_mem, "ones_h", [P, P], BF16)
        row = sb(c_mem, "row", [P, B, NIN])
        row2 = sb(c_mem, "row2", [P, NPROC])
        krow = sb(c_mem, "krow", [P, NIN])
        CR = 4
        less = sb(c_mem, "less", [P, CR, NIN], BF16)
        tied = sb(c_mem, "tied", [P, CR, P], BF16)
        cdump = sb(c_mem, "cdump", [P, 2, NIN], BF16)
        cnt = sb(c_mem, "cnt", [P, 3, NPROC // P])
        msk = sb(c_mem, "msk", [P, NPROC // P])
        wt = sb(c_mem, "wt", [P, 8])
        pacc = sb(c_mem, "pacc", [P, 8])
        pact = sb(c_mem, "pact", [P, 8])
        pex = sb(c_mem, "pex", [P, 8])
        sc = sb(c_mem, "sc", [P, 4])
        agg = sb(c_mem, "agg", [P, 1])
        oact = sb(c_mem, "oact", [P, B, 16])
        kept = sb(c_mem, "kept", [P, 16])
        c_mem.close()

        PS = top.enter_context(nc.psum_tensor("PS", [P, 8, 512], F32))
        TP = [PS[:, i, :] for i in range(2)]
        M = [PS[:, 2 + i, :] for i in range(6)]

        ld_wq, ld_ws, ld_wg, ld_ctx, ld_vec = (sem(n) for n in ("ld_wq", "ld_ws", "ld_wg", "ld_ctx", "ld_vec"))
        ld_x = [sem(f"ld_x{g}") for g in range(NG)]
        consts = sem("consts")
        tp_done, tp_out = sem("tp_done"), sem("tp_out")
        dv = sem("dv")
        q_mm, q_sb, k_mm, k_sb, v_mm, v_sb = (sem(n) for n in ("q_mm", "q_sb", "k_mm", "k_sb", "v_mm", "v_sb"))
        s_mm, s_sub, w_exp, nd_mm, o_sb = (sem(n) for n in ("s_mm", "s_sub", "w_exp", "nd_mm", "o_sb"))
        par_ok = sem("par_ok")
        NL = range(1, 7)
        pm = [None] + [sem(f"pm{n}") for n in NL]
        rs = [None] + [sem(f"rs{n}") for n in NL]
        vr = [None] + [sem(f"vr{n}") for n in NL]
        sd = [None] + [sem(f"sd{n}") for n in NL]
        xo = [None] + [sem(f"xo{n}") for n in NL]
        iv, isd = sem("iv"), sem("isd")
        l_mm, l_mx, l_exp = sem("l_mm"), sem("l_mx"), sem("l_exp")
        mix_sb, r_mm, r_sb, kk_mm, kk_rel, kk_sb = (sem(n) for n in ("mix_sb", "r_mm", "r_sb", "kk_mm", "kk_rel", "kk_sb"))
        vv_mm, vv_sb, halo, g_mm, g_sig, g_mul, acc_sb, at_mm, at_rd = (
            sem(n) for n in ("vv_mm", "vv_sb", "halo", "g_mm", "g_sig", "g_mul", "acc_sb", "at_mm", "at_rd"))
        wt_half, k_free, c_zero, big_ok = sem("wt_half"), sem("k_free"), sem("c_zero"), sem("big_ok")
        a_ok, sq_sb, c2_sb, d_mm, d_max, d_rt, dw_fill, big_st, dw_st, dw_ld = (
            sem(n) for n in ("a_ok", "sq_sb", "c2_sb", "d_mm", "d_max", "d_rt", "dw_fill", "big_st", "dw_st", "dw_ld"))
        w_init, w_min, w_row, w_edge = (sem(n) for n in ("w_init", "w_min", "w_row", "w_edge"))
        rw_st = [sem(f"rw_st{i}") for i in range(-(-T // 16))]
        rrA_ld, rrB_ld, pad_ok, z_ok, io_f, z_mm, p_ok = (
            sem(n) for n in ("rrA_ld", "rrB_ld", "pad_ok", "z_ok", "io_f", "z_mm", "p_ok"))
        chased = [sem(f"chased{b}") for b in range(B)]
        ld_ip, ld_ow, ld_pv, ld_op = sem("ld_ip"), sem("ld_ow"), sem("ld_pv"), sem("ld_op")
        ld_pw = [sem(f"ld_pw{i}") for i in range(3)]
        pw_used = sem("pw_used")
        ow_t, ow_sb, a_mm, a_gelu, m_ok, bc_mm, bc_out, row2_free, kept_ok = (
            sem(n) for n in ("ow_t", "ow_sb", "a_mm", "a_gelu", "m_ok", "bc_mm", "bc_out", "row2_free", "kept_ok"))
        cmp_ok, rank_mm, p_pre, p_act, c_ok, e_arg, e_ok, wt_ok, tot_mm, agg_ok, oa_mm, oa_act, kc_mm, ko_ok, f_mm = (
            sem(n) for n in ("cmp_ok", "rank_mm", "p_pre", "p_act", "c_ok", "e_arg", "e_ok", "wt_ok", "tot_mm", "agg_ok",
                             "oa_mm", "oa_act", "kc_mm", "ko_ok", "f_mm"))
        out_st = sem("out_st")

        TP_WQ, TP_X0, TP_CTX, TP_WS, TP_WG = 0, 6, 22, 26, 36
        TP_X1 = TP_WG + 2 * NSH
        TP_E = TP_X1 + NT
        TP_X2 = TP_E + NT
        TP_X3 = TP_X2 + NT
        TP_X4 = TP_X3 + NT
        TP_IP = TP_X4 + NT
        TP_X5 = TP_IP + NIN // P

        SIDE = [range(0, 4), range(4, 9), range(9, 14), range(14, 19), range(19, 24), range(24, 28), range(28, 32), range(0)]
        NP_ = NPROC // P

        NQ = NIN // P
        assert NOUT == NIN

        def items(g):
            return [("new", 4 * g + j) for j in range(4)] + [("old", h) for h in range(g)]
        ITEMS = [(g, it) for g in range(4) for it in items(g)]
        OPS = [4 if kind == "old" else 2 if q % 4 == 3 else 3 for _, (kind, q) in ITEMS]
        ROWS = ([("in", 0, g) for g in range(4)] + [("in", 1, g) for g in range(3)] + [("proc", 0, g) for g in range(2)]
                + [("in", 1, 3)] + [("out", 0, g) for g in range(4)] + [("proc", 1, g) for g in range(2)]
                + [("out", 1, g) for g in range(4)])
        BEHIND = {u: [] for u in range(B * NQ)}
        BEHIND[0] += [("turn", t) for t in range(TB, TB + 4)]
        BEHIND[2] += [("turn", t) for t in range(TB + 4, NT)]
        for n, (b, g) in enumerate((b, g) for b in range(B) for g in range(4)):
            if 4 * n + 5 < B * NQ:
                BEHIND[4 * n + 5].append(("row", ("in", b, g)))
                todo = [("rank", b, i) for i, (g_, _) in enumerate(ITEMS) if g_ == g]
                for k in range(4):
                    part = todo[2 * k:2 * k + 2]
                    BEHIND.setdefault(4 * n + 6 + k, [])
                    BEHIND[4 * n + 6 + k] += part
        PROC_AT = 29
        STEP = 16
        STORES = {}
        for t0 in range(0, T, STEP):
            n = min(T, t0 + STEP) - t0
            STORES[t0] = 2 * B if (t0 + 1) % RING + n > RING else B

        def stored(eng, t):
            eng.wait_ge(rw_st[t // STEP], 16 * STORES[t // STEP * STEP])

        block = block_stack.enter_context(nc.Block())

        def rows(w):
            return w.rearrange("(r p) c -> p r c", p=P)

        @block.sync
        def _(sp):
            xt = x.rearrange("b l d -> (b l) d").rearrange("(t p) d -> p t d", p=P)
            ot = out.rearrange("b l d -> (b l) d").rearrange("(t p) d -> p t d", p=P)
            sp.dma_start(rawq[:, :, :], rows(w_qkv)).then_inc(ld_wq, 16)
            for g in range(NG):
                sp.dma_start(X[:, 4 * g:4 * g + 4, :], xt[:, 4 * g:4 * g + 4, :]).then_inc(ld_x[g], 16)
            sp.wait_ge(c_zero, 1)
            for b in range(B):
                sp.dma_start(ctxA[b][:, :], ctx_in[b, 0:P, :]).then_inc(ld_ctx, 16)
                sp.dma_start(ctxB[b][0:SB_, :], ctx_in[b, P:S, :]).then_inc(ld_ctx, 16)
                sp.dma_start(ctxBB[32 * b:32 * b + SB_, :], ctx_in[b, P:S, :]).then_inc(ld_ctx, 16)
            for n, w in enumerate((w_out, w_r, w_k, w_v, value_w)):
                sp.dma_start(raws[:, 2 * n:2 * n + 2, :], rows(w)).then_inc(ld_ws, 16)
            sp.dma_start(rawg[:, :, :], rows(gate_w)).then_inc(ld_wg, 16)
            with nc.allow_non_contiguous_dma(reason="two vectors of 256 values onto partitions"):
                for n, v in enumerate((mu_r, mu_k)):
                    sp.dma_start(mus[:, :, n:n + 1], v.rearrange("(k p) -> p k", p=P).unsqueeze(2)).then_inc(ld_vec, 16)
            for t_, v in ((gam, gamma), (bet, beta)):
                sp.dma_start(t_[:, :], bass.AP(tensor=v.tensor, offset=v.offset, ap=[[0, P], [1, D]])).then_inc(ld_vec, 16)
            sp.wait_ge(big_ok, 1)
            per = C * B * T * W // P
            sp.dma_start(bass.AP(tensor=wave_d.tensor, offset=wave_d.offset, ap=[[per, P], [per // 8, 8], [1, per // 8]]),
                         bass.AP(tensor=bigt[:, :].tensor, offset=bigt[:, :].offset, ap=[bigt[:, :].ap[0], [0, 8], [1, per // 8]])).then_inc(big_st, 16)

            def skewed(dram, b, i0, n):
                return bass.AP(tensor=dram.tensor, offset=dram.offset + b * C * T * W + i0 * W,
                               ap=[[W, n], [(T + SKEW) * W, C], [1, W]])

            def chunks(ap):
                return ap.rearrange("p (c w) -> p c w", w=W)

            sp.wait_ge(big_st, 16)
            for b in range(B):
                sp.wait_ge(d_rt, 4 * b + 3)
                sp.dma_start(skewed(wave_d, b, 0, P), chunks(Drow[:, b, :])).then_inc(dw_st, 16)
                sp.wait_ge(d_rt, 4 * b + 4)
                sp.dma_start(skewed(wave_d, b, P, SB_), chunks(Drow[32 * b:32 * b + SB_, 2, :])).then_inc(dw_st, 16)
            sp.wait_ge(dw_st, 64)
            sp.wait_ge(dw_fill, 1)
            for b in range(B):
                sp.dma_start(Dw[32 * b + 1:32 * b + 1 + C, :, :].rearrange("p t w -> p (t w)"),
                             wave_d[b * C:(b + 1) * C].rearrange("p t w -> p (t w)")).then_inc(dw_ld, 16)
            sp.wait_ge(d_mm, 2 * NG)
            sp.dma_start(ipraw, rows(in_pat)).then_inc(ld_ip, 16)
            sp.wait_ge(xo[4], NT)
            sp.dma_start(owraw, rows(out_w)).then_inc(ld_ow, 16)
            tA = P + SKEW * (C - 1)
            for t0 in list(range(0, T, STEP)):
                t1 = min(T, t0 + STEP)
                sp.wait_ge(w_row, t1)
                for b in range(B):
                    s0 = (t0 + 1) % RING
                    n0 = min(t1 - t0, RING - s0)
                    sp.dma_start(wave_r[b * C:(b + 1) * C, t0:t0 + n0, :],
                                 Rw[32 * b + 1:32 * b + 1 + C, s0:s0 + n0, 1:W + 1]).then_inc(rw_st[t0 // STEP], 16)
                    if n0 < t1 - t0:
                        sp.dma_start(wave_r[b * C:(b + 1) * C, t0 + n0:t1, :],
                                     Rw[32 * b + 1:32 * b + 1 + C, 0:t1 - t0 - n0, 1:W + 1]).then_inc(rw_st[t0 // STEP], 16)
                if t0 < tA <= t1:
                    for s0 in range(0, t1, STEP):
                        sp.wait_ge(rw_st[s0 // STEP], 16 * STORES[s0])
                    sp.wait_ge(pad_ok, 6)
                    for b in range(B):
                        sp.dma_start(chunks(Rc[:, b, 1:L + 1]), skewed(wave_r, b, 0, P)).then_inc(rrA_ld, 16)
                        sp.dma_start(chunks(Rp[1:P, b, 1:L + 1]), skewed(wave_r, b, 0, P - 1)).then_inc(rrA_ld, 16)
            for s0 in range(0, T, STEP):
                sp.wait_ge(rw_st[s0 // STEP], 16 * STORES[s0])
            for b in range(B):
                q0 = 32 * b
                sp.dma_start(chunks(Rc[q0:q0 + SB_, 2, 1:L + 1]), skewed(wave_r, b, P, SB_)).then_inc(rrB_ld, 16)
                sp.dma_start(chunks(Rp[q0:q0 + SB_, 2, 1:L + 1]), skewed(wave_r, b, P - 1, SB_)).then_inc(rrB_ld, 16)
            sp.dma_start(pv[:, :, :], rows(proc_v)).then_inc(ld_pv, 16)
            sp.dma_start(op[:, :, :], rows(out_pat)).then_inc(ld_op, 16)
            for n in range(B * NP_):
                if n >= 3:
                    sp.wait_ge(pw_used, n - 2)
                sp.dma_start(pwt[:, n % 3, :], rows(proc_w)[:, n % NP_, :]).then_inc(ld_pw[n % 3], 16)
            for g in range(NG):
                sp.wait_ge(xo[6], 4 * g + 4)
                sp.dma_start(ot[:, 4 * g:4 * g + 4, :], X[:, 4 * g:4 * g + 4, :]).then_inc(out_st, 16)
            sp.wait_ge(out_st, 16 * NG)

        def walk_back(eng, copy, b):
            at = L - 1
            for i in range(S - 1, -1, -1):
                if i == S - 1:
                    eng.wait_ge(z_ok, 1)
                if i == P - 1:
                    eng.wait_ge(z_ok, 2 + b)
                q = i if i < P else 32 * b + i - P
                z = eng.value_load(Zi[q:q + 1, b if i < P else 2, bass.ds(at, 1)], min_val=0, max_val=2 * (L - 1))
                copy(zrow[:, b, i:i + 1], iotaf[:, bass.ds(z, 1)]).then_inc(chased[b], 1)
                at = z // 2

        @block.gpsimd
        def _(pool):
            nc.gpsimd.memset(ctxBB[:, :], 0.0).then_inc(c_zero, 1)
            nc.gpsimd.memset(ident[:, :], 0.0).then_inc(consts, 1)
            nc.gpsimd.memset(ones[:, :], 1.0).then_inc(consts, 1)
            nc.gpsimd.memset(nhalf[:, :], -0.5).then_inc(consts, 1)
            nc.gpsimd.iota(pidx[:, :], pattern=[[0, 1]], base=0, channel_multiplier=1).then_inc(consts, 1)
            nc.gpsimd.memset(vbd[:, :, :, :, :], 0.0).then_inc(consts, 1)
            nc.gpsimd.memset(halves[:, :, :], 0.0).then_inc(consts, 1)
            pool.wait_ge(consts, 6)
            nc.gpsimd.affine_select(out=ident[:, :], in_=ident[:, :], compare_op=ALU.not_equal, fill=1.0, base=0,
                                    pattern=[[-1, P]], channel_multiplier=1).then_inc(consts, 1)
            for h in range(2):
                pool.wait_ge(consts, 7 + h)
                nc.gpsimd.memset(halves[64 * h:64 * h + 64, h, :], 1.0).then_inc(consts, 1)
            pool.wait_ge(consts, 9)
            nc.gpsimd.memset(bigt[:, :], BIG).then_inc(big_ok, 1)

            def inv_std(seen, made, g):
                pool.wait_ge(seen, g + 1)
                nc.gpsimd.tensor_tensor(rstd[:, 4 * g:4 * g + 4], ve[:, 4 * g:4 * g + 4], nhalf[:, :], ALU.pow).then_inc(made, 1)

            for n in (1, 2, 3):
                for g in range(NG):
                    inv_std(vr[n], sd[n], g)
            for g in range(NG):
                inv_std(iv, isd, g)
                inv_std(vr[4], sd[4], g)
            pool.wait_ge(xo[4], NT)
            nc.gpsimd.memset(Dw[:, :, :], BIG).then_inc(dw_fill, 1)
            nc.gpsimd.memset(Rc[:, :, 0:1], BIG).then_inc(pad_ok, 1)
            nc.gpsimd.memset(Rp[:, :, 0:1], BIG).then_inc(pad_ok, 1)
            nc.gpsimd.memset(Rp[0:1, 0, 1:L + 1], BIG).then_inc(pad_ok, 1)
            nc.gpsimd.memset(Rp[0:1, 1, 1:L + 1], BIG).then_inc(pad_ok, 1)
            nc.gpsimd.memset(Rc[:, 2, 1:L + 1], BIG).then_inc(pad_ok, 1)
            nc.gpsimd.memset(Rp[:, 2, 1:L + 1], BIG).then_inc(pad_ok, 1)
            nc.gpsimd.memset(zcol[:, :, :], BIG).then_inc(pad_ok, 1)
            nc.gpsimd.iota(Zi[:, 2, :], pattern=[[2, L]], base=0, channel_multiplier=0).then_inc(io_f, 1)
            nc.gpsimd.iota(Zi[0:1, 0:2, :], pattern=[[1, 2 * L]], base=0, channel_multiplier=0).then_inc(io_f, 1)
            nc.gpsimd.memset(zrow[:, :, S:S + 1], float(2 * (L - 1))).then_inc(io_f, 1)
            pool.wait_ge(io_f, 3)
            nc.gpsimd.tensor_copy(iota2[:, :], Zi[:, 2, :]).then_inc(io_f, 1)
            nc.gpsimd.tensor_copy(iotaf[:, :], Zi[0:1, 0:2, :].rearrange("p a b -> p (a b)")).then_inc(io_f, 1)
            pool.wait_ge(io_f, 5)
            walk_back(pool, nc.gpsimd.tensor_copy, 1)
            for g in range(NG):
                inv_std(vr[5], sd[5], g)
            pool.wait_ge(pm[5], NT)
            nc.gpsimd.memset(before[:, :], 1.0).then_inc(c_ok, 1)
            nc.gpsimd.memset(after[:, :], 1.0).then_inc(c_ok, 1)
            nc.gpsimd.memset(ones_h[:, :], 1.0).then_inc(c_ok, 1)
            pool.wait_ge(c_ok, 3)
            nc.gpsimd.affine_select(out=before[:, :], in_=before[:, :], compare_op=ALU.is_gt, fill=0.0, base=0,
                                    pattern=[[-1, P]], channel_multiplier=1).then_inc(c_ok, 1)
            nc.gpsimd.affine_select(out=after[:, :], in_=after[:, :], compare_op=ALU.is_gt, fill=0.0, base=0,
                                    pattern=[[1, P]], channel_multiplier=-1).then_inc(c_ok, 1)
            for g in range(NG):
                inv_std(vr[6], sd[6], g)

        @block.scalar
        def _(act):
            def pair(i):
                return TP[i % 2][:, 0:2 * P].rearrange("p (k c) -> p k c", k=2)

            def tp_copy(i, dst, n=P):
                act.wait_ge(tp_done, i + 1)
                nc.scalar.copy(dst, pair(i)[:, :, 0:n]).then_inc(tp_out, 1)

            def x_copy(first, buf, t):
                tp_copy(first + t, XT[buf][:, :, P * t:P * t + P])

            for r in range(6):
                tp_copy(TP_WQ + r, wqkvT[:, :, P * r:P * r + P])
            for t in range(NT):
                x_copy(TP_X0, 0, t)
            for u in range(32):
                act.wait_ge(s_sub, u + 1)
                if u >= 8:
                    act.wait_ge(nd_mm, u // 4 - 1)
                nc.scalar.activation(Wx[:, u % 8, :], Sm[:, u % 4, :], ACT.Exp, scale=float(HD) ** -0.5).then_inc(w_exp, 1)
                if u % 4 == 3:
                    for n in SIDE[u // 4]:
                        if n < 4:
                            tp_copy(TP_CTX + n, ctxT[n // 2][:, :, 0:P] if n % 2 == 0 else ctxT[n // 2][:, :, P:S], P if n % 2 == 0 else SB_)
                        elif n < 14:
                            tp_copy(TP_CTX + n, wsT[:, (n - 4) // 2, :, P * (n % 2):P * (n % 2) + P])
                        else:
                            tp_copy(TP_CTX + n, gateT[:, :, P * (n - 14):P * (n - 14) + P])
            for t in range(NT):
                x_copy(TP_X1, 1, t)
            for t in range(NT + 2):
                if t < NT:
                    act.wait_ge(l_mx, t + 1)
                    if t >= 4:
                        act.wait_ge(tp_done, TP_E + t - 3)
                    nc.scalar.activation(Et[:, t % 4, :], M[4 + t % 2][:, 0:S], ACT.Exp, scale=float(D) ** -0.5,
                                         bias=nmx[:, t:t + 1], accum_out=ssum[:, t:t + 1]).then_inc(l_exp, 1)
                if t >= 2:
                    s = t - 2
                    act.wait_ge(tp_done, TP_E + s + 1)
                    if s >= 4:
                        act.wait_ge(pm[2], s - 3)
                    src = pair(TP_E + s)
                    nc.scalar.copy(WT2[:, s % 4, 0, :], src[:, 0, :]).then_inc(wt_half, 1)
                    nc.scalar.copy(WT2[0:SB_, s % 4, 1, :], src[0:SB_, 1, :]).then_inc(tp_out, 1)
            for t in range(NT):
                x_copy(TP_X2, 0, t)
            for t in range(NT):
                act.wait_ge(r_mm, t + 1)
                nc.scalar.activation(rgate[:, t, :], M[t % 2][:, 0:D], ACT.Sigmoid).then_inc(r_sb, 1)
            for u in range(8):
                act.wait_ge(kk_mm, u + 1)
                if u >= 2:
                    act.wait_ge(kk_sb, u - 1)
                nc.scalar.activation(krel[:, u % 2, :], M[2 + u % 2], ACT.Relu).then_inc(kk_rel, 1)
            for t in range(NT):
                x_copy(TP_X3, 1, t)
            for u in range(8):
                c, g = u // NG, u % NG
                act.wait_ge(vv_mm, u + 1)
                c0 = HALO + (g % 2) * G
                nc.scalar.copy(Vh[:, c, g // 2, c0:c0 + G], M[u % 2]).then_inc(vv_sb, 1)
            for u in range(NG * 2 * NSH):
                act.wait_ge(g_mm, u + 1)
                if u >= 4:
                    act.wait_ge(g_mul, u - 3)
                nc.scalar.activation(gs[:, u % 4, :], M[u % 4], ACT.Sigmoid).then_inc(g_sig, 1)
            for t in range(NT):
                x_copy(TP_X4, 0, t)
                if t % 4 == 3:
                    g = t // 4
                    act.wait_ge(tp_out, TP_X4 + t + 1)
                    for k in range(2):
                        nc.scalar.activation(XT[1][:, k, G * g:G * g + G], XT[0][:, k, G * g:G * g + G], ACT.Square).then_inc(sq_sb, 1)
            for u in range(2 * NG):
                g, r = u // 2, u % 2
                b, h = g // 2, g % 2
                act.wait_ge(d_max, u + 1)
                q0, n = (0, P) if r == 0 else (32 * b, SB_)
                dst = Drow[q0:q0 + n, b if r == 0 else 2, G * h:G * h + G]
                nc.scalar.activation(dst, dst, ACT.Sqrt).then_inc(d_rt, 1)
            for r in range(NIN // P):
                tp_copy(TP_IP + r, ipT[:, :, P * r:P * r + P])
            act.wait_ge(io_f, 5)
            walk_back(act, nc.scalar.copy, 0)
            for t in range(TB):
                x_copy(TP_X5, 1, t)

            def row_copy(what):
                s = ROWS.index(what)
                kind, b, g = what
                act.wait_ge(bc_mm, s + 1)
                if kind == "out":
                    act.wait_ge(kept_ok, b + 1)
                if kind == "proc" and b:
                    act.wait_ge(row2_free, b)
                dst = row2[:, 512 * g:512 * g + 512] if kind == "proc" else row[:, b, 512 * g:512 * g + 512]
                nc.scalar.copy(dst, TP[0]).then_inc(bc_out, 1)

            def proc_gelu(b):
                act.wait_ge(p_pre, b + 1)
                nc.scalar.activation(pact[:, :], pacc[:, :], ACT.Gelu).then_inc(p_act, 1)

            def behind(job):
                if job[0] == "turn":
                    x_copy(TP_X5, 1, job[1])
                elif job[0] == "row":
                    row_copy(job[1])

            def proc_exp(b):
                act.wait_ge(e_arg, b + 1)
                nc.scalar.activation(pex[:, :], pact[:, :], ACT.Exp, bias=sc[:, 1:2]).then_inc(e_ok, 1)

            def out_gelu(b):
                act.wait_ge(oa_mm, b + 1)
                nc.scalar.activation(oact[:, b, :], TP[1][:, 16:16 + NQ], ACT.Gelu).then_inc(oa_act, 1)

            for u in range(B * NQ):
                b, q = u // NQ, u % NQ
                for h in range(2):
                    act.wait_ge(a_mm, 2 * u + h + 1)
                    nc.scalar.activation(M[h], M[h], ACT.Gelu, accum_out=acts[:, b, q, h:h + 1]).then_inc(a_gelu, 1)
                for job in BEHIND[u]:
                    behind(job)
                if u == PROC_AT:
                    proc_gelu(0)
                    for g in range(2):
                        row_copy(("proc", 0, g))
            row_copy(("in", 1, 3))
            proc_exp(0)
            out_gelu(0)
            for g in range(4):
                row_copy(("out", 0, g))
            proc_gelu(1)
            for g in range(2):
                row_copy(("proc", 1, g))
            proc_exp(1)
            out_gelu(1)
            for g in range(4):
                row_copy(("out", 1, g))

        @block.tensor
        def _(pe):
            def turn(i, lo, hi, n=P):
                if i >= 2:
                    pe.wait_ge(tp_out, i - 1)
                nc.tensor.transpose(TP[i % 2][0:lo.shape[1], 0:n], lo, ident[0:n, 0:n])
                nc.tensor.transpose(TP[i % 2][0:hi.shape[1], P:P + n], hi, ident[0:n, 0:n]).then_inc(tp_done, 1)

            def turn_tile(i, src, n=P):
                turn(i, src[:, 0:P], src[:, P:2 * P], n)

            def accumulate(dst, parts, sem_=None):
                for i, (a, b_) in enumerate(parts):
                    last = nc.tensor.matmul(dst, a, b_, start=i == 0, stop=i == len(parts) - 1)
                if sem_ is not None:
                    last.then_inc(sem_, 1)

            def side_jobs(q):
                for n in SIDE[q]:
                    i = TP_CTX + n
                    if n < 4:
                        pe.wait_ge(ld_ctx, 96)
                        if n % 2 == 0:
                            turn_tile(i, ctxA[n // 2][:, :])
                        else:
                            turn_tile(i, ctxB[n // 2][0:SB_, :], SB_)
                    elif n < 14:
                        pe.wait_ge(ld_ws, 80)
                        turn_tile(i, raws[:, n - 4, :])
                    else:
                        pe.wait_ge(ld_wg, 16)
                        turn_tile(i, rawg[:, n - 14, :])

            pe.wait_ge(consts, 9)
            pe.wait_ge(ld_wq, 16)
            for r in range(6):
                turn_tile(TP_WQ + r, rawq[:, r, :])
            for t in range(NT):
                if t % 4 == 0:
                    pe.wait_ge(ld_x[t // 4], 16)
                turn_tile(TP_X0 + t, X[:, t, :])
            pe.wait_ge(tp_out, TP_X0 + NT)
            for m in range(2):
                accumulate(M[2][:, 256 * m:256 * m + 256],
                           [(wqkvT[:, k, D + P * m:D + P * m + P], XT[0][:, k, ::DIL]) for k in range(2)], k_mm)
            for g in range(NG):
                keys = [XT[0][:, k, SEG * g:SEG * g + SEG:DIL] for k in range(2)]
                for h in range(2):
                    accumulate(M[3 + g // 2][64 * h:64 * h + 64, 256 * (g % 2):256 * (g % 2) + 256],
                               [(keys[k], wqkvT[:, k, 2 * D:3 * D]) for k in range(2)], v_mm if h else None)
            for u in range(8):
                g, m = u // 2, u % 2
                if u >= 2:
                    pe.wait_ge(q_sb, u - 1)
                accumulate(M[u % 2], [(wqkvT[:, k, P * m:P * m + P], XT[0][:, k, G * g:G * g + G]) for k in range(2)], q_mm)
            pe.wait_ge(q_sb, 8)
            pe.wait_ge(k_sb, 4)
            pe.wait_ge(v_sb, 8)
            for q in range(9):
                if q < 8:
                    g, m = q // 2, q % 2
                    for j in range(4):
                        if q >= 1:
                            pe.wait_ge(s_sub, 4 * (q - 1) + j + 1)
                        r = slice(32 * j, 32 * j + 32)
                        nc.tensor.matmul(M[j], kbd[r, m, g, :, :].rearrange("p h k -> p (h k)"),
                                         qT[r, m, G * g:G * g + G], start=True, stop=True).then_inc(s_mm, 1)
                if q >= 1:
                    g, m = (q - 1) // 2, (q - 1) % 2
                    if q >= 2:
                        pe.wait_ge(o_sb, q - 1)
                    for j in range(4):
                        u = 4 * (q - 1) + j
                        pe.wait_ge(w_exp, u + 1)
                        r = slice(32 * j, 32 * j + 32)
                        nc.tensor.matmul(M[4][r, :], vbd[:, g, 4 * m + j, :, :].rearrange("p h d -> p (h d)"),
                                         Wx[:, u % 8, :], start=True, stop=True)
                        last = nc.tensor.matmul(M[5][r, :], halves[:, :, :].rearrange("p h d -> p (h d)"),
                                                Wx[:, u % 8, :], start=True, stop=True)
                    last.then_inc(nd_mm, 1)
                    side_jobs(q - 1)
            for t in range(NT):
                pe.wait_ge(o_sb, 2 * (t // 4) + 2)
                pe.wait_ge(s_sub, 32)
                if t >= 4:
                    pe.wait_ge(rs[1], t - 3)
                accumulate(M[t % 4][:, 0:D], [(oT[:, k, P * t:P * t + P], wsT[:, 0, k, :]) for k in range(2)], pm[1])

            def turn_x(first, n):
                for t in range(NT):
                    pe.wait_ge(xo[n], t + 1)
                    turn_tile(first + t, X[:, t, :])

            turn_x(TP_X1, 1)
            for t in range(NT + 3):
                if t < NT:
                    pe.wait_ge(tp_out, TP_X1 + t + 1)
                    if t >= 2:
                        pe.wait_ge(l_exp, t - 1)
                    accumulate(M[4 + t % 2][:, 0:S], [(XT[1][:, k, P * t:P * t + P], ctxT[t // TB][:, k, :]) for k in range(2)], l_mm)
                if 1 <= t <= NT:
                    s = t - 1
                    i = TP_E + s
                    pe.wait_ge(l_exp, s + 1)
                    pe.wait_ge(tp_out, i - 1)
                    nc.tensor.transpose(TP[i % 2][:, 0:P], Et[:, s % 4, 0:P], ident[:, :])
                    nc.tensor.transpose(TP[i % 2][0:SB_, P:2 * P], Et[:, s % 4, P:S], ident[:, :]).then_inc(tp_done, 1)
                if t >= 3:
                    s = t - 3
                    pe.wait_ge(tp_out, TP_E + s + 1)
                    pe.wait_ge(wt_half, s + 1)
                    if s >= 4:
                        pe.wait_ge(rs[2], s - 3)
                    accumulate(M[s % 4][:, 0:D], [(WT2[:, s % 4, 0, :], ctxA[s // TB][:, :]),
                                                  (WT2[0:SB_, s % 4, 1, :], ctxB[s // TB][0:SB_, :])], pm[2])
            turn_x(TP_X2, 2)
            pe.wait_ge(mix_sb, 2)
            for t in range(NT):
                if t % TB == 0:
                    pe.wait_ge(mix_sb, 2 * (t // TB) + 2)
                pe.wait_ge(rs[2], NT)
                if t >= 2:
                    pe.wait_ge(r_sb, t - 1)
                accumulate(M[t % 2][:, 0:D], [(mixT[:, k, P * t:P * t + P], wsT[:, 1, k, :]) for k in range(2)], r_mm)
            for u in range(8):
                g, m = u // 2, u % 2
                pe.wait_ge(mix_sb, 4 + 2 * (g // 2) + 2)
                if u >= 2:
                    pe.wait_ge(kk_rel, u - 1)
                accumulate(M[2 + u % 2], [(wsT[:, 2, k, P * m:P * m + P], XT[0][:, k, G * g:G * g + G]) for k in range(2)], kk_mm)
            pe.wait_ge(r_sb, NT)
            for t in range(NT):
                pe.wait_ge(kk_sb, 8)
                if t >= 4:
                    pe.wait_ge(rs[3], t - 3)
                accumulate(M[t % 4][:, 0:D], [(XT[1][:, k, P * t:P * t + P], wsT[:, 3, k, :]) for k in range(2)], pm[3])
            turn_x(TP_X3, 3)
            pe.wait_ge(tp_out, TP_X3 + NT)
            pe.wait_ge(rs[3], NT)
            for u in range(8):
                c, g = u // NG, u % NG
                if u >= 2:
                    pe.wait_ge(vv_sb, u - 1)
                accumulate(M[u % 2], [(wsT[:, 4, k, P * c:P * c + P], XT[1][:, k, G * g:G * g + G]) for k in range(2)], vv_mm)
            pe.wait_ge(vv_sb, 8)

            def turn_mixed(g):
                pe.wait_ge(acc_sb, 2 * g + 2)
                pe.wait_ge(at_rd, 4 * g) if g else None
                for j in range(4):
                    for c in range(2):
                        c0 = 256 * (j % 2) + P * c
                        last = nc.tensor.transpose(M[4 + j // 2][:, c0:c0 + P], acc[:, g % 2, c, P * j:P * j + P], ident[:, :])
                    last.then_inc(at_mm, 1)

            for g in range(NG):
                for c in range(2):
                    for n in range(NSH):
                        u = (2 * g + c) * NSH + n
                        if u >= 4:
                            pe.wait_ge(g_sig, u - 3)
                        e0 = D * n + P * c
                        accumulate(M[u % 4], [(gateT[:, k, e0:e0 + P], XT[1][:, k, G * g:G * g + G]) for k in range(2)], g_mm)
                    if c == 0 and g >= 1:
                        turn_mixed(g - 1)
            turn_mixed(NG - 1)
            turn_x(TP_X4, 4)
            pe.wait_ge(c2_sb, 2)
            pe.wait_ge(tp_out, TP_X4 + NT)
            for u in range(2 * NG):
                g, r = u // 2, u % 2
                b = g // 2
                pe.wait_ge(sq_sb, 2 * g + 2)
                if u >= 4:
                    pe.wait_ge(d_max, u - 3)
                q0, n = (0, P) if r == 0 else (32 * b, SB_)
                cols = slice(0, P) if r == 0 else slice(P, S)
                accumulate(M[u % 4][q0:q0 + n, :],
                           [(ctx2[b][:, k, cols], XT[0][:, k, G * g:G * g + G]) for k in range(2)]
                           + [(ones[:, 0:n], XT[1][:, k, G * g:G * g + G]) for k in range(2)], d_mm)
            pe.wait_ge(ld_ip, 16)
            for r in range(NIN // P):
                turn_tile(TP_IP + r, ipraw[:, r, :])
            pe.wait_ge(ld_ow, 16)
            pe.wait_ge(d_max, 2 * NG)
            for k in range(4):
                for j in range(4):
                    last = nc.tensor.transpose(M[2 + k][:, P * j:P * j + P], owraw[:, 4 * k + j, :], ident[:, :])
                last.then_inc(ow_t, 1)
            for b in range(B):
                pe.wait_ge(chased[b], S)
                pe.wait_ge(io_f, 3)
                for n, (i0, cnt_) in enumerate(((0, P), (P, SB_))):
                    q0 = 0 if n == 0 else 32 * b
                    for e in range(2):
                        last = nc.tensor.matmul(M[b][q0:q0 + cnt_, 2 * n + e:2 * n + e + 1], zrow[:, b, i0 + e:i0 + e + cnt_],
                                                ones[0:1, 0:1], start=True, stop=True)
                last.then_inc(z_mm, 1)
            for t in range(NT):
                b, c0 = t // TB, P * (t % TB)
                pe.wait_ge(p_ok, 2 * b + 2)
                if t >= 4:
                    pe.wait_ge(rs[5], t - 3)
                else:
                    pe.wait_ge(ow_sb, 4)
                accumulate(M[2 + t % 4][:, 0:D], [(Pm[:, b, c0:c0 + P], ctxA[b][:, :]), (Pm[:, 2 + b, c0:c0 + P], ctxBB[:, :])], pm[5])

            def turn_x5(t):
                pe.wait_ge(xo[5], t + 1)
                turn_tile(TP_X5 + t, X[:, t, :])

            for t in range(TB):
                turn_x5(t)

            def make_row(what):
                s = ROWS.index(what)
                kind, b, g = what
                if kind == "in":
                    pe.wait_ge(m_ok, 4 * b + g + 1)
                    vals = mact[:, b, :]
                elif kind == "proc":
                    pe.wait_ge(p_act, b + 1)
                    vals = pact[:, :]
                else:
                    pe.wait_ge(oa_act, b + 1)
                    vals = oact[:, b, :]
                if s:
                    pe.wait_ge(bc_out, s)
                else:
                    pe.wait_ge(tp_out, TP_X5 + NT)
                for j in range(4):
                    v = vals[:, 4 * g + j:4 * g + j + 1]
                    last = nc.tensor.transpose(TP[0][:, P * j:P * j + P],
                                               bass.AP(tensor=v.tensor, offset=v.offset, ap=[v.ap[0], [0, P]]), ident[:, :])
                last.then_inc(bc_mm, 1)

            def rank(c, i):
                g, (kind, q) = ITEMS[i]
                n = len(ITEMS) * c + i
                pe.wait_ge(cmp_ok, sum(OPS) * c + sum(OPS[:i + 1]))
                if i == 0:
                    if c:
                        pe.wait_ge(kept_ok, c)
                    else:
                        pe.wait_ge(rs[5], NT)
                        pe.wait_ge(c_ok, 5)
                if kind == "new":
                    for k in range(g + 1):
                        nc.tensor.matmul(M[2 + k], ones_h[:, :], less[:, n % CR, 512 * k:512 * k + 512],
                                         start=q == 4 * k, stop=q == NQ - 1 and k < g)
                    last = nc.tensor.matmul(M[2 + g][:, P * (q % 4):P * (q % 4) + P], ones_h[:, :], tied[:, n % CR, :],
                                            start=False, stop=False)
                else:
                    for j in range(4):
                        last = nc.tensor.matmul(M[2 + g], ones_h[:, :], less[:, n % CR, 512 * j:512 * j + 512],
                                                start=False, stop=j == 3 and i == len(ITEMS) - 1)
                last.then_inc(rank_mm, 1)

            def behind(job):
                if job[0] == "turn":
                    turn_x5(job[1])
                elif job[0] == "row":
                    make_row(job[1])
                else:
                    rank(job[1], job[2])

            def aggregate(b):
                pe.wait_ge(wt_ok, b + 1)
                if b:
                    pe.wait_ge(ko_ok, b)
                nc.tensor.matmul(TP[1][:, 0:NP_], ones[:, :], wt[:, :], start=True, stop=True)
                for r in range(NP_):
                    last = nc.tensor.matmul(TP[1][:, 8:9], pv[:, r, :], wt[:, r:r + 1], start=r == 0, stop=r == NP_ - 1)
                last.then_inc(tot_mm, 1)
                pe.wait_ge(agg_ok, b + 1)
                for q in range(NQ):
                    last = nc.tensor.matmul(TP[1][:, 16 + q:17 + q], owT[:, P * q:P * q + P], agg[:, :], start=True, stop=True)
                last.then_inc(oa_mm, 1)

            def rank_group(c, g):
                for i, (g_, _) in enumerate(ITEMS):
                    if g_ == g:
                        rank(c, i)

            def output(b):
                pe.wait_ge(kept_ok, 2 + b + 1)
                for q in range(NQ):
                    last = nc.tensor.transpose(TP[1][:, 32 + q:33 + q], krow[0:1, P * q:P * q + P], ident[0:1, 0:1])
                last.then_inc(kc_mm, 1)
                pe.wait_ge(ko_ok, b + 1)
                for q in range(NQ):
                    a = kept[:, q:q + 1]
                    last = nc.tensor.matmul(M[b][:, 0:D], bass.AP(tensor=a.tensor, offset=a.offset, ap=[a.ap[0], [0, P]]),
                                            op[:, q, :], start=q == 0, stop=q == NQ - 1)
                last.then_inc(f_mm, 1)

            for u in range(B * NQ):
                b, q = u // NQ, u % NQ
                if q == 0:
                    pe.wait_ge(tp_out, TP_X5 + TB * b + TB)
                for h in range(2):
                    if u:
                        pe.wait_ge(a_gelu, 2 * u + h - 1)
                    accumulate(M[h], [(ipT[:, k, P * q:P * q + P], XT[1][:, k, L * b + G * h:L * b + G * h + G]) for k in range(2)], a_mm)
                for job in BEHIND[u]:
                    behind(job)
                if u == PROC_AT:
                    for g in range(2):
                        make_row(("proc", 0, g))
            for u in range(B * NQ, max(BEHIND) + 1):
                for job in BEHIND[u]:
                    behind(job)
            pe.wait_ge(a_gelu, 2 * B * NQ)
            make_row(("in", 1, 3))
            rank_group(1, 3)
            pe.wait_ge(ld_pv, 16)
            aggregate(0)
            for g in range(4):
                make_row(("out", 0, g))
            for g in range(4):
                rank_group(2, g)
            for g in range(2):
                make_row(("proc", 1, g))
            pe.wait_ge(ld_op, 16)
            output(0)
            aggregate(1)
            for g in range(4):
                make_row(("out", 1, g))
            for g in range(4):
                rank_group(3, g)
            output(1)

        @block.vector
        def _(dve):
            steps = [0]

            def tick(ins):
                ins.then_inc(dv, 1)
                steps[0] += 1

            def settle(but=0):
                dve.wait_ge(dv, steps[0] - but)

            V = nc.vector

            def moments(src, seen, g):
                for j in range(4):
                    tick(V.bn_stats(stat[:, j, :], src(j)))
                settle()
                for j in range(4):
                    tick(V.bn_aggr(mv[:, 4 * g + j, :], stat[:, j, :]))
                settle()
                V.tensor_scalar(ve[:, 4 * g:4 * g + 4], mv[:, 4 * g:4 * g + 4, 1], EPS, None, ALU.add).then_inc(seen, 1)

            def norm(n, g, summed):
                if g >= 2:
                    dve.wait_ge(xo[n], 4 * g - 4)
                elif g == 0 and n >= 2:
                    dve.wait_ge(xo[n - 1], NT)
                for j in range(4):
                    summed(4 * g + j, res[:, g % 2, j, :]).then_inc(rs[n], 1)
                dve.wait_ge(rs[n], 4 * g + 4)
                moments(lambda j: res[:, g % 2, j, :], vr[n], g)

            def apply(n, g):
                dve.wait_ge(sd[n], g + 1)
                for j in range(4):
                    t = 4 * g + j
                    V.tensor_scalar(X[:, t, :], res[:, g % 2, j, :], mv[:, t, 0:1], rstd[:, t:t + 1],
                                    ALU.subtract, ALU.mult).then_inc(xo[n], 1)

            def plus_x(n):
                def summed(t, dst):
                    dve.wait_ge(pm[n], t + 1)
                    return V.tensor_tensor(dst, M[t % 4][:, 0:D], X[:, t, :], ALU.add)
                return summed

            dve.wait_ge(consts, 9)
            tick(V.tensor_scalar(pbit[:, :], pidx[:, :], 4, 1, ALU.logical_shift_right, ALU.bitwise_and))
            settle()
            tick(V.tensor_copy(parm[:, 1:2], pbit[:, :]))
            settle()
            tick(V.tensor_scalar(parm[:, 0:1], parm[:, 1:2], -1.0, 1.0, ALU.mult, ALU.add))
            settle()
            for m in range(2):
                dve.wait_ge(k_mm, 2)
                src = M[2][:, 256 * m:256 * m + 256].rearrange("p (g k) -> p g k", g=NG)
                for h in range(2):
                    V.tensor_scalar(kbd[:, m, :, h, :], src, parm[:, h:h + 1], None, ALU.mult).then_inc(k_sb, 1)
            for g in range(NG):
                dve.wait_ge(v_mm, 2 * (g // 2) + 2)
                src = M[3 + g // 2][:, 256 * (g % 2):256 * (g % 2) + 256].rearrange("p (a h d) -> p a h d", a=NPAIR, h=2)
                for h in range(2):
                    V.tensor_copy(vbd[64 * h:64 * h + 64, g, :, h, :], src[64 * h:64 * h + 64, :, h, :]).then_inc(v_sb, 1)
            for u in range(8):
                dve.wait_ge(q_mm, u + 1)
                V.tensor_copy(qT[:, u % 2, G * (u // 2):G * (u // 2) + G], M[u % 2]).then_inc(q_sb, 1)
            for q in range(9):
                if q < 8:
                    for j in range(4):
                        u = 4 * q + j
                        dve.wait_ge(s_mm, u + 1)
                        tick(V.tensor_reduce(cmax[:, u, :], M[j].rearrange("p (n b) -> p n b", b=BLK), AX.X, ALU.max))
                    settle()
                    for j in range(4):
                        u = 4 * q + j
                        if u >= 4:
                            dve.wait_ge(w_exp, u - 3)
                        cm = cmax[:, u, :]
                        V.tensor_tensor(Sm[:, j, :].rearrange("p (n b) -> p n b", b=BLK), M[j].rearrange("p (n b) -> p n b", b=BLK),
                                        bass.AP(tensor=cm.tensor, offset=cm.offset, ap=[cm.ap[0], cm.ap[1], [0, BLK]]),
                                        ALU.subtract).then_inc(s_sub, 1)
                if q >= 1:
                    g, m = (q - 1) // 2, (q - 1) % 2
                    dve.wait_ge(nd_mm, q)
                    tick(V.tensor_scalar(den[:, :], M[5], 1e-10, None, ALU.add))
                    settle()
                    tick(V.reciprocal(rden[:, :], den[:, :]))
                    settle()
                    V.tensor_tensor(oT[:, m, G * g:G * g + G], M[4], rden[:, :], ALU.mult).then_inc(o_sb, 1)
            for g in range(NG):
                norm(1, g, plus_x(1))
                if g:
                    apply(1, g - 1)
            apply(1, NG - 1)
            for t in range(NT):
                dve.wait_ge(l_mm, t + 1)
                tick(V.tensor_reduce(mx[:, t:t + 1], M[4 + t % 2][:, 0:S], AX.X, ALU.max))
                settle()
                V.tensor_scalar(nmx[:, t:t + 1], mx[:, t:t + 1], -float(D) ** -0.5, None, ALU.mult).then_inc(l_mx, 1)
                if t % 4 == 3 and t >= 7:
                    g = t // 4 - 1

                    def summed(s, dst):
                        dve.wait_ge(pm[2], s + 1)
                        tick(V.reciprocal(rsum[:, s:s + 1], ssum[:, s:s + 1]))
                        settle()
                        return V.scalar_tensor_tensor(out=dst, in0=M[s % 4][:, 0:D], scalar=rsum[:, s:s + 1], in1=X[:, s, :], op0=ALU.mult, op1=ALU.add)
                    norm(2, g, summed)
                    if g:
                        apply(2, g - 1)
            norm(2, NG - 1, summed)
            apply(2, NG - 2)
            apply(2, NG - 1)
            dve.wait_ge(ld_vec, 64)
            tick(V.tensor_scalar(omm[:, :, :], mus[:, :, :], -1.0, 1.0, ALU.mult, ALU.add))
            settle()
            tick(V.memset(mtmp[:, :, 0:1], 0.0))
            for n in range(2):
                for b in range(B):
                    dve.wait_ge(tp_out, TP_X2 + TB * b + TB)
                    c0 = L * b
                    if n or b:
                        dve.wait_ge(mix_sb, 4 * n + 2 * b)
                    for k in range(2):
                        tick(V.tensor_scalar(mtmp[:, k, 1:L], XT[0][:, k, c0:c0 + L - 1], omm[:, k, n:n + 1], None, ALU.mult))
                    settle()
                    for k in range(2):
                        dst = (mixT if n == 0 else XT[0])[:, k, c0:c0 + L]
                        V.scalar_tensor_tensor(out=dst, in0=XT[0][:, k, c0:c0 + L], scalar=mus[:, k, n:n + 1], in1=mtmp[:, k, :],
                                               op0=ALU.mult, op1=ALU.add).then_inc(mix_sb, 1)
            for u in range(8):
                g, m = u // 2, u % 2
                dve.wait_ge(kk_rel, u + 1)
                V.tensor_tensor(XT[1][:, m, G * g:G * g + G], krel[:, u % 2, :], krel[:, u % 2, :], ALU.mult).then_inc(kk_sb, 1)

            def gated(t, dst):
                dve.wait_ge(pm[3], t + 1)
                tick(V.tensor_tensor(dst, M[t % 4][:, 0:D], rgate[:, t, :], ALU.mult))
                settle()
                return V.tensor_tensor(dst, dst, X[:, t, :], ALU.add)
            dve.wait_ge(r_sb, NT)
            for g in range(NG):
                norm(3, g, gated)
                if g:
                    apply(3, g - 1)
            apply(3, NG - 1)
            for c in range(2):
                for b in range(B):
                    dve.wait_ge(vv_sb, NG * c + 2 * b + 2)
                    V.tensor_copy(Vh[:, c, b, 0:HALO], Vh[:, c, b, L:L + HALO]).then_inc(halo, 1)
                    V.tensor_copy(Vh[:, c, b, HALO + L:], Vh[:, c, b, HALO:2 * HALO]).then_inc(halo, 1)
            dve.wait_ge(halo, 8)

            def mixed_norm(g):
                dve.wait_ge(at_mm, 4 * g + 4)

                def at(j):
                    return M[4 + j // 2][:, 256 * (j % 2):256 * (j % 2) + 256]
                moments(at, iv, g)
                dve.wait_ge(isd, g + 1)
                for j in range(4):
                    t = 4 * g + j
                    V.tensor_scalar(y2[:, j, :], at(j), mv[:, t, 0:1], rstd[:, t:t + 1], ALU.subtract, ALU.mult).then_inc(at_rd, 1)
                dve.wait_ge(at_rd, 4 * g + 4)
                for j in range(4):
                    tick(V.tensor_tensor(y2[:, j, :], y2[:, j, :], gam[:, :], ALU.mult))
                settle()
                for j in range(4):
                    tick(V.tensor_tensor(y2[:, j, :], y2[:, j, :], bet[:, :], ALU.add))
                settle()
                norm(4, g, lambda t, dst: V.tensor_tensor(dst, y2[:, t % 4, :], X[:, t, :], ALU.add))
                apply(4, g)

            pend = None
            for g in range(NG):
                b, h = g // 2, g % 2
                for c in range(2):
                    for n in range(NSH):
                        u = (2 * g + c) * NSH + n
                        dve.wait_ge(g_sig, u + 1)
                        v0 = HALO + SHIFTS[n] + G * h
                        dst = acc[:, g % 2, c, :] if n == 0 else pr[:, u % 4, :]
                        V.tensor_tensor(dst, gs[:, u % 4, :], Vh[:, c, b, v0:v0 + G], ALU.mult).then_inc(g_mul, 1)
                        if n >= 2:
                            dve.wait_ge(g_mul, u)
                            settle()
                            tick(V.tensor_tensor(acc[:, g % 2, c, :], acc[:, g % 2, c, :], pr[:, (u - 1) % 4, :], ALU.add))
                    dve.wait_ge(g_mul, u + 1)
                    settle()
                    V.tensor_tensor(acc[:, g % 2, c, :], acc[:, g % 2, c, :], pr[:, u % 4, :], ALU.add).then_inc(acc_sb, 1)
                    if c == 0 and g >= 1:
                        mixed_norm(g - 1)
            mixed_norm(NG - 1)
            for b in range(B):
                tick(V.tensor_scalar(ctx2[b][:, :, :], ctxT[b][:, :, :], -2.0, None, ALU.mult))
                settle()
            for b in range(B):
                tick(V.scalar_tensor_tensor(out=adump[:, :], in0=ctxA[b][:, :], scalar=1.0, in1=ctxA[b][:, :], op0=ALU.mult, op1=ALU.mult,
                                            accum_out=aa[:, b:b + 1]))
                settle()
            tick(V.scalar_tensor_tensor(out=adump[:, :], in0=ctxBB[:, :], scalar=1.0, in1=ctxBB[:, :], op0=ALU.mult, op1=ALU.mult,
                                        accum_out=aa[:, 2:3]))
            settle()
            V.memset(Mw[:, :, :], 0.0).then_inc(c2_sb, 2)
            for u in range(2 * NG):
                g, r = u // 2, u % 2
                b, h = g // 2, g % 2
                q0, n = (0, P) if r == 0 else (32 * b, SB_)
                k = b if r == 0 else 2
                dve.wait_ge(d_mm, u + 1)
                V.tensor_scalar(Drow[q0:q0 + n, k, G * h:G * h + G], M[u % 4][q0:q0 + n, :], aa[q0:q0 + n, k:k + 1], 0.0,
                                ALU.add, ALU.max).then_inc(d_max, 1)
            V.memset(Rw[:, 0:3, :], BIG).then_inc(w_init, 1)
            dve.wait_ge(w_init, 1)
            dve.wait_ge(dw_ld, 32)
            lanes = [0] + list(range(31))
            for t in range(T):
                cur, prev, nxt2 = (t + 1) % RING, t % RING, (t + 3) % RING
                if t >= 1:
                    dve.wait_ge(w_row, t)
                V.tensor_tensor(Mw[:, t % 2, :], Rw[:, prev, 0:W], Rw[:, prev, 1:W + 1], ALU.min).then_inc(w_min, 1)
                if t >= 1:
                    if t + 1 >= RING:
                        stored(dve, t + 1 - RING)
                    V.stream_shuffle(Rw[:, (t + 2) % RING, 0:1], Rw[:, prev, W:W + 1], lanes).then_inc(w_edge, 1)
                dve.wait_ge(w_min, t + 1)
                if t >= 2:
                    dve.wait_ge(w_edge, t - 1)
                if t >= RING:
                    stored(dve, t - RING)
                V.tensor_tensor_scan(Rw[:, cur, 1:W + 1], Mw[:, t % 2, :], Dw[:, t, :], Rw[:, cur, 0:1] if t else 0.0,
                                     ALU.min, ALU.add).then_inc(w_row, 1)
            dve.wait_ge(pad_ok, 7)
            dve.wait_ge(io_f, 5)
            dve.wait_ge(w_row, T)
            for n, k in enumerate((2, 0, 1)):
                dve.wait_ge(*((rrB_ld, 64) if k == 2 else (rrA_ld, 64)))
                tick(V.tensor_tensor(tmpa[:, :], Rp[:, k, 0:L], Rp[:, k, 1:L + 1], ALU.min))
                tick(V.tensor_tensor(tmpb[:, :], Rp[:, k, 0:L], Rp[:, k, 1:L + 1], ALU.is_le))
                settle()
                tick(V.tensor_tensor(tmpa[:, :], Rc[:, k, 0:L], tmpa[:, :], ALU.is_ge))
                tick(V.tensor_tensor(tmpb[:, :], iota2[:, :], tmpb[:, :], ALU.subtract))
                settle()
                tick(V.tensor_tensor(tmpa[:, :], tmpa[:, :], tmpb[:, :], ALU.mult))
                settle()
                if n:
                    dve.wait_ge(z_ok, n)
                tick(V.tensor_tensor_scan(Zf[:, :], tmpa[:, :], tmpa[:, :], 0.0, ALU.max, ALU.max))
                settle()
                V.tensor_copy(Zi[:, k, :], Zf[:, :]).then_inc(z_ok, 1)
            def warped(t, dst):
                dve.wait_ge(pm[5], t + 1)
                return V.tensor_tensor(dst, M[2 + t % 4][:, 0:D], X[:, t, :], ALU.add)

            for k in range(4):
                dve.wait_ge(ow_t, k + 1)
                V.tensor_copy(owT[:, 512 * k:512 * k + 512], M[2 + k]).then_inc(ow_sb, 1)
            for b in range(B):
                dve.wait_ge(z_mm, b + 1)
                tick(V.tensor_copy(zcol[:, b, :], M[b][:, 0:2]))
                tick(V.tensor_copy(zcol[32 * b:32 * b + SB_, 2 + b, :], M[b][32 * b:32 * b + SB_, 2:4]))
                settle()
                for k in (b, 2 + b):
                    if b or k > 1:
                        dve.wait_ge(p_ok, 2 * b + (1 if k > 1 else 0))
                    tick(V.tensor_scalar(tmpa[:, :], iota2[:, :], zcol[:, k, 0:1], None, ALU.is_ge))
                    settle()
                    V.scalar_tensor_tensor(out=Pm[:, k, :], in0=iota2[:, :], scalar=zcol[:, k, 1:2], in1=tmpa[:, :],
                                           op0=ALU.is_le, op1=ALU.mult).then_inc(p_ok, 1)
            for g in range(NG):
                norm(5, g, warped)
                if g:
                    apply(5, g - 1)
            apply(5, NG - 1)
            dve.wait_ge(c_ok, 5)
            made = [0]

            def compare(vals, r, g):
                for kind, q in items(g):
                    slot = made[0] % CR
                    if made[0] >= CR:
                        dve.wait_ge(rank_mm, made[0] - CR + 1)
                    if kind == "new":
                        v, c0, c1, c2 = vals[:, q:q + 1], P * q, P * q + P, 512 * (g + 1)
                        V.tensor_scalar(less[:, slot, 0:c1], r[:, 0:c1], v, None, ALU.is_lt).then_inc(cmp_ok, 1)
                        if c1 < c2:
                            V.tensor_scalar(less[:, slot, c1:c2], r[:, c1:c2], v, None, ALU.is_le).then_inc(cmp_ok, 1)
                        V.scalar_tensor_tensor(out=tied[:, slot, :], in0=r[:, c0:c1], scalar=v, in1=after[:, :],
                                               op0=ALU.is_equal, op1=ALU.mult).then_inc(cmp_ok, 1)
                    else:
                        for j in range(4):
                            V.tensor_scalar(less[:, slot, 512 * j:512 * j + 512], r[:, 512 * g:512 * g + 512],
                                            vals[:, 4 * q + j:4 * q + j + 1], None, ALU.is_le).then_inc(cmp_ok, 1)
                    made[0] += 1

            def row_ready(what):
                dve.wait_ge(bc_out, ROWS.index(what) + 1)

            def inputs(b, g):
                mean(b, g)
                row_ready(("in", b, g))
                compare(mact[:, b, :], row[:, b, :], g)

            def mean(b, g):
                dve.wait_ge(a_gelu, 2 * (NQ * b + 4 * g + 4))
                m = mact[:, b, 4 * g:4 * g + 4]
                tick(V.tensor_tensor(m, acts[:, b, 4 * g:4 * g + 4, 0], acts[:, b, 4 * g:4 * g + 4, 1], ALU.add))
                settle()
                V.tensor_scalar(m, m, 1.0 / L, None, ALU.mult).then_inc(m_ok, 1)
                dve.wait_ge(m_ok, 4 * b + g + 1)

            def keep(c, b, n, K):
                dve.wait_ge(rank_mm, len(ITEMS) * (c + 1))
                V.scalar_tensor_tensor(out=krow[0:n, :], in0=PS[0:n, 4:8, :].rearrange("p a b -> p (a b)"), scalar=float(K),
                                       in1=row[0:n, b, :], op0=ALU.is_lt, op1=ALU.mult).then_inc(kept_ok, 1)
                dve.wait_ge(kept_ok, c + 1)

            def process(b, parts):
                for r in parts:
                    n = NP_ * b + r
                    dve.wait_ge(ld_pw[n % 3], 16 * (n // 3 + 1))
                    if n >= 2:
                        dve.wait_ge(pw_used, n - 1)
                    if r == 0 and b:
                        dve.wait_ge(p_act, b)
                    V.scalar_tensor_tensor(out=cdump[:, r % 2, :], in0=pwt[:, n % 3, :], scalar=1.0, in1=krow[:, :], op0=ALU.mult, op1=ALU.mult,
                                           accum_out=pacc[:, r:r + 1]).then_inc(pw_used, 1)
                    if r == NP_ - 1:
                        dve.wait_ge(pw_used, n + 1)
                        V.memset(sc[:, 3:4], 0.0).then_inc(p_pre, 1)

            def weigh(b):
                dve.wait_ge(p_act, b + 1)
                tick(V.memset(cnt[:, :, :], 0.0))
                settle()
                row_ready(("proc", b, 1))
                for q in range(NP_):
                    v, c0, c1 = pact[:, q:q + 1], P * q, P * q + P
                    settle(3 if q else 0)
                    if q:
                        tick(V.tensor_scalar(cdump[:, q % 2, 0:c0], row2[:, 0:c0], v, 0.0, ALU.is_ge, ALU.add, accum_out=cnt[:, 0, q:q + 1]))
                    tick(V.tensor_scalar(cdump[:, q % 2, c0:NPROC], row2[:, c0:NPROC], v, 0.0, ALU.is_gt, ALU.add, accum_out=cnt[:, 1, q:q + 1]))
                    tick(V.scalar_tensor_tensor(out=cdump[:, q % 2, NPROC:NPROC + P], in0=row2[:, c0:c1], scalar=v, in1=before[:, :],
                                                op0=ALU.is_equal, op1=ALU.mult, accum_out=cnt[:, 2, q:q + 1]))
                V.tensor_reduce(sc[:, 0:1], row2[:, :], AX.X, ALU.max).then_inc(row2_free, 1)
                dve.wait_ge(row2_free, b + 1)
                V.tensor_scalar(sc[:, 1:2], sc[:, 0:1], -1.0, None, ALU.mult).then_inc(e_arg, 1)
                settle()
                tick(V.tensor_tensor(cnt[:, 0, :], cnt[:, 0, :], cnt[:, 1, :], ALU.add))
                settle()
                tick(V.tensor_tensor(cnt[:, 0, :], cnt[:, 0, :], cnt[:, 2, :], ALU.add))
                settle()
                tick(V.tensor_scalar(msk[:, :], cnt[:, 0, :], float(KPROC), None, ALU.is_lt))
                settle()

            def weights(b):
                dve.wait_ge(e_ok, b + 1)
                V.tensor_tensor(wt[:, :], pex[:, :], msk[:, :], ALU.mult).then_inc(wt_ok, 1)

            def aggregate(b):
                dve.wait_ge(tot_mm, b + 1)
                tick(V.tensor_reduce(sc[:, 2:3], TP[1][:, 0:NP_], AX.X, ALU.add))
                settle()
                tick(V.reciprocal(sc[:, 2:3], sc[:, 2:3]))
                settle()
                V.tensor_scalar(agg[:, :], TP[1][:, 8:9], sc[:, 2:3], None, ALU.mult).then_inc(agg_ok, 1)

            def outputs(b):
                for g in range(4):
                    row_ready(("out", b, g))
                    compare(oact[:, b, :], row[:, b, :], g)
                keep(2 + b, b, 1, KOUT)
                dve.wait_ge(kc_mm, b + 1)
                V.tensor_copy(kept[:, :], TP[1][:, 32:32 + NQ]).then_inc(ko_ok, 1)

            def last_norm(b):
                dve.wait_ge(f_mm, b + 1)
                for g in (2 * b, 2 * b + 1):
                    norm(6, g, lambda t, dst: V.tensor_tensor(dst, M[b][:, 0:D], X[:, t, :], ALU.add))
                    if g % 2:
                        apply(6, g - 1)
                apply(6, 2 * b + 1)

            for g in range(4):
                inputs(0, g)
            keep(0, 0, P, KIN)
            process(0, range(0, 4))
            inputs(1, 0)
            process(0, range(4, NP_))
            inputs(1, 1)
            inputs(1, 2)
            weigh(0)
            inputs(1, 3)
            weights(0)
            dve.wait_ge(pw_used, NP_)
            keep(1, 1, P, KIN)
            process(1, range(2))
            aggregate(0)
            process(1, range(2, NP_))
            dve.wait_ge(pw_used, 2 * NP_)
            outputs(0)
            weigh(1)
            weights(1)
            aggregate(1)
            last_norm(0)
            outputs(1)
            last_norm(1)

        block_stack.close()


_INS = ["x", "ctx_1024", "L0_attn_Wqkv", "L0_attn_Wout", "L0_ffn_W_r", "L0_ffn_W_k", "L0_ffn_W_v", "L0_ffn_mu_r",
        "L0_ffn_mu_k", "L1_attn_gate_W", "L1_attn_value_W", "L1_attn_gamma", "L1_attn_beta", "L1_ffn_input_patterns",
        "L1_ffn_process_input_weights", "L1_ffn_process_values", "L1_ffn_output_input_weights", "L1_ffn_output_patterns"]


def build(nc, arrays_of):
    args = [nc.dram_tensor(f"in_{n}", a.shape, F32, kind="ExternalInput").ap() for n, a in arrays_of.items()]
    out = nc.dram_tensor("out_0", arrays_of["x"].shape, F32, kind="ExternalOutput").ap()
    T = arrays_of["ctx_1024"].shape[1] + 2 * (arrays_of["x"].shape[1] // 64 - 1)
    C = arrays_of["x"].shape[1] // 64
    wave = [nc.dram_tensor(n, (2 * C, T, 64), F32, kind="Internal").ap() for n in ("wave_d", "wave_r")]
    decoder(nc, *args, out, *wave)


def kernel(**inputs):
    import numpy as np
    from concourse import bacc
    from concourse.bass_utils import run_bass_kernel_spmd

    nc = bacc.Bacc("TRN2", target_bir_lowering=False, num_devices=1)
    arrays = {n: np.ascontiguousarray(inputs[n]) for n in _INS}
    build(nc, arrays)
    r = run_bass_kernel_spmd(nc, [{f"in_{n}": a for n, a in arrays.items()}], core_ids=[0])
    return r.results[0]["out_0"]
```

```python
from contextlib import ExitStack

import concourse.bass as bass
from concourse import mybir

F32 = mybir.dt.float32
I32 = mybir.dt.int32
BF16 = mybir.dt.bfloat16
ALU = mybir.AluOpType
ACT = mybir.ActivationFunctionType
AX = mybir.AxisListType

P = 128
SHIFTS = (0, -32, -16, -4, -1, 1, 4, 16, 32)
HALO = 32
BIG = 1e30
EPS = 1e-5


def decoder(nc, x, ctx_in, w_qkv, w_out, w_r, w_k, w_v, mu_r, mu_k, gate_w, value_w, gamma, beta,
            in_pat, proc_w, proc_v, out_w, out_pat, out, wave_d, wave_r):
    B, L, D = x.shape
    TOK = B * L
    NT = TOK // P
    NG = 4
    G = TOK // NG
    TB = L // P
    S = ctx_in.shape[1]
    SB_ = S - P
    HEADS, HD, SEG, DIL, BLK = 16, 16, 512, 8, 64
    KEYS = SEG // DIL
    NPAIR = HEADS // 2
    NSH = len(SHIFTS)
    W = 64
    C = L // W
    SKEW = 2
    T = S + SKEW * (C - 1)
    NIN, NPROC, NOUT, DPV = in_pat.shape[0], proc_w.shape[0], out_w.shape[0], proc_v.shape[1]
    KIN, KPROC, KOUT = max(NIN // 8, 64), max(NPROC // 8, 32), max(NOUT // 8, 64)

    with ExitStack() as top:
        block_stack = ExitStack()

        def sb(stack, name, shape, dt=F32):
            return stack.enter_context(nc.sbuf_tensor(name, shape, dt))

        def sem(name):
            return top.enter_context(nc.semaphore(name))

        X = sb(top, "X", [P, NT, D])
        XT = [sb(top, f"XT{i}", [P, 2, TOK]) for i in range(2)]
        identx = sb(top, "identx", [P, P + 1])
        ident = identx[:, 0:P]
        ones = sb(top, "ones", [P, P])
        nhalf = sb(top, "nhalf", [P, 4])
        nhalves = sb(top, "nhalves", [P, P])
        aah = sb(top, "aah", [P, 3])
        bigt = sb(top, "bigt", [P, C * B * T * W // P // 16])
        res = sb(top, "res", [P, 2, 4, D])
        stat = sb(top, "stat", [P, 4, 6])
        mv = sb(top, "mv", [P, NT, 2])
        ve = sb(top, "ve", [P, NT])
        rstd = sb(top, "rstd", [P, NT])
        ctxA = [sb(top, f"ctxA{b}", [P, D]) for b in range(B)]
        ctxB = [sb(top, f"ctxB{b}", [P, D]) for b in range(B)]
        ctxBB = sb(top, "ctxBB", [P, D])
        ctxT = [sb(top, f"ctxT{b}", [P, 2, S]) for b in range(B)]

        a_mem = ExitStack()
        mus = sb(a_mem, "mus", [P, 2, 2])
        omm = sb(a_mem, "omm", [P, 2, 2])
        gam = sb(a_mem, "gam", [P, D])
        bet = sb(a_mem, "bet", [P, D])
        rawq = sb(a_mem, "rawq", [P, 6, D])
        raws = sb(a_mem, "raws", [P, 10, D])
        rawg = sb(a_mem, "rawg", [P, 2 * NSH, D])
        wqkvT = sb(a_mem, "wqkvT", [P, 2, 3 * D])
        wsT = sb(a_mem, "wsT", [P, 5, 2, D])
        gateT = sb(a_mem, "gateT", [P, 2, NSH * D])
        at_mem = ExitStack()
        qT = sb(at_mem, "qT", [P, 2, TOK])
        kbd = sb(at_mem, "kbd", [P, 2, NG, 2, KEYS])
        vbd = sb(at_mem, "vbd", [P, NG, NPAIR, 2, HD])
        halves = sb(at_mem, "halves", [P, 2, HD])
        pidx = sb(at_mem, "pidx", [P, 1], I32)
        pbit = sb(at_mem, "pbit", [P, 1], I32)
        parm = sb(at_mem, "parm", [P, 2])
        cmax = sb(at_mem, "cmax", [P, 32, SEG // BLK])
        Sm = sb(at_mem, "Sm", [P, 4, SEG])
        Wx = sb(at_mem, "Wx", [P, 8, SEG])
        den = sb(at_mem, "den", [P, SEG])
        rden = sb(at_mem, "rden", [P, SEG])
        oT = sb(at_mem, "oT", [P, 2, TOK])
        at_mem.close()
        ff_mem = ExitStack()
        Et = sb(ff_mem, "Et", [P, 4, S])
        WT2 = sb(ff_mem, "WT2", [P, 4, 2, P])
        mx = sb(ff_mem, "mx", [P, NT])
        nmx = sb(ff_mem, "nmx", [P, NT])
        ssum = sb(ff_mem, "ssum", [P, NT])
        rsum = sb(ff_mem, "rsum", [P, NT])
        mixT = sb(ff_mem, "mixT", [P, 2, TOK])
        mtmp = sb(ff_mem, "mtmp", [P, 2, L])
        rgate = sb(ff_mem, "rgate", [P, NT, D])
        krel = sb(ff_mem, "krel", [P, 2, G])
        ff_mem.close()
        mix_mem = ExitStack()
        VW = L + 2 * HALO
        gs = sb(mix_mem, "gs", [P, 4, G])
        pr = sb(mix_mem, "pr", [P, 4, G])
        Vh = sb(mix_mem, "Vh", [P, 2, B, VW])
        acc = sb(mix_mem, "acc", [P, 2, 2, G])
        y2 = sb(mix_mem, "y2", [P, 4, D])
        mix_mem.close()
        a_mem.close()

        b_mem = ExitStack()
        RR = sb(b_mem, "RR", [P, 2, 3, L + 1])
        Rc = RR[:, 0, :, :]
        Rp = RR[:, 1, :, :]
        Zs = sb(b_mem, "Zs", [P, 3, L + 1])
        iota2 = sb(b_mem, "iota2", [P, L])
        iotaf = sb(b_mem, "iotaf", [1, 2 * L])
        Zi = sb(b_mem, "Zi", [P, 3, L], I32)
        zrow = sb(b_mem, "zrow", [1, B, S + 1])
        zcol = sb(b_mem, "zcol", [P, 4, 2])
        en = sb(b_mem, "en", [P, 3])
        yz = sb(b_mem, "yz", [P, 3])
        w_mem = ExitStack()
        Drow = sb(w_mem, "Drow", [P, 3, L])
        Dw = sb(w_mem, "Dw", [64, T, W])
        RING = 64
        Rw = sb(w_mem, "Rw", [64, RING, W + 1])
        TC = T // 4
        Mw = sb(w_mem, "Mw", [64, 2, W])
        w_mem.close()
        p_mem = ExitStack()
        tmpa = sb(p_mem, "tmpa", [P, L])
        tmpb = sb(p_mem, "tmpb", [P, L])
        Zf = sb(p_mem, "Zf", [P, 3, L])
        Pm = RR[:, :, :, :].rearrange("p a k l -> p (a k l)")[:, 0:4 * L].rearrange("p (k l) -> p k l", k=4)
        owT = sb(p_mem, "owT", [P, NOUT])
        pv = sb(p_mem, "pv", [P, NPROC // P, DPV])
        op = sb(p_mem, "op", [P, NOUT // P, D])
        pwt_a = sb(p_mem, "pwt_a", [P, 3, NIN])
        acts = sb(p_mem, "acts", [P, B, 16, 2])
        mact = sb(p_mem, "mact", [P, B, 16])
        p_mem.close()
        b_mem.close()
        ipraw = XT[1][:, :, :].rearrange("p k t -> p (k t)").rearrange("p (r c) -> p r c", c=D)
        ipT = XT[0]
        owraw = res[:, :, :, :].rearrange("p a j c -> p (a j c)").rearrange("p (r c) -> p r c", c=DPV)
        c_mem = ExitStack()
        before = sb(c_mem, "before", [P, P])
        after = sb(c_mem, "after", [P, P])
        ones_h = sb(c_mem, "ones_h", [P, P], BF16)
        row = sb(c_mem, "row", [P, B, NIN])
        row2 = sb(c_mem, "row2", [P, NPROC])
        krow = sb(c_mem, "krow", [P, NIN])
        CR = 4
        less = sb(c_mem, "less", [P, CR, NIN], BF16)
        tied = sb(c_mem, "tied", [P, CR, P], BF16)
        cdump = sb(c_mem, "cdump", [P, 2, NIN], BF16)
        cnt = sb(c_mem, "cnt", [P, 3, NPROC // P])
        msk = sb(c_mem, "msk", [P, NPROC // P])
        wt = sb(c_mem, "wt", [P, 8])
        pacc = sb(c_mem, "pacc", [P, 8])
        pact = sb(c_mem, "pact", [P, 8])
        pex = sb(c_mem, "pex", [P, 8])
        sc = sb(c_mem, "sc", [P, 4])
        agg = sb(c_mem, "agg", [P, 1])
        oact = sb(c_mem, "oact", [P, B, 16])
        kept = sb(c_mem, "kept", [P, 16])
        pwt_b = sb(c_mem, "pwt_b", [P, 3, NIN])
        pwt = [t[:, i, :] for t in (pwt_a, pwt_b) for i in range(3)]
        PW = len(pwt)
        c_mem.close()

        PS = top.enter_context(nc.psum_tensor("PS", [P, 8, 512], F32))
        TP = [PS[:, i, :] for i in range(2)]
        M = [PS[:, 2 + i, :] for i in range(6)]

        MV = [M[i] for i in (0, 1, 4, 5)]

        ld_wq, ld_ws, ld_wg, ld_ctx, ld_vec = (sem(n) for n in ("ld_wq", "ld_ws", "ld_wg", "ld_ctx", "ld_vec"))
        ld_x = [sem(f"ld_x{g}") for g in range(NG)]
        consts = sem("consts")
        tp_done, tp_out = sem("tp_done"), sem("tp_out")
        dv = sem("dv")
        q_mm, q_sb, k_mm, k_sb, v_mm, v_sb = (sem(n) for n in ("q_mm", "q_sb", "k_mm", "k_sb", "v_mm", "v_sb"))
        s_mm, s_sub, w_exp, nd_mm, o_sb = (sem(n) for n in ("s_mm", "s_sub", "w_exp", "nd_mm", "o_sb"))
        NL = range(1, 7)
        pm = [None] + [sem(f"pm{n}") for n in NL]
        rs = [None] + [sem(f"rs{n}") for n in NL]
        vr = [None] + [sem(f"vr{n}") for n in NL]
        sd = [None] + [sem(f"sd{n}") for n in NL]
        xo = [None] + [sem(f"xo{n}") for n in NL]
        iv, isd = sem("iv"), sem("isd")
        l_mm, l_mx, l_exp = sem("l_mm"), sem("l_mx"), sem("l_exp")
        mix_sb, r_mm, r_sb, kk_mm, kk_rel, kk_sb = (sem(n) for n in ("mix_sb", "r_mm", "r_sb", "kk_mm", "kk_rel", "kk_sb"))
        vv_mm, vv_sb, halo, g_mm, g_sig, g_mul, acc_sb, at_mm, at_rd = (
            sem(n) for n in ("vv_mm", "vv_sb", "halo", "g_mm", "g_sig", "g_mul", "acc_sb", "at_mm", "at_rd"))
        wt_half, c_zero, big_ok = sem("wt_half"), sem("c_zero"), sem("big_ok")
        sq_sb, ah_sb, d_mm, d_sq, d_rt, dw_fill, big_st = (
            sem(n) for n in ("sq_sb", "ah_sb", "d_mm", "d_sq", "d_rt", "dw_fill", "big_st"))
        dw_st = [sem(f"dw_st{b}") for b in range(B)]
        dw_ld = [sem(f"dw_ld{c}") for c in range(4)]
        w_init, w_min, w_row, w_edge = (sem(n) for n in ("w_init", "w_min", "w_row", "w_edge"))
        rw_st = [sem(f"rw_st{i}") for i in range(8)]
        rrA_ld, rrB_ld, pad_ok, z_ok, io_f, z_mm, p_ok = (
            sem(n) for n in ("rrA_ld", "rrB_ld", "pad_ok", "z_ok", "io_f", "z_mm", "p_ok"))
        sq_sum, zf_ok, en_mm, y_ok = sem("sq_sum"), sem("zf_ok"), sem("en_mm"), sem("y_ok")
        zs_ld = [sem(f"zs_ld{k}") for k in range(3)]
        chased = [sem(f"chased{b}") for b in range(B)]
        ld_ip, ld_ow, ld_pv, ld_op = sem("ld_ip"), sem("ld_ow"), sem("ld_pv"), sem("ld_op")
        ld_pw = [sem(f"ld_pw{i}") for i in range(6)]
        pw_used = sem("pw_used")
        ow_t, ow_sb, a_mm, a_gelu, m_ok, bc_mm, bc_out, row2_free, kept_ok = (
            sem(n) for n in ("ow_t", "ow_sb", "a_mm", "a_gelu", "m_ok", "bc_mm", "bc_out", "row2_free", "kept_ok"))
        cmp_ok, rank_mm, p_act, c_ok, e_arg, e_ok, wt_ok, tot_mm, agg_ok, oa_mm, oa_act, kc_mm, ko_ok, f_mm = (
            sem(n) for n in ("cmp_ok", "rank_mm", "p_act", "c_ok", "e_arg", "e_ok", "wt_ok", "tot_mm", "agg_ok",
                             "oa_mm", "oa_act", "kc_mm", "ko_ok", "f_mm"))
        out_st = sem("out_st")

        TP_WQ, TP_X0, TP_CTX, TP_WS, TP_WG = 0, 6, 22, 26, 36
        TP_X1 = TP_WG + 2 * NSH
        TP_E = TP_X1 + NT
        TP_X2 = TP_E + NT
        TP_X3 = TP_X2 + NT
        TP_X4 = TP_X3 + NT
        TP_IP = TP_X4 + NT
        TP_X5 = TP_IP + NIN // P

        SIDE = [range(0, 4), range(4, 9), range(9, 14), range(14, 19), range(19, 24), range(24, 28), range(28, 32), range(0)]
        NP_ = NPROC // P
        TURN_AT = 1
        NORM_AT = [3, 5, 7, 9, 11, 14]

        DIST = (("x", 0), ("x", 1), ("d", 0), ("x", 2), ("d", 1), ("x", 3), ("d", 2), ("d", 3))

        NQ = NIN // P
        assert NOUT == NIN

        def items(g):
            return [("new", 4 * g + j) for j in range(4)] + [("old", h) for h in range(g)]
        ITEMS = [(g, it) for g in range(4) for it in items(g)]
        OPS = [4 if kind == "old" else 2 if q % 4 == 3 else 3 for _, (kind, q) in ITEMS]
        ROWS = ([("in", 0, g) for g in range(4)] + [("in", 1, g) for g in range(3)] + [("proc", 0, g) for g in range(2)]
                + [("in", 1, 3)] + [("out", 0, g) for g in range(4)] + [("proc", 1, g) for g in range(2)]
                + [("out", 1, g) for g in range(4)])
        BEHIND = {u: [] for u in range(B * NQ)}
        BEHIND[1] += [("cross", 1)]
        BEHIND[4] += [("warp", t) for t in range(TB, TB + 4)]
        BEHIND[5] += [("warp", t) for t in range(TB + 4, NT)]
        BEHIND[6] += [("turn", t) for t in range(TB, TB + 4)]
        BEHIND[7] += [("turn", t) for t in range(TB + 4, NT)]
        ROW_AT = (8, 9, 12, 16, 21, 25, 28, 33)
        for n, (b, g) in enumerate((b, g) for b in range(B) for g in range(4)):
            at = ROW_AT[n]
            if at < B * NQ:
                BEHIND[at].append(("row", ("in", b, g)))
                todo = [("rank", b, i) for i, (g_, _) in enumerate(ITEMS) if g_ == g]
                for k, (i0, i1) in enumerate(((0, 2), (2, 4), (4, 7)) if n == 3 else ((0, 2), (2, 4), (4, 6), (6, 7))):
                    BEHIND.setdefault(at + 1 + k, [])
                    BEHIND[at + 1 + k] += todo[i0:i1]
        PROC_AT = 29
        STEP = T // 8
        STORES = {}
        for t0 in range(0, T, STEP):
            n = min(T, t0 + STEP) - t0
            STORES[t0] = 2 * B if (t0 + 1) % RING + n > RING else B

        def stored(eng, t):
            eng.wait_ge(rw_st[t // STEP], 16 * STORES[t // STEP * STEP])

        block = block_stack.enter_context(nc.Block())

        def rows(w):
            return w.rearrange("(r p) c -> p r c", p=P)

        @block.sync
        def _(sp):
            xt = x.rearrange("b l d -> (b l) d").rearrange("(t p) d -> p t d", p=P)
            ot = out.rearrange("b l d -> (b l) d").rearrange("(t p) d -> p t d", p=P)
            sp.dma_start(rawq[:, :, :], rows(w_qkv)).then_inc(ld_wq, 16)
            for g in range(NG):
                sp.dma_start(X[:, 4 * g:4 * g + 4, :], xt[:, 4 * g:4 * g + 4, :]).then_inc(ld_x[g], 16)
            sp.wait_ge(c_zero, 1)
            for b in range(B):
                sp.dma_start(ctxA[b][:, :], ctx_in[b, 0:P, :]).then_inc(ld_ctx, 16)
                sp.dma_start(ctxB[b][0:SB_, :], ctx_in[b, P:S, :]).then_inc(ld_ctx, 16)
                sp.dma_start(ctxBB[32 * b:32 * b + SB_, :], ctx_in[b, P:S, :]).then_inc(ld_ctx, 16)
            for n, w in enumerate((w_out, w_r, w_k, w_v, value_w)):
                sp.dma_start(raws[:, 2 * n:2 * n + 2, :], rows(w)).then_inc(ld_ws, 16)
            sp.dma_start(rawg[:, :, :], rows(gate_w)).then_inc(ld_wg, 16)
            with nc.allow_non_contiguous_dma(reason="two vectors of 256 values onto partitions"):
                for n, v in enumerate((mu_r, mu_k)):
                    sp.dma_start(mus[:, :, n:n + 1], v.rearrange("(k p) -> p k", p=P).unsqueeze(2)).then_inc(ld_vec, 16)
            for t_, v in ((gam, gamma), (bet, beta)):
                sp.dma_start(t_[:, :], bass.AP(tensor=v.tensor, offset=v.offset, ap=[[0, P], [1, D]])).then_inc(ld_vec, 16)
            sp.wait_ge(big_ok, 1)
            per = C * B * T * W // P
            sp.dma_start(bass.AP(tensor=wave_d.tensor, offset=wave_d.offset, ap=[[per, P], [per // 16, 16], [1, per // 16]]),
                         bass.AP(tensor=bigt[:, :].tensor, offset=bigt[:, :].offset, ap=[bigt[:, :].ap[0], [0, 16], [1, per // 16]])).then_inc(big_st, 16)

            def skewed(dram, b, i0, n, c0=0, nc_=C):
                return bass.AP(tensor=dram.tensor, offset=dram.offset + b * C * T * W + c0 * (T + SKEW) * W + i0 * W,
                               ap=[[W, n], [(T + SKEW) * W, nc_], [1, W]])

            def chunks(ap):
                return ap.rearrange("p (c w) -> p c w", w=W)

            sp.wait_ge(big_st, 16)
            for b in range(B):
                for h in range(2):
                    for r, (q0, i0, n, k) in enumerate(((0, 0, P, b), (32 * b, P, SB_, 2))):
                        sp.wait_ge(d_rt, 4 * b + 2 * h + r + 1)
                        sp.dma_start(skewed(wave_d, b, i0, n, C // 2 * h, C // 2),
                                     chunks(Drow[q0:q0 + n, k, G * h:G * h + G])).then_inc(dw_st[b], 16)
            for c in range(4):
                sp.wait_ge(dw_fill, c + 1)
                for b in range(B):
                    sp.wait_ge(dw_st[b], 64)
                    sp.dma_start(Dw[32 * b + 1:32 * b + 1 + C, TC * c:TC * (c + 1), :].rearrange("p t w -> p (t w)"),
                                 wave_d[b * C:(b + 1) * C, TC * c:TC * (c + 1), :].rearrange("p t w -> p (t w)")).then_inc(dw_ld[c], 16)
            sp.wait_ge(d_mm, 2 * NG)
            sp.dma_start(ipraw, rows(in_pat)).then_inc(ld_ip, 16)
            sp.wait_ge(xo[4], NT)
            sp.dma_start(owraw, rows(out_w)).then_inc(ld_ow, 16)
            tA = P + SKEW * (C - 1)
            for t0 in list(range(0, T, STEP)):
                t1 = min(T, t0 + STEP)
                sp.wait_ge(w_row, t1)
                for b in range(B):
                    s0 = (t0 + 1) % RING
                    n0 = min(t1 - t0, RING - s0)
                    sp.dma_start(wave_r[b * C:(b + 1) * C, t0:t0 + n0, :],
                                 Rw[32 * b + 1:32 * b + 1 + C, s0:s0 + n0, 1:W + 1]).then_inc(rw_st[t0 // STEP], 16)
                    if n0 < t1 - t0:
                        sp.dma_start(wave_r[b * C:(b + 1) * C, t0 + n0:t1, :],
                                     Rw[32 * b + 1:32 * b + 1 + C, 0:t1 - t0 - n0, 1:W + 1]).then_inc(rw_st[t0 // STEP], 16)
                if t0 < tA <= t1:
                    for s0 in range(0, t1, STEP):
                        sp.wait_ge(rw_st[s0 // STEP], 16 * STORES[s0])
                    sp.wait_ge(pad_ok, 6)
                    for b in range(B):
                        sp.dma_start(chunks(Rc[:, b, 1:L + 1]), skewed(wave_r, b, 0, P)).then_inc(rrA_ld, 16)
                        sp.dma_start(chunks(Rp[1:P, b, 1:L + 1]), skewed(wave_r, b, 0, P - 1)).then_inc(rrA_ld, 16)
            for s0 in range(0, T, STEP):
                sp.wait_ge(rw_st[s0 // STEP], 16 * STORES[s0])
            for b in range(B):
                q0 = 32 * b
                sp.dma_start(chunks(Rc[q0:q0 + SB_, 2, 1:L + 1]), skewed(wave_r, b, P, SB_)).then_inc(rrB_ld, 16)
                sp.dma_start(chunks(Rp[q0:q0 + SB_, 2, 1:L + 1]), skewed(wave_r, b, P - 1, SB_)).then_inc(rrB_ld, 16)
            for n, k in enumerate((0, 2, 1)):
                sp.wait_ge(zf_ok, n + 1)
                sp.wait_ge(pad_ok, 10)
                sp.dma_start(Zs[1:P, k, 1:L + 1], Zf[0:P - 1, k, :]).then_inc(zs_ld[k], 16)
            sp.dma_start(pv[:, :, :], rows(proc_v)).then_inc(ld_pv, 16)
            sp.dma_start(op[:, :, :], rows(out_pat)).then_inc(ld_op, 16)
            for n in range(B * NP_):
                if n == 3:
                    sp.wait_ge(pm[5], NT)
                if n >= PW:
                    sp.wait_ge(pw_used, n - PW + 1)
                sp.dma_start(pwt[n % PW], rows(proc_w)[:, n % NP_, :]).then_inc(ld_pw[n % PW], 16)
            for g in range(NG):
                sp.wait_ge(xo[6], 4 * g + 4)
                sp.dma_start(ot[:, 4 * g:4 * g + 4, :], X[:, 4 * g:4 * g + 4, :]).then_inc(out_st, 16)
            sp.wait_ge(out_st, 16 * NG)

        def walk_back(eng, copy, b):
            at = L - 1
            for i in range(S - 1, -1, -2):
                if i == S - 1:
                    eng.wait_ge(z_ok, 2)
                if i == P - 1 and b:
                    eng.wait_ge(z_ok, 3)
                q = i if i < P else 32 * b + i - P
                z = eng.value_load(Zi[q:q + 1, b if i < P else 2, bass.ds(at, 1)], min_val=0, max_val=2 * (L - 1))
                copy(zrow[:, b, i - 1:i], iotaf[:, bass.ds(z, 1)]).then_inc(chased[b], 1)
                at = z // 2

        @block.gpsimd
        def _(pool):
            nc.gpsimd.memset(ctxBB[:, :], 0.0).then_inc(c_zero, 1)
            nc.gpsimd.memset(identx[:, :], 0.0).then_inc(consts, 1)
            nc.gpsimd.memset(ones[:, :], 1.0).then_inc(consts, 1)
            nc.gpsimd.memset(nhalf[:, :], -0.5).then_inc(consts, 1)
            nc.gpsimd.iota(pidx[:, :], pattern=[[0, 1]], base=0, channel_multiplier=1).then_inc(consts, 1)
            nc.gpsimd.memset(vbd[:, :, :, :, :], 0.0).then_inc(consts, 1)
            nc.gpsimd.memset(halves[:, :, :], 0.0).then_inc(consts, 1)
            pool.wait_ge(consts, 6)
            nc.gpsimd.affine_select(out=ident[:, :], in_=ident[:, :], compare_op=ALU.not_equal, fill=1.0, base=0,
                                    pattern=[[-1, P]], channel_multiplier=1).then_inc(consts, 1)
            for h in range(2):
                pool.wait_ge(consts, 7 + h)
                nc.gpsimd.memset(halves[64 * h:64 * h + 64, h, :], 1.0).then_inc(consts, 1)
            pool.wait_ge(consts, 9)
            nc.gpsimd.memset(nhalves[:, :], -0.5).then_inc(consts, 1)
            nc.gpsimd.memset(bigt[:, :], BIG).then_inc(big_ok, 1)

            def inv_std(seen, made, g):
                pool.wait_ge(seen, g + 1)
                nc.gpsimd.tensor_tensor(rstd[:, 4 * g:4 * g + 4], ve[:, 4 * g:4 * g + 4], nhalf[:, :], ALU.pow).then_inc(made, 1)

            for n in (1, 2, 3):
                for g in range(NG):
                    inv_std(vr[n], sd[n], g)
            for g in range(NG):
                inv_std(iv, isd, g)
                inv_std(vr[4], sd[4], g)
            pool.wait_ge(xo[4], NT)
            for c in range(4):
                nc.gpsimd.memset(Dw[:, TC * c:TC * (c + 1), :], BIG).then_inc(dw_fill, 1)
            nc.gpsimd.memset(Rc[:, :, 0:1], BIG).then_inc(pad_ok, 1)
            nc.gpsimd.memset(Rp[:, :, 0:1], BIG).then_inc(pad_ok, 1)
            nc.gpsimd.memset(Rp[0:1, 0, 1:L + 1], BIG).then_inc(pad_ok, 1)
            nc.gpsimd.memset(Rp[0:1, 1, 1:L + 1], BIG).then_inc(pad_ok, 1)
            nc.gpsimd.memset(Rc[:, 2, 1:L + 1], BIG).then_inc(pad_ok, 1)
            nc.gpsimd.memset(Rp[:, 2, 1:L + 1], BIG).then_inc(pad_ok, 1)
            nc.gpsimd.memset(zcol[:, :, :], BIG).then_inc(pad_ok, 1)
            nc.gpsimd.memset(yz[:, :], 0.0).then_inc(pad_ok, 1)
            nc.gpsimd.memset(Zs[:, :, 0:1], 0.0).then_inc(pad_ok, 1)
            nc.gpsimd.memset(Zs[0:1, :, 1:L + 1], 0.0).then_inc(pad_ok, 1)
            nc.gpsimd.iota(Zi[:, 2, :], pattern=[[2, L]], base=0, channel_multiplier=0).then_inc(io_f, 1)
            nc.gpsimd.iota(Zi[0:1, 0:2, :], pattern=[[1, 2 * L]], base=0, channel_multiplier=0).then_inc(io_f, 1)
            nc.gpsimd.memset(zrow[:, :, S:S + 1], float(2 * (L - 1))).then_inc(io_f, 1)
            nc.gpsimd.memset(zrow[:, :, 0:S], 0.0).then_inc(io_f, 1)
            pool.wait_ge(io_f, 4)
            nc.gpsimd.tensor_copy(iota2[:, :], Zi[:, 2, :]).then_inc(io_f, 1)
            nc.gpsimd.tensor_copy(iotaf[:, :], Zi[0:1, 0:2, :].rearrange("p a b -> p (a b)")).then_inc(io_f, 1)
            pool.wait_ge(io_f, 6)
            walk_back(pool, nc.gpsimd.tensor_copy, 1)
            for g in range(NG):
                inv_std(vr[5], sd[5], g)
            pool.wait_ge(pm[5], NT)
            nc.gpsimd.memset(before[:, :], 1.0).then_inc(c_ok, 1)
            nc.gpsimd.memset(after[:, :], 1.0).then_inc(c_ok, 1)
            nc.gpsimd.memset(ones_h[:, :], 1.0).then_inc(c_ok, 1)
            pool.wait_ge(c_ok, 3)
            nc.gpsimd.affine_select(out=before[:, :], in_=before[:, :], compare_op=ALU.is_gt, fill=0.0, base=0,
                                    pattern=[[-1, P]], channel_multiplier=1).then_inc(c_ok, 1)
            nc.gpsimd.affine_select(out=after[:, :], in_=after[:, :], compare_op=ALU.is_gt, fill=0.0, base=0,
                                    pattern=[[1, P]], channel_multiplier=-1).then_inc(c_ok, 1)
            for g in range(NG):
                inv_std(vr[6], sd[6], g)

        @block.scalar
        def _(act):
            def pair(i):
                return TP[i % 2][:, 0:2 * P].rearrange("p (k c) -> p k c", k=2)

            def tp_copy(i, dst, n=P):
                act.wait_ge(tp_done, i + 1)
                nc.scalar.copy(dst, pair(i)[:, :, 0:n]).then_inc(tp_out, 1)

            def x_copy(first, buf, t):
                tp_copy(first + t, XT[buf][:, :, P * t:P * t + P])

            for r in range(6):
                tp_copy(TP_WQ + r, wqkvT[:, :, P * r:P * r + P])
            for t in range(NT):
                x_copy(TP_X0, 0, t)
            for u in range(2, 8):
                act.wait_ge(q_mm, u + 1)
                nc.scalar.copy(qT[:, u % 2, G * (u // 2):G * (u // 2) + G], M[4 + u % 2]).then_inc(q_sb, 1)
            for u in range(32):
                act.wait_ge(s_sub, u + 1)
                if u >= 8:
                    act.wait_ge(nd_mm, u // 4 - 1)
                nc.scalar.activation(Wx[:, u % 8, :], Sm[:, u % 4, :], ACT.Exp, scale=float(HD) ** -0.5).then_inc(w_exp, 1)
                if u % 4 == 3:
                    for n in SIDE[u // 4]:
                        if n < 4:
                            tp_copy(TP_CTX + n, ctxT[n // 2][:, :, 0:P] if n % 2 == 0 else ctxT[n // 2][:, :, P:S], P if n % 2 == 0 else SB_)
                        elif n < 14:
                            tp_copy(TP_CTX + n, wsT[:, (n - 4) // 2, :, P * (n % 2):P * (n % 2) + P])
                        else:
                            tp_copy(TP_CTX + n, gateT[:, :, P * (n - 14):P * (n - 14) + P])
            for t in range(NT):
                x_copy(TP_X1, 1, t)
            for p in range(NT // 2 + 1):
                if p < NT // 2:
                    act.wait_ge(l_mx, p + 1)
                    for h in range(2):
                        t = 2 * p + h
                        if t >= 4:
                            act.wait_ge(tp_done, TP_E + t - 3)
                        nc.scalar.activation(Et[:, t % 4, :], M[4 + p % 2][:, 256 * h:256 * h + S], ACT.Exp, scale=float(D) ** -0.5,
                                             bias=nmx[:, t:t + 1], accum_out=ssum[:, t:t + 1]).then_inc(l_exp, 1)
                if p >= 1:
                    for s in (2 * p - 2, 2 * p - 1):
                        act.wait_ge(tp_done, TP_E + s + 1)
                        if s >= 4:
                            act.wait_ge(pm[2], s - 3)
                        src = pair(TP_E + s)
                        nc.scalar.copy(WT2[:, s % 4, 0, :], src[:, 0, :]).then_inc(wt_half, 1)
                        nc.scalar.copy(WT2[0:SB_, s % 4, 1, :], src[0:SB_, 1, :]).then_inc(tp_out, 1)
            for t in range(NT):
                x_copy(TP_X2, 0, t)
            for t in range(NT):
                act.wait_ge(r_mm, t + 1)
                nc.scalar.activation(rgate[:, t, :], M[t % 2][:, 0:D], ACT.Sigmoid).then_inc(r_sb, 1)
            for u in range(8):
                act.wait_ge(kk_mm, u + 1)
                if u >= 2:
                    act.wait_ge(kk_sb, u - 1)
                nc.scalar.activation(krel[:, u % 2, :], M[2 + u % 2], ACT.Relu).then_inc(kk_rel, 1)
            for b in range(B):
                for t in range(TB * b, TB * b + TB):
                    x_copy(TP_X3, 1, t)
                for u in range(4 * b, 4 * b + 4):
                    g, c = u // 2, u % 2
                    act.wait_ge(vv_mm, u + 1)
                    c0 = HALO + (g % 2) * G
                    nc.scalar.copy(Vh[:, c, b, c0:c0 + G], M[2 + u % 2]).then_inc(vv_sb, 1)
            for u in range(NG * 2 * NSH):
                act.wait_ge(g_mm, u + 1)
                if u >= 4:
                    act.wait_ge(g_mul, u - 3)
                nc.scalar.activation(gs[:, u % 4, :], M[u % 4], ACT.Sigmoid).then_inc(g_sig, 1)
            act.wait_ge(g_mul, NG * 2 * NSH)
            for what, g in DIST:
                if what == "x":
                    for t in range(4 * g, 4 * g + 4):
                        x_copy(TP_X4, 0, t)
                    act.wait_ge(tp_out, TP_X4 + 4 * g + 4)
                    for k in range(2):
                        nc.scalar.activation(XT[1][:, k, G * g:G * g + G], XT[0][:, k, G * g:G * g + G], ACT.Square).then_inc(sq_sb, 1)
                else:
                    b, h = g // 2, g % 2
                    for r in range(2):
                        u = 2 * g + r
                        q0, n = (0, P) if r == 0 else (32 * b, SB_)
                        k = b if r == 0 else 2
                        dst = Drow[q0:q0 + n, k, G * h:G * h + G]
                        act.wait_ge(d_mm, u + 1)
                        nc.scalar.activation(dst, M[u % 4][q0:q0 + n, :], ACT.Relu, scale=-1.0, bias=aah[q0:q0 + n, k:k + 1]).then_inc(d_sq, 1)
                        act.wait_ge(d_sq, u + 1)
                        nc.scalar.activation(dst, dst, ACT.Sqrt, scale=2.0).then_inc(d_rt, 1)
            for r in range(NIN // P):
                tp_copy(TP_IP + r, ipT[:, :, P * r:P * r + P])
            act.wait_ge(io_f, 6)
            walk_back(act, nc.scalar.copy, 0)
            for t in range(TB):
                x_copy(TP_X5, 1, t)

            def row_copy(what):
                s = ROWS.index(what)
                kind, b, g = what
                act.wait_ge(bc_mm, s + 1)
                if s == 0:
                    act.wait_ge(pm[5], NT)
                if kind == "out":
                    act.wait_ge(kept_ok, b + 1)
                if kind == "proc" and b:
                    act.wait_ge(row2_free, b)
                dst = row2[:, 512 * g:512 * g + 512] if kind == "proc" else row[:, b, 512 * g:512 * g + 512]
                nc.scalar.copy(dst, TP[0]).then_inc(bc_out, 1)

            def proc_gelu(b):
                act.wait_ge(pw_used, NP_ * (b + 1))
                nc.scalar.activation(pact[:, :], pacc[:, :], ACT.Gelu).then_inc(p_act, 1)

            def behind(job):
                if job[0] == "turn":
                    x_copy(TP_X5, 1, job[1])
                elif job[0] == "row":
                    row_copy(job[1])

            def proc_exp(b):
                act.wait_ge(e_arg, b + 1)
                nc.scalar.activation(pex[:, :], pact[:, :], ACT.Exp, bias=sc[:, 1:2]).then_inc(e_ok, 1)

            def out_gelu(b):
                act.wait_ge(oa_mm, b + 1)
                nc.scalar.activation(oact[:, b, :], TP[1][:, 16:16 + NQ], ACT.Gelu).then_inc(oa_act, 1)

            for u in range(B * NQ):
                b, q = u // NQ, u % NQ
                for h in range(2):
                    act.wait_ge(a_mm, 2 * u + h + 1)
                    nc.scalar.activation(M[h], M[h], ACT.Gelu, accum_out=acts[:, b, q, h:h + 1]).then_inc(a_gelu, 1)
                for job in BEHIND[u]:
                    behind(job)
                if u == PROC_AT:
                    proc_gelu(0)
                    for g in range(2):
                        row_copy(("proc", 0, g))
            row_copy(("in", 1, 3))
            proc_exp(0)
            out_gelu(0)
            for g in range(4):
                row_copy(("out", 0, g))
            proc_gelu(1)
            for g in range(2):
                row_copy(("proc", 1, g))
            proc_exp(1)
            out_gelu(1)
            for g in range(4):
                row_copy(("out", 1, g))

        @block.tensor
        def _(pe):
            def turn(i, lo, hi, n=P):
                if i >= 2:
                    pe.wait_ge(tp_out, i - 1)
                nc.tensor.transpose(TP[i % 2][0:lo.shape[1], 0:n], lo, ident[0:n, 0:n])
                nc.tensor.transpose(TP[i % 2][0:hi.shape[1], P:P + n], hi, ident[0:n, 0:n]).then_inc(tp_done, 1)

            def turn_tile(i, src, n=P):
                turn(i, src[:, 0:P], src[:, P:2 * P], n)

            def accumulate(dst, parts, sem_=None):
                for i, (a, b_) in enumerate(parts):
                    last = nc.tensor.matmul(dst, a, b_, start=i == 0, stop=i == len(parts) - 1)
                if sem_ is not None:
                    last.then_inc(sem_, 1)

            def side_jobs(q):
                for n in SIDE[q]:
                    i = TP_CTX + n
                    if n < 4:
                        pe.wait_ge(ld_ctx, 96)
                        if n % 2 == 0:
                            turn_tile(i, ctxA[n // 2][:, :])
                        else:
                            turn_tile(i, ctxB[n // 2][0:SB_, :], SB_)
                    elif n < 14:
                        pe.wait_ge(ld_ws, 80)
                        turn_tile(i, raws[:, n - 4, :])
                    else:
                        pe.wait_ge(ld_wg, 16)
                        turn_tile(i, rawg[:, n - 14, :])

            pe.wait_ge(consts, 9)
            pe.wait_ge(ld_wq, 16)
            for r in range(6):
                turn_tile(TP_WQ + r, rawq[:, r, :])
            for t in range(NT):
                if t % 4 == 0:
                    pe.wait_ge(ld_x[t // 4], 16)
                turn_tile(TP_X0 + t, X[:, t, :])
            pe.wait_ge(tp_out, TP_X0 + NT)
            for m in range(2):
                accumulate(M[2][:, 256 * m:256 * m + 256],
                           [(wqkvT[:, k, D + P * m:D + P * m + P], XT[0][:, k, ::DIL]) for k in range(2)], k_mm)
            for b in range(B):
                accumulate(M[3 + b][:, 0:D], [(XT[0][:, k, L * b:L * b + L:DIL], wqkvT[:, k, 2 * D:3 * D]) for k in range(2)], v_mm)

            def queries(u, bank):
                g, m = u // 2, u % 2
                accumulate(bank, [(wqkvT[:, k, P * m:P * m + P], XT[0][:, k, G * g:G * g + G]) for k in range(2)], q_mm)

            for u in range(2):
                queries(u, M[u])
            pe.wait_ge(q_sb, 2)
            pe.wait_ge(k_sb, 4)
            pe.wait_ge(v_sb, 8)
            for q in range(9):
                if q < 8:
                    g, m = q // 2, q % 2
                    for j in range(4):
                        if q >= 1:
                            pe.wait_ge(s_sub, 4 * (q - 1) + j + 1)
                        r = slice(32 * j, 32 * j + 32)
                        nc.tensor.matmul(M[j], kbd[r, m, g, :, :].rearrange("p h k -> p (h k)"),
                                         qT[r, m, G * g:G * g + G], start=True, stop=True).then_inc(s_mm, 1)
                if q == 0:
                    for u in range(2, 8):
                        if u >= 4:
                            pe.wait_ge(q_sb, u - 1)
                        queries(u, M[4 + u % 2])
                    pe.wait_ge(q_sb, 8)
                if q >= 1:
                    g, m = (q - 1) // 2, (q - 1) % 2
                    if q >= 2:
                        pe.wait_ge(o_sb, q - 1)
                    for j in range(4):
                        u = 4 * (q - 1) + j
                        pe.wait_ge(w_exp, u + 1)
                        r = slice(32 * j, 32 * j + 32)
                        nc.tensor.matmul(M[4][r, :], vbd[:, g, 4 * m + j, :, :].rearrange("p h d -> p (h d)"),
                                         Wx[:, u % 8, :], start=True, stop=True)
                        last = nc.tensor.matmul(M[5][r, :], halves[:, :, :].rearrange("p h d -> p (h d)"),
                                                Wx[:, u % 8, :], start=True, stop=True)
                    last.then_inc(nd_mm, 1)
                    side_jobs(q - 1)
            for t in range(NT):
                pe.wait_ge(o_sb, 2 * (t // 4) + 2)
                pe.wait_ge(s_sub, 32)
                if t >= 4:
                    pe.wait_ge(rs[1], t - 3)
                accumulate(M[t % 4][:, 0:D], [(oT[:, k, P * t:P * t + P], wsT[:, 0, k, :]) for k in range(2)], pm[1])

            def turn_x(first, n):
                for t in range(NT):
                    pe.wait_ge(xo[n], t + 1)
                    turn_tile(first + t, X[:, t, :])

            turn_x(TP_X1, 1)
            for p in range(NT // 2 + 2):
                if p < NT // 2:
                    pe.wait_ge(tp_out, TP_X1 + 2 * p + 2)
                    if p >= 2:
                        pe.wait_ge(l_exp, 2 * p - 2)
                    for h in range(2):
                        t = 2 * p + h
                        accumulate(M[4 + p % 2][:, 256 * h:256 * h + S],
                                   [(XT[1][:, k, P * t:P * t + P], ctxT[t // TB][:, k, :]) for k in range(2)], l_mm)
                if 1 <= p <= NT // 2:
                    for s in (2 * p - 2, 2 * p - 1):
                        i = TP_E + s
                        pe.wait_ge(l_exp, s + 1)
                        pe.wait_ge(tp_out, i - 1)
                        nc.tensor.transpose(TP[i % 2][:, 0:P], Et[:, s % 4, 0:P], ident[:, :])
                        nc.tensor.transpose(TP[i % 2][0:SB_, P:2 * P], Et[:, s % 4, P:S], ident[:, :]).then_inc(tp_done, 1)
                if p >= 2:
                    for s in (2 * p - 4, 2 * p - 3):
                        pe.wait_ge(tp_out, TP_E + s + 1)
                        pe.wait_ge(wt_half, s + 1)
                        if s >= 4:
                            pe.wait_ge(rs[2], s - 3)
                        accumulate(M[s % 4][:, 0:D], [(WT2[:, s % 4, 0, :], ctxA[s // TB][:, :]),
                                                      (WT2[0:SB_, s % 4, 1, :], ctxB[s // TB][0:SB_, :])], pm[2])
            turn_x(TP_X2, 2)
            pe.wait_ge(mix_sb, 2)
            for t in range(NT):
                if t % TB == 0:
                    pe.wait_ge(mix_sb, 2 * (t // TB) + 2)
                pe.wait_ge(rs[2], NT)
                if t >= 2:
                    pe.wait_ge(r_sb, t - 1)
                accumulate(M[t % 2][:, 0:D], [(mixT[:, k, P * t:P * t + P], wsT[:, 1, k, :]) for k in range(2)], r_mm)
            def keys(g):
                for m in range(2):
                    u = 2 * g + m
                    pe.wait_ge(mix_sb, 4 + 2 * (g // 2) + 2)
                    if u >= 2:
                        pe.wait_ge(kk_rel, u - 1)
                    accumulate(M[2 + m], [(wsT[:, 2, k, P * m:P * m + P], XT[0][:, k, G * g:G * g + G]) for k in range(2)], kk_mm)

            keys(0)
            pe.wait_ge(r_sb, NT)
            for g in range(NG):
                if g + 1 < NG:
                    keys(g + 1)
                for t in range(4 * g, 4 * g + 4):
                    pe.wait_ge(kk_sb, 2 * g + 2)
                    if t >= 4:
                        pe.wait_ge(rs[3], t - 3)
                    accumulate(MV[t % 4][:, 0:D], [(XT[1][:, k, P * t:P * t + P], wsT[:, 3, k, :]) for k in range(2)], pm[3])
            for b in range(B):
                for t in range(TB * b, TB * b + TB):
                    pe.wait_ge(xo[3], t + 1)
                    turn_tile(TP_X3 + t, X[:, t, :])
                pe.wait_ge(tp_out, TP_X3 + TB * b + TB)
                for u in range(4 * b, 4 * b + 4):
                    g, c = u // 2, u % 2
                    pe.wait_ge(*((vv_sb, u - 1) if u >= 2 else (kk_rel, 2 * NG)))
                    accumulate(M[2 + u % 2], [(wsT[:, 4, k, P * c:P * c + P], XT[1][:, k, G * g:G * g + G]) for k in range(2)], vv_mm)
            pe.wait_ge(rs[3], NT)
            pe.wait_ge(vv_sb, 8)

            def turn_mixed(g):
                pe.wait_ge(acc_sb, 2 * g + 2)
                if g:
                    pe.wait_ge(at_rd, 4 * g)
                for j in range(4):
                    for c in range(2):
                        c0 = 256 * (j % 2) + P * c
                        last = nc.tensor.transpose(M[4 + j // 2][:, c0:c0 + P], acc[:, g % 2, c, P * j:P * j + P], ident[:, :])
                    last.then_inc(at_mm, 1)

            for g in range(NG):
                for c in range(2):
                    for n in range(NSH):
                        u = (2 * g + c) * NSH + n
                        if u >= 4:
                            pe.wait_ge(g_sig, u - 3)
                        e0 = D * n + P * c
                        accumulate(M[u % 4], [(gateT[:, k, e0:e0 + P], XT[1][:, k, G * g:G * g + G]) for k in range(2)], g_mm)
                        if c == 0 and n == TURN_AT and g >= 1:
                            turn_mixed(g - 1)
            turn_mixed(NG - 1)
            pe.wait_ge(consts, 10)
            pe.wait_ge(ah_sb, 3)
            for what, g in DIST:
                if what == "x":
                    for t in range(4 * g, 4 * g + 4):
                        pe.wait_ge(xo[4], t + 1)
                        turn_tile(TP_X4 + t, X[:, t, :])
                else:
                    b = g // 2
                    parts = 2 if g < NG // 2 else 1
                    pe.wait_ge(*((sq_sb, 2 * g + 2) if parts == 2 else (tp_out, TP_X4 + 4 * g + 4)))
                    for r in range(2):
                        u = 2 * g + r
                        pe.wait_ge(*((d_sq, u - 3) if u >= 4 else (g_sig, NG * 2 * NSH)))
                        q0, n = (0, P) if r == 0 else (32 * b, SB_)
                        cols = slice(0, P) if r == 0 else slice(P, S)
                        for k in range(2):
                            nc.tensor.matmul(M[u % 4][q0:q0 + n, :], ctxT[b][:, k, cols], XT[0][:, k, G * g:G * g + G], start=k == 0, stop=False)
                        if parts == 1:
                            pe.wait_ge(sq_sum, g - NG // 2 + 1)
                        for k in range(parts):
                            last = nc.tensor.matmul(M[u % 4][q0:q0 + n, :], nhalves[:, 0:n], XT[1][:, k, G * g:G * g + G],
                                                    start=False, stop=k == parts - 1)
                        last.then_inc(d_mm, 1)
            pe.wait_ge(ld_ip, 16)
            for r in range(NIN // P):
                turn_tile(TP_IP + r, ipraw[:, r, :])
            pe.wait_ge(ld_ow, 16)
            pe.wait_ge(d_sq, 2 * NG)
            for k in range(4):
                for j in range(4):
                    last = nc.tensor.transpose(M[2 + k][:, P * j:P * j + P], owraw[:, 4 * k + j, :], ident[:, :])
                last.then_inc(ow_t, 1)
            ZC = (M[0], M[5])
            PARTS = [((0, 0, P, b), (32 * b, P, SB_, 2)) for b in range(B)]

            def entries(b):
                pe.wait_ge(chased[b], S // 2)
                pe.wait_ge(io_f, 6)
                if b:
                    pe.wait_ge(rs[5], TB)
                for n, (q0, i0, cnt_, _) in enumerate(PARTS[b]):
                    last = nc.tensor.matmul(ZC[b][q0:q0 + cnt_, n:n + 1], zrow[:, b, i0 + 1:i0 + 1 + cnt_], ones[0:1, 0:1],
                                            start=True, stop=True)
                last.then_inc(en_mm, 1)

            def crossings(b):
                pe.wait_ge(y_ok, 2 * b + 2)
                for n, (q0, i0, cnt_, k) in enumerate(PARTS[b]):
                    for e in range(2):
                        c = 4 + 2 * n + e
                        nc.tensor.matmul(ZC[b][q0:q0 + cnt_, c:c + 1], zrow[:, b, i0 + e:i0 + e + cnt_], ones[0:1, 0:1],
                                         start=True, stop=False)
                        last = nc.tensor.matmul(ZC[b][q0:q0 + cnt_, c:c + 1], identx[:, q0 + e:q0 + e + cnt_],
                                                yz[:, k:k + 1], start=False, stop=True)
                last.then_inc(z_mm, 1)

            def warp(t):
                b, c0 = t // TB, P * (t % TB)
                pe.wait_ge(p_ok, 4 * b + 2 * (t % TB // 4) + 2)
                if t >= 4:
                    pe.wait_ge(rs[5], t - 3)
                else:
                    pe.wait_ge(ow_sb, 4)
                accumulate(M[2 + t % 4][:, 0:D], [(Pm[:, b, c0:c0 + P], ctxA[b][:, :]), (Pm[:, 2 + b, c0:c0 + P], ctxBB[:, :])], pm[5])

            entries(0)
            crossings(0)
            for t in range(TB):
                warp(t)
            entries(1)

            def turn_x5(t):
                pe.wait_ge(xo[5], t + 1)
                turn_tile(TP_X5 + t, X[:, t, :])

            for t in range(TB):
                turn_x5(t)

            def make_row(what):
                s = ROWS.index(what)
                kind, b, g = what
                if kind == "in":
                    pe.wait_ge(m_ok, 4 * b + g + 1)
                    vals = mact[:, b, :]
                elif kind == "proc":
                    pe.wait_ge(p_act, b + 1)
                    vals = pact[:, :]
                else:
                    pe.wait_ge(oa_act, b + 1)
                    vals = oact[:, b, :]
                if s:
                    pe.wait_ge(bc_out, s)
                else:
                    pe.wait_ge(tp_out, TP_X5 + NT)
                for j in range(4):
                    v = vals[:, 4 * g + j:4 * g + j + 1]
                    last = nc.tensor.transpose(TP[0][:, P * j:P * j + P],
                                               bass.AP(tensor=v.tensor, offset=v.offset, ap=[v.ap[0], [0, P]]), ident[:, :])
                last.then_inc(bc_mm, 1)

            def rank(c, i):
                g, (kind, q) = ITEMS[i]
                n = len(ITEMS) * c + i
                pe.wait_ge(cmp_ok, sum(OPS) * c + sum(OPS[:i + 1]))
                if i == 0:
                    if c:
                        pe.wait_ge(kept_ok, c)
                    else:
                        pe.wait_ge(rs[5], NT)
                        pe.wait_ge(c_ok, 5)
                if kind == "new":
                    for k in range(g + 1):
                        nc.tensor.matmul(M[2 + k], ones_h[:, :], less[:, n % CR, 512 * k:512 * k + 512],
                                         start=q == 4 * k, stop=q == NQ - 1 and k < g)
                    last = nc.tensor.matmul(M[2 + g][:, P * (q % 4):P * (q % 4) + P], ones_h[:, :], tied[:, n % CR, :],
                                            start=False, stop=False)
                else:
                    for j in range(4):
                        last = nc.tensor.matmul(M[2 + g], ones_h[:, :], less[:, n % CR, 512 * j:512 * j + 512],
                                                start=False, stop=j == 3 and i == len(ITEMS) - 1)
                last.then_inc(rank_mm, 1)

            def behind(job):
                if job[0] == "turn":
                    turn_x5(job[1])
                elif job[0] == "cross":
                    crossings(job[1])
                elif job[0] == "warp":
                    warp(job[1])
                elif job[0] == "row":
                    make_row(job[1])
                else:
                    rank(job[1], job[2])

            def chosen(b):
                pe.wait_ge(wt_ok, b + 1)
                nc.tensor.matmul(TP[1][:, 0:NP_], ones[:, :], wt[:, :], start=True, stop=True)
                for r in range(NP_):
                    last = nc.tensor.matmul(TP[1][:, 8:9], pv[:, r, :], wt[:, r:r + 1], start=r == 0, stop=r == NP_ - 1)
                last.then_inc(tot_mm, 1)

            def out_product(b):
                pe.wait_ge(agg_ok, b + 1)
                for q in range(NQ):
                    last = nc.tensor.matmul(TP[1][:, 16 + q:17 + q], owT[:, P * q:P * q + P], agg[:, :], start=True, stop=True)
                last.then_inc(oa_mm, 1)

            def rank_group(c, g):
                for i, (g_, _) in enumerate(ITEMS):
                    if g_ == g:
                        rank(c, i)

            def kept_columns(b):
                pe.wait_ge(kept_ok, 2 + b + 1)
                pe.wait_ge(oa_act, 2)
                for q in range(NQ):
                    last = nc.tensor.transpose(TP[1][:, 32 + q:33 + q], krow[0:1, P * q:P * q + P], ident[0:1, 0:1])
                last.then_inc(kc_mm, 1)

            def output(b):
                pe.wait_ge(ko_ok, b + 1)
                for q in range(NQ):
                    a = kept[:, q:q + 1]
                    last = nc.tensor.matmul(M[b][:, 0:D], bass.AP(tensor=a.tensor, offset=a.offset, ap=[a.ap[0], [0, P]]),
                                            op[:, q, :], start=q == 0, stop=q == NQ - 1)
                last.then_inc(f_mm, 1)

            for u in range(B * NQ):
                b, q = u // NQ, u % NQ
                if q == 0:
                    pe.wait_ge(tp_out, TP_X5 + TB * b + TB)
                for h in range(2):
                    if u:
                        pe.wait_ge(a_gelu, 2 * u + h - 1)
                    accumulate(M[h], [(ipT[:, k, P * q:P * q + P], XT[1][:, k, L * b + G * h:L * b + G * h + G]) for k in range(2)], a_mm)
                for job in BEHIND[u]:
                    behind(job)
                if u == PROC_AT:
                    for g in range(2):
                        make_row(("proc", 0, g))
            for u in range(B * NQ, max(BEHIND) + 1):
                for job in BEHIND[u]:
                    behind(job)
            pe.wait_ge(a_gelu, 2 * B * NQ)
            make_row(("in", 1, 3))
            rank_group(1, 3)
            pe.wait_ge(ld_pv, 16)
            chosen(0)
            out_product(0)
            for g in range(4):
                make_row(("out", 0, g))
            rank_group(2, 0)
            rank_group(2, 1)
            for g in range(2):
                make_row(("proc", 1, g))
            chosen(1)
            rank_group(2, 2)
            out_product(1)
            rank_group(2, 3)
            pe.wait_ge(ld_op, 16)
            kept_columns(0)
            for g in range(4):
                make_row(("out", 1, g))
            for g in range(3):
                rank_group(3, g)
            output(0)
            rank_group(3, 3)
            kept_columns(1)
            output(1)

        @block.vector
        def _(dve):
            steps = [0]

            def tick(ins):
                ins.then_inc(dv, 1)
                steps[0] += 1

            def settle(but=0):
                dve.wait_ge(dv, steps[0] - but)

            V = nc.vector

            def moments(src, seen, g):
                for j in range(4):
                    tick(V.bn_stats(stat[:, j, :], src(j)))
                settle()
                for j in range(4):
                    tick(V.bn_aggr(mv[:, 4 * g + j, :], stat[:, j, :]))
                settle()
                V.tensor_scalar(ve[:, 4 * g:4 * g + 4], mv[:, 4 * g:4 * g + 4, 1], EPS, None, ALU.add).then_inc(seen, 1)

            def norm_sums(n, g, summed):
                if g >= 2:
                    dve.wait_ge(xo[n], 4 * g - 4)
                elif g == 0 and n >= 2:
                    dve.wait_ge(xo[n - 1], NT)
                for j in range(4):
                    summed(4 * g + j, res[:, g % 2, j, :]).then_inc(rs[n], 1)

            def norm_moments(n, g):
                dve.wait_ge(rs[n], 4 * g + 4)
                moments(lambda j: res[:, g % 2, j, :], vr[n], g)

            def norm(n, g, summed):
                norm_sums(n, g, summed)
                norm_moments(n, g)

            def apply(n, g):
                dve.wait_ge(sd[n], g + 1)
                for j in range(4):
                    t = 4 * g + j
                    V.tensor_scalar(X[:, t, :], res[:, g % 2, j, :], mv[:, t, 0:1], rstd[:, t:t + 1],
                                    ALU.subtract, ALU.mult).then_inc(xo[n], 1)

            def plus_x(n):
                def summed(t, dst):
                    dve.wait_ge(pm[n], t + 1)
                    return V.tensor_tensor(dst, M[t % 4][:, 0:D], X[:, t, :], ALU.add)
                return summed

            dve.wait_ge(consts, 9)
            tick(V.tensor_scalar(pbit[:, :], pidx[:, :], 4, 1, ALU.logical_shift_right, ALU.bitwise_and))
            settle()
            tick(V.tensor_copy(parm[:, 1:2], pbit[:, :]))
            settle()
            tick(V.tensor_scalar(parm[:, 0:1], parm[:, 1:2], -1.0, 1.0, ALU.mult, ALU.add))
            settle()
            for m in range(2):
                dve.wait_ge(k_mm, 2)
                src = M[2][:, 256 * m:256 * m + 256].rearrange("p (g k) -> p g k", g=NG)
                for h in range(2):
                    V.tensor_scalar(kbd[:, m, :, h, :], src, parm[:, h:h + 1], None, ALU.mult).then_inc(k_sb, 1)
            for g in range(NG):
                dve.wait_ge(v_mm, g // 2 + 1)
                src = M[3 + g // 2][64 * (g % 2):64 * (g % 2) + 64, 0:D].rearrange("p (a h d) -> p a h d", a=NPAIR, h=2)
                for h in range(2):
                    V.tensor_copy(vbd[64 * h:64 * h + 64, g, :, h, :], src[:, :, h, :]).then_inc(v_sb, 1)
            for u in range(2):
                dve.wait_ge(q_mm, u + 1)
                V.tensor_copy(qT[:, u % 2, G * (u // 2):G * (u // 2) + G], M[u % 2]).then_inc(q_sb, 1)
            for q in range(9):
                if q < 8:
                    for j in range(4):
                        u = 4 * q + j
                        dve.wait_ge(s_mm, u + 1)
                        tick(V.tensor_reduce(cmax[:, u, :], M[j].rearrange("p (n b) -> p n b", b=BLK), AX.X, ALU.max))
                    settle()
                    for j in range(4):
                        u = 4 * q + j
                        if u >= 4:
                            dve.wait_ge(w_exp, u - 3)
                        cm = cmax[:, u, :]
                        V.tensor_tensor(Sm[:, j, :].rearrange("p (n b) -> p n b", b=BLK), M[j].rearrange("p (n b) -> p n b", b=BLK),
                                        bass.AP(tensor=cm.tensor, offset=cm.offset, ap=[cm.ap[0], cm.ap[1], [0, BLK]]),
                                        ALU.subtract).then_inc(s_sub, 1)
                if q >= 1:
                    g, m = (q - 1) // 2, (q - 1) % 2
                    dve.wait_ge(nd_mm, q)
                    tick(V.tensor_scalar(den[:, :], M[5], 1e-10, None, ALU.add))
                    settle()
                    tick(V.reciprocal(rden[:, :], den[:, :]))
                    settle()
                    V.tensor_tensor(oT[:, m, G * g:G * g + G], M[4], rden[:, :], ALU.mult).then_inc(o_sb, 1)
            for g in range(NG):
                norm(1, g, plus_x(1))
                if g:
                    apply(1, g - 1)
            apply(1, NG - 1)
            def summed(t, dst):
                if t % 4 == 0:
                    dve.wait_ge(l_exp, t + 4)
                    tick(V.reciprocal(rsum[:, t:t + 4], ssum[:, t:t + 4]))
                    settle()
                dve.wait_ge(pm[2], t + 1)
                return V.scalar_tensor_tensor(out=dst, in0=M[t % 4][:, 0:D], scalar=rsum[:, t:t + 1], in1=X[:, t, :], op0=ALU.mult, op1=ALU.add)

            for p in range(NT // 2):
                dve.wait_ge(l_mm, 2 * p + 2)
                tick(V.tensor_reduce(mx[:, 2 * p:2 * p + 2], M[4 + p % 2].rearrange("p (h c) -> p h c", h=2)[:, :, 0:S], AX.X, ALU.max))
                settle()
                V.tensor_scalar(nmx[:, 2 * p:2 * p + 2], mx[:, 2 * p:2 * p + 2], -float(D) ** -0.5, None, ALU.mult).then_inc(l_mx, 1)
                if p % 2 == 1 and p >= 3:
                    g = p // 2 - 1
                    norm(2, g, summed)
                    if g:
                        apply(2, g - 1)
            norm(2, NG - 1, summed)
            apply(2, NG - 2)
            apply(2, NG - 1)
            dve.wait_ge(ld_vec, 64)
            tick(V.tensor_scalar(omm[:, :, :], mus[:, :, :], -1.0, 1.0, ALU.mult, ALU.add))
            settle()
            tick(V.memset(mtmp[:, :, 0:1], 0.0))
            for n in range(2):
                for b in range(B):
                    dve.wait_ge(tp_out, TP_X2 + TB * b + TB)
                    c0 = L * b
                    if n or b:
                        dve.wait_ge(mix_sb, 4 * n + 2 * b)
                    for k in range(2):
                        tick(V.tensor_scalar(mtmp[:, k, 1:L], XT[0][:, k, c0:c0 + L - 1], omm[:, k, n:n + 1], None, ALU.mult))
                    settle()
                    for k in range(2):
                        dst = (mixT if n == 0 else XT[0])[:, k, c0:c0 + L]
                        V.scalar_tensor_tensor(out=dst, in0=XT[0][:, k, c0:c0 + L], scalar=mus[:, k, n:n + 1], in1=mtmp[:, k, :],
                                               op0=ALU.mult, op1=ALU.add).then_inc(mix_sb, 1)
            def squares(g):
                for m in range(2):
                    u = 2 * g + m
                    dve.wait_ge(kk_rel, u + 1)
                    V.tensor_tensor(XT[1][:, m, G * g:G * g + G], krel[:, m, :], krel[:, m, :], ALU.mult).then_inc(kk_sb, 1)

            def gate(g):
                if g >= 2:
                    dve.wait_ge(xo[3], 4 * g - 4)
                elif g == 0:
                    dve.wait_ge(xo[2], NT)
                for t in range(4 * g, 4 * g + 4):
                    dve.wait_ge(pm[3], t + 1)
                    tick(V.tensor_tensor(res[:, g % 2, t % 4, :], MV[t % 4][:, 0:D], rgate[:, t, :], ALU.mult))
                settle()

            squares(0)
            dve.wait_ge(r_sb, NT)
            for g in range(NG):
                if g + 1 < NG:
                    squares(g + 1)
                gate(g)
                norm(3, g, lambda t, dst: V.tensor_tensor(dst, dst, X[:, t, :], ALU.add))
                if g:
                    apply(3, g - 1)
            apply(3, NG - 1)
            for n, cx in enumerate((ctxA[0], ctxA[1], ctxBB)):
                if n:
                    dve.wait_ge(ah_sb, n)
                V.scalar_tensor_tensor(out=pr[:, 0, 0:D], in0=cx[:, :], scalar=0.5, in1=cx[:, :], op0=ALU.mult, op1=ALU.mult,
                                       accum_out=aah[:, n:n + 1]).then_inc(ah_sb, 1)
            dve.wait_ge(ah_sb, 3)

            def halos(b):
                dve.wait_ge(vv_sb, 4 * b + 4)
                for c in range(2):
                    V.tensor_copy(Vh[:, c, b, 0:HALO], Vh[:, c, b, L:L + HALO]).then_inc(halo, 1)
                    V.tensor_copy(Vh[:, c, b, HALO + L:], Vh[:, c, b, HALO:2 * HALO]).then_inc(halo, 1)
                dve.wait_ge(halo, 4 * b + 4)

            def mixed_norm(g, step):
                def at(j):
                    return M[4 + j // 2][:, 256 * (j % 2):256 * (j % 2) + 256]

                def scaled(t, dst):
                    return V.tensor_tensor(dst, y2[:, t % 4, :], X[:, t, :], ALU.add)

                if step == 0:
                    dve.wait_ge(at_mm, 4 * g + 4)
                    moments(at, iv, g)
                elif step == 1:
                    for j in range(4):
                        tick(V.scalar_tensor_tensor(out=y2[:, j, :], in0=at(j), scalar=mv[:, 4 * g + j, 0:1], in1=gam[:, :],
                                                    op0=ALU.subtract, op1=ALU.mult))
                elif step == 2:
                    dve.wait_ge(isd, g + 1)
                    settle()
                    for j in range(4):
                        V.scalar_tensor_tensor(out=y2[:, j, :], in0=y2[:, j, :], scalar=rstd[:, 4 * g + j:4 * g + j + 1], in1=bet[:, :],
                                               op0=ALU.mult, op1=ALU.add).then_inc(at_rd, 1)
                elif step == 3:
                    dve.wait_ge(at_rd, 4 * g + 4)
                    norm_sums(4, g, scaled)
                elif step == 4:
                    norm_moments(4, g)
                else:
                    apply(4, g)

            for g in range(NG):
                b, h = g // 2, g % 2
                if h == 0:
                    halos(b)
                for c in range(2):
                    for n in range(NSH):
                        u = (2 * g + c) * NSH + n
                        dve.wait_ge(g_sig, u + 1)
                        v0 = HALO + SHIFTS[n] + G * h
                        dst = acc[:, g % 2, c, :] if n == 0 else pr[:, u % 4, :]
                        V.tensor_tensor(dst, gs[:, u % 4, :], Vh[:, c, b, v0:v0 + G], ALU.mult).then_inc(g_mul, 1)
                        if n >= 2:
                            dve.wait_ge(g_mul, u)
                            settle()
                            tick(V.tensor_tensor(acc[:, g % 2, c, :], acc[:, g % 2, c, :], pr[:, (u - 1) % 4, :], ALU.add))
                        if g >= 1 and c * NSH + n in NORM_AT:
                            mixed_norm(g - 1, NORM_AT.index(c * NSH + n))
                    dve.wait_ge(g_mul, u + 1)
                    settle()
                    V.tensor_tensor(acc[:, g % 2, c, :], acc[:, g % 2, c, :], pr[:, u % 4, :], ALU.add).then_inc(acc_sb, 1)
            for step in range(6):
                mixed_norm(NG - 1, step)
            for g in range(NG // 2, NG):
                dve.wait_ge(sq_sb, 2 * g + 2)
                both = XT[1][:, :, G * g:G * g + G]
                V.tensor_tensor(both[:, 0, :], both[:, 0, :], both[:, 1, :], ALU.add).then_inc(sq_sum, 1)
            V.memset(Rw[:, 0:3, :], BIG).then_inc(w_init, 1)
            dve.wait_ge(w_init, 1)
            lanes = [0] + list(range(31))
            for t in range(T):
                cur, prev = (t + 1) % RING, t % RING
                if t % TC == 0:
                    dve.wait_ge(dw_ld[t // TC], 32)
                if t >= 1:
                    dve.wait_ge(w_row, t)
                V.tensor_tensor(Mw[:, t % 2, :], Rw[:, prev, 0:W], Rw[:, prev, 1:W + 1], ALU.min).then_inc(w_min, 1)
                if t >= 1:
                    if t + 1 >= RING:
                        stored(dve, t + 1 - RING)
                    V.stream_shuffle(Rw[:, (t + 2) % RING, 0:1], Rw[:, prev, W:W + 1], lanes).then_inc(w_edge, 1)
                dve.wait_ge(w_min, t + 1)
                if t >= 2:
                    dve.wait_ge(w_edge, t - 1)
                if t >= RING:
                    stored(dve, t - RING)
                V.tensor_tensor_scan(Rw[:, cur, 1:W + 1], Mw[:, t % 2, :], Dw[:, t, :], Rw[:, cur, 0:1] if t else 0.0,
                                     ALU.min, ALU.add).then_inc(w_row, 1)
            dve.wait_ge(pad_ok, 10)
            dve.wait_ge(io_f, 6)
            dve.wait_ge(w_row, T)

            def row_exits(n, k):
                dve.wait_ge(*((rrB_ld, 64) if k == 2 else (rrA_ld, 64)))
                up, here = Rp[:, k, 0:L], Rc[:, k, 0:L]
                tick(V.tensor_tensor(tmpa[:, :], up, Rp[:, k, 1:L + 1], ALU.min))
                settle()
                tick(V.tensor_tensor(up, up, Rp[:, k, 1:L + 1], ALU.is_gt))
                tick(V.tensor_tensor(here, here, tmpa[:, :], ALU.is_ge))
                settle(1)
                tick(V.scalar_tensor_tensor(out=tmpb[:, :], in0=up, scalar=-1.0, in1=iota2[:, :], op0=ALU.add, op1=ALU.add))
                settle()
                tick(V.tensor_tensor(tmpb[:, :], tmpb[:, :], here, ALU.mult))
                settle()
                V.tensor_tensor_scan(Zf[:, k, :], tmpb[:, :], tmpb[:, :], 0.0, ALU.max, ALU.max).then_inc(zf_ok, 1)
                dve.wait_ge(zf_ok, n + 1)

            def pair_exits(n, k):
                dve.wait_ge(zs_ld[k], 16)
                up, here = Rp[:, k, 0:L], Rc[:, k, 0:L]
                tick(V.scalar_tensor_tensor(out=tmpa[:, :], in0=up, scalar=4.0 * L, in1=Zs[:, k, 0:L], op0=ALU.mult, op1=ALU.add))
                settle()
                tick(V.tensor_tensor(tmpb[:, :], tmpa[:, :], Zs[:, k, 1:L + 1], ALU.min))
                settle()
                tick(V.tensor_tensor(tmpa[:, :], tmpb[:, :], here, ALU.mult))
                settle()
                V.tensor_tensor_scan(Zi[:, k, :], tmpa[:, :], tmpa[:, :], 0.0, ALU.max, ALU.max).then_inc(z_ok, 1)
                dve.wait_ge(z_ok, n + 1)

            row_exits(0, 0)
            row_exits(1, 2)
            pair_exits(0, 0)
            pair_exits(1, 2)
            row_exits(2, 1)
            pair_exits(2, 1)
            def warped(t, dst):
                dve.wait_ge(pm[5], t + 1)
                return V.tensor_tensor(dst, M[2 + t % 4][:, 0:D], X[:, t, :], ALU.add)

            for k in range(4):
                dve.wait_ge(ow_t, k + 1)
                V.tensor_copy(owT[:, 512 * k:512 * k + 512], M[2 + k]).then_inc(ow_sb, 1)
            ZC = (M[0], M[5])

            def path_masks(b):
                dve.wait_ge(en_mm, b + 1)
                parts = ((0, P, b, tmpa), (32 * b, 32 * b + SB_, 2, tmpb))
                for n, (q0, q1, k, _) in enumerate(parts):
                    tick(V.tensor_copy(en[q0:q1, k:k + 1], ZC[b][q0:q1, n:n + 1]))
                settle()
                for q0, q1, k, tmp in parts:
                    tick(V.scalar_tensor_tensor(out=tmp[q0:q1, :], in0=iota2[q0:q1, :], scalar=en[q0:q1, k:k + 1], in1=Zf[q0:q1, k, :],
                                                op0=ALU.is_le, op1=ALU.mult))
                settle()
                for q0, q1, k, tmp in parts:
                    V.tensor_reduce(yz[q0:q1, k:k + 1], tmp[q0:q1, :], AX.X, ALU.max).then_inc(y_ok, 1)
                dve.wait_ge(y_ok, 2 * b + 2)
                dve.wait_ge(z_mm, b + 1)
                tick(V.tensor_copy(zcol[:, b, :], ZC[b][:, 4:6]))
                tick(V.tensor_copy(zcol[32 * b:32 * b + SB_, 2 + b, :], ZC[b][32 * b:32 * b + SB_, 6:8]))
                settle()
                for h in range(2):
                    c0, c1 = G * h, G * h + G
                    for k, tmp in ((b, tmpa), (2 + b, tmpb)):
                        tick(V.tensor_scalar(tmp[:, c0:c1], iota2[:, c0:c1], zcol[:, k, 0:1], None, ALU.is_ge))
                    settle()
                    for k, tmp in ((b, tmpa), (2 + b, tmpb)):
                        V.scalar_tensor_tensor(out=Pm[:, k, c0:c1], in0=iota2[:, c0:c1], scalar=zcol[:, k, 1:2], in1=tmp[:, c0:c1],
                                               op0=ALU.is_le, op1=ALU.mult).then_inc(p_ok, 1)
                dve.wait_ge(p_ok, 4 * b + 4)

            for b in range(B):
                path_masks(b)
                norm(5, 2 * b, warped)
                norm(5, 2 * b + 1, warped)
                apply(5, 2 * b)
                apply(5, 2 * b + 1)
            dve.wait_ge(c_ok, 5)
            made = [0]

            def compare(vals, r, g):
                for kind, q in items(g):
                    slot = made[0] % CR
                    if made[0] >= CR:
                        dve.wait_ge(rank_mm, made[0] - CR + 1)
                    if kind == "new":
                        v, c0, c1, c2 = vals[:, q:q + 1], P * q, P * q + P, 512 * (g + 1)
                        V.tensor_scalar(less[:, slot, 0:c1], r[:, 0:c1], v, None, ALU.is_lt).then_inc(cmp_ok, 1)
                        if c1 < c2:
                            V.tensor_scalar(less[:, slot, c1:c2], r[:, c1:c2], v, None, ALU.is_le).then_inc(cmp_ok, 1)
                        V.scalar_tensor_tensor(out=tied[:, slot, :], in0=r[:, c0:c1], scalar=v, in1=after[:, :],
                                               op0=ALU.is_equal, op1=ALU.mult).then_inc(cmp_ok, 1)
                    else:
                        for j in range(4):
                            V.tensor_scalar(less[:, slot, 512 * j:512 * j + 512], r[:, 512 * g:512 * g + 512],
                                            vals[:, 4 * q + j:4 * q + j + 1], None, ALU.is_le).then_inc(cmp_ok, 1)
                    made[0] += 1

            def row_ready(what):
                dve.wait_ge(bc_out, ROWS.index(what) + 1)

            def inputs(b, g):
                mean(b, g)
                row_ready(("in", b, g))
                compare(mact[:, b, :], row[:, b, :], g)

            def mean(b, g):
                dve.wait_ge(a_gelu, 2 * (NQ * b + 4 * g + 4))
                m = mact[:, b, 4 * g:4 * g + 4]
                tick(V.tensor_tensor(m, acts[:, b, 4 * g:4 * g + 4, 0], acts[:, b, 4 * g:4 * g + 4, 1], ALU.add))
                settle()
                V.tensor_scalar(m, m, 1.0 / L, None, ALU.mult).then_inc(m_ok, 1)
                dve.wait_ge(m_ok, 4 * b + g + 1)

            def keep(c, b, n, K):
                dve.wait_ge(rank_mm, len(ITEMS) * (c + 1))
                V.scalar_tensor_tensor(out=krow[0:n, :], in0=PS[0:n, 4:8, :].rearrange("p a b -> p (a b)"), scalar=float(K),
                                       in1=row[0:n, b, :], op0=ALU.is_lt, op1=ALU.mult).then_inc(kept_ok, 1)
                dve.wait_ge(kept_ok, c + 1)

            def process(b, parts):
                for r in parts:
                    n = NP_ * b + r
                    dve.wait_ge(ld_pw[n % PW], 16 * (n // PW + 1))
                    if n >= 2:
                        dve.wait_ge(pw_used, n - 1)
                    if r == 0 and b:
                        dve.wait_ge(p_act, b)
                    V.scalar_tensor_tensor(out=cdump[:, r % 2, :], in0=pwt[n % PW], scalar=1.0, in1=krow[:, :], op0=ALU.mult, op1=ALU.mult,
                                           accum_out=pacc[:, r:r + 1]).then_inc(pw_used, 1)

            def weigh(b):
                dve.wait_ge(p_act, b + 1)
                tick(V.memset(cnt[:, :, :], 0.0))
                settle()
                row_ready(("proc", b, 1))
                for q in range(NP_):
                    v, c0, c1 = pact[:, q:q + 1], P * q, P * q + P
                    settle(3 if q else 0)
                    if q:
                        tick(V.tensor_scalar(cdump[:, q % 2, 0:c0], row2[:, 0:c0], v, 0.0, ALU.is_ge, ALU.add, accum_out=cnt[:, 0, q:q + 1]))
                    tick(V.tensor_scalar(cdump[:, q % 2, c0:NPROC], row2[:, c0:NPROC], v, 0.0, ALU.is_gt, ALU.add, accum_out=cnt[:, 1, q:q + 1]))
                    tick(V.scalar_tensor_tensor(out=cdump[:, q % 2, NPROC:NPROC + P], in0=row2[:, c0:c1], scalar=v, in1=before[:, :],
                                                op0=ALU.is_equal, op1=ALU.mult, accum_out=cnt[:, 2, q:q + 1]))
                V.tensor_reduce(sc[:, 0:1], row2[:, :], AX.X, ALU.max).then_inc(row2_free, 1)
                dve.wait_ge(row2_free, b + 1)
                V.tensor_scalar(sc[:, 1:2], sc[:, 0:1], -1.0, None, ALU.mult).then_inc(e_arg, 1)
                settle()
                tick(V.tensor_tensor(cnt[:, 0, :], cnt[:, 0, :], cnt[:, 1, :], ALU.add))
                settle()
                tick(V.tensor_tensor(cnt[:, 0, :], cnt[:, 0, :], cnt[:, 2, :], ALU.add))
                settle()
                tick(V.tensor_scalar(msk[:, :], cnt[:, 0, :], float(KPROC), None, ALU.is_lt))
                settle()

            def weights(b):
                dve.wait_ge(e_ok, b + 1)
                V.tensor_tensor(wt[:, :], pex[:, :], msk[:, :], ALU.mult).then_inc(wt_ok, 1)

            def aggregate(b):
                dve.wait_ge(tot_mm, b + 1)
                tick(V.tensor_reduce(sc[:, 2:3], TP[1][:, 0:NP_], AX.X, ALU.add))
                settle()
                tick(V.reciprocal(sc[:, 2:3], sc[:, 2:3]))
                settle()
                V.tensor_scalar(agg[:, :], TP[1][:, 8:9], sc[:, 2:3], None, ALU.mult).then_inc(agg_ok, 1)

            def out_group(b, g):
                row_ready(("out", b, g))
                compare(oact[:, b, :], row[:, b, :], g)

            def out_kept(b):
                keep(2 + b, b, 1, KOUT)
                dve.wait_ge(kc_mm, b + 1)
                V.tensor_copy(kept[:, :], TP[1][:, 32:32 + NQ]).then_inc(ko_ok, 1)

            def last_norm(b, g):
                if g == 0:
                    dve.wait_ge(f_mm, b + 1)
                norm(6, 2 * b + g, lambda t, dst: V.tensor_tensor(dst, M[b][:, 0:D], X[:, t, :], ALU.add))

            for g in range(4):
                inputs(0, g)
            keep(0, 0, P, KIN)
            process(0, range(0, 1))
            inputs(1, 0)
            process(0, range(1, 5))
            inputs(1, 1)
            process(0, range(5, NP_))
            inputs(1, 2)
            weigh(0)
            inputs(1, 3)
            weights(0)
            dve.wait_ge(pw_used, NP_)
            keep(1, 1, P, KIN)
            process(1, range(2))
            aggregate(0)
            process(1, range(2, NP_))
            dve.wait_ge(pw_used, 2 * NP_)
            out_group(0, 0)
            out_group(0, 1)
            weigh(1)
            weights(1)
            out_group(0, 2)
            aggregate(1)
            out_group(0, 3)
            out_kept(0)
            out_group(1, 0)
            out_group(1, 1)
            out_group(1, 2)
            out_group(1, 3)
            out_kept(1)
            last_norm(0, 0)
            last_norm(0, 1)
            apply(6, 0)
            apply(6, 1)
            last_norm(1, 0)
            last_norm(1, 1)
            apply(6, 2)
            apply(6, 3)

        block_stack.close()


_INS = ["x", "ctx_1024", "L0_attn_Wqkv", "L0_attn_Wout", "L0_ffn_W_r", "L0_ffn_W_k", "L0_ffn_W_v", "L0_ffn_mu_r",
        "L0_ffn_mu_k", "L1_attn_gate_W", "L1_attn_value_W", "L1_attn_gamma", "L1_attn_beta", "L1_ffn_input_patterns",
        "L1_ffn_process_input_weights", "L1_ffn_process_values", "L1_ffn_output_input_weights", "L1_ffn_output_patterns"]


def build(nc, arrays_of):
    args = [nc.dram_tensor(f"in_{n}", a.shape, F32, kind="ExternalInput").ap() for n, a in arrays_of.items()]
    out = nc.dram_tensor("out_0", arrays_of["x"].shape, F32, kind="ExternalOutput").ap()
    T = arrays_of["ctx_1024"].shape[1] + 2 * (arrays_of["x"].shape[1] // 64 - 1)
    C = arrays_of["x"].shape[1] // 64
    wave = [nc.dram_tensor(n, (2 * C, T, 64), F32, kind="Internal").ap() for n in ("wave_d", "wave_r")]
    decoder(nc, *args, out, *wave)


def kernel(**inputs):
    import numpy as np
    from concourse import bacc
    from concourse.bass_utils import run_bass_kernel_spmd

    nc = bacc.Bacc("TRN2", target_bir_lowering=False, num_devices=1)
    arrays = {n: np.ascontiguousarray(inputs[n]) for n in _INS}
    build(nc, arrays)
    r = run_bass_kernel_spmd(nc, [{f"in_{n}": a for n, a in arrays.items()}], core_ids=[0])
    return r.results[0]["out_0"]
```
